# Optimizing a Trainium2 kernel written in Bass

```python
import numpy as np
import jax
import jax.numpy as jnp

def _softmax(x, axis=-1):
    return jax.nn.softmax(x, axis=axis)

def _gelu(x):
    return jax.nn.gelu(x, approximate=True)

def _silu(x):
    return jax.nn.silu(x)

def _sigmoid(x):
    return jax.nn.sigmoid(x)

def _layernorm(x, axis=-1, eps=1e-05):
    m = jnp.mean(x, axis=axis, keepdims=True)
    v = jnp.var(x, axis=axis, keepdims=True)
    return (x - m) / jnp.sqrt(v + eps)

def _scatter_add(tgt, idx, src, axis=0):
    return tgt.at[idx].add(src)

def _segment_sum(src, seg, n):
    return jax.ops.segment_sum(src, seg, n)
kernel_name = 'mk_adaln_d2_jaxref_r8_37340a'

def setup_inputs(seed: int=0):
    np.random.seed(seed)
    _w = jnp.asarray

    def _L0_attn_setup():
        import jax, jax.numpy as jnp
        import numpy as np
        H = 16
        KVH = 4
        G = H // KVH
        HD = 128
        D = 256
        BASE = 10000.0

        def _rope(x, cos, sin):
            half = HD // 2
            x1, x2 = (x[..., :half], x[..., half:])
            return jnp.concatenate([x1 * cos - x2 * sin, x1 * sin + x2 * cos], axis=-1)
        key = jax.random.key(seed)
        ks = jax.random.split(key, 5)
        B, S = (2, 256)
        x = jax.random.normal(ks[0], (B, S, D), dtype=jnp.float32)
        Wq = jax.random.normal(ks[1], (D, H * HD), dtype=jnp.float32) * 0.02
        Wk = jax.random.normal(ks[2], (D, KVH * HD), dtype=jnp.float32) * 0.02
        Wv = jax.random.normal(ks[3], (D, KVH * HD), dtype=jnp.float32) * 0.02
        Wo = jax.random.normal(ks[4], (H * HD, D), dtype=jnp.float32) * 0.02
        return {'x': x, 'Wq': Wq, 'Wk': Wk, 'Wv': Wv, 'Wo': Wo}
    _L0_attn_in = _L0_attn_setup()

    def _L0_ffn_setup():
        import jax, jax.numpy as jnp
        import numpy as np
        D = 256
        F = 176
        E = 8
        K = 2
        FS = 352
        B, S = (2, 128)
        key = jax.random.key(seed)
        ks = jax.random.split(key, 9)
        sc = 0.02
        return {'x': jax.random.normal(ks[0], (B, S, D), dtype=jnp.float32), 'Wr': jax.random.normal(ks[1], (E, D), dtype=jnp.float32) * sc, 'Wg': jax.random.normal(ks[2], (E, F, D), dtype=jnp.float32) * sc, 'Wu': jax.random.normal(ks[3], (E, F, D), dtype=jnp.float32) * sc, 'Wd': jax.random.normal(ks[4], (E, D, F), dtype=jnp.float32) * sc, 'Wsg': jax.random.normal(ks[5], (FS, D), dtype=jnp.float32) * sc, 'Wsu': jax.random.normal(ks[6], (FS, D), dtype=jnp.float32) * sc, 'Wsd': jax.random.normal(ks[7], (D, FS), dtype=jnp.float32) * sc}
    _L0_ffn_in = _L0_ffn_setup()
    _L0_c = _w((lambda *s: np.random.randn(*s).astype(np.float32) * 0.05)(8, 256))
    _L0_wmod = _w((lambda *s: np.random.randn(*s).astype(np.float32) * 0.05)(256, 6 * 256) * 256 ** (-0.5))

    def _L1_attn_setup():
        import jax, jax.numpy as jnp
        import numpy as np
        BLOCK = 32
        NUM_HEADS = 16
        HEAD_DIM = 128
        FP4_GRID = jnp.array([0.0, 0.5, 1.0, 1.5, 2.0, 3.0, 4.0, 6.0], dtype=jnp.float32)

        def quantize_to_mxfp4(w, block_size=BLOCK):
            D, F = w.shape
            blocks = w.reshape(D // block_size, block_size, F)
            amax = jnp.max(jnp.abs(blocks), axis=1)
            e = jnp.floor(jnp.log2(jnp.maximum(amax, 1e-12) / 6.0))
            scale = jnp.exp2(e)
            v = blocks / scale[:, None, :]
            idx = jnp.argmin(jnp.abs(jnp.abs(v)[..., None] - FP4_GRID), axis=-1)
            codes = jnp.sign(v) * FP4_GRID[idx]
            return (codes.reshape(D, F).astype(jnp.float32), scale.astype(jnp.float32))

        def _mxfp4_matmul(x, codes, scales, block_size=BLOCK):
            w = codes * jnp.repeat(scales, block_size, axis=0)
            return x @ w
        key = jax.random.key(seed)
        ks = jax.random.split(key, 9)
        B, S, D = (2, 256, 256)
        feat = NUM_HEADS * HEAD_DIM
        x = jax.random.normal(ks[0], (B, S, D), dtype=jnp.float32)

        def make_w(k, din, dout):
            w = jax.random.normal(k, (din, dout), dtype=jnp.float32) * (1.0 / np.sqrt(din))
            return quantize_to_mxfp4(w, BLOCK)
        wq_codes, wq_scales = make_w(ks[1], D, feat)
        wk_codes, wk_scales = make_w(ks[2], D, feat)
        wv_codes, wv_scales = make_w(ks[3], D, feat)
        wo_codes, wo_scales = make_w(ks[4], feat, D)
        bq = jnp.zeros((feat,), jnp.float32)
        bk = jnp.zeros((feat,), jnp.float32)
        bv = jnp.zeros((feat,), jnp.float32)
        bo = jnp.zeros((D,), jnp.float32)
        return {'x': x, 'wq_codes': wq_codes, 'wq_scales': wq_scales, 'bq': bq, 'wk_codes': wk_codes, 'wk_scales': wk_scales, 'bk': bk, 'wv_codes': wv_codes, 'wv_scales': wv_scales, 'bv': bv, 'wo_codes': wo_codes, 'wo_scales': wo_scales, 'bo': bo}
    _L1_attn_in = _L1_attn_setup()

    def _L1_ffn_setup():
        import jax, jax.numpy as jnp
        import numpy as np
        H = 256
        E = 8
        K = 2
        I = 16
        key = jax.random.key(seed)
        k1, k2, k3, k4 = jax.random.split(key, 4)
        B, T = (2, 512)
        x = jax.random.normal(k1, (B, T, H), dtype=jnp.float32)
        router_w = jax.random.normal(k2, (E, H), dtype=jnp.float32) / np.sqrt(H)
        down_w = jax.random.normal(k3, (E, I, H), dtype=jnp.float32) / np.sqrt(H)
        up_w = jax.random.normal(k4, (E, H, I), dtype=jnp.float32) / np.sqrt(I)
        return {'x': x, 'router_w': router_w, 'down_w': down_w, 'up_w': up_w}
    _L1_ffn_in = _L1_ffn_setup()
    _L1_c = _w((lambda *s: np.random.randn(*s).astype(np.float32) * 0.05)(8, 256))
    _L1_wmod = _w((lambda *s: np.random.randn(*s).astype(np.float32) * 0.05)(256, 6 * 256) * 256 ** (-0.5))
    _d = {'L0_attn_x': _L0_attn_in['x'], 'L0_attn_Wq': _L0_attn_in['Wq'], 'L0_attn_Wk': _L0_attn_in['Wk'], 'L0_attn_Wv': _L0_attn_in['Wv'], 'L0_attn_Wo': _L0_attn_in['Wo'], 'L0_ffn_Wr': _L0_ffn_in['Wr'], 'L0_ffn_Wg': _L0_ffn_in['Wg'], 'L0_ffn_Wu': _L0_ffn_in['Wu'], 'L0_ffn_Wd': _L0_ffn_in['Wd'], 'L0_ffn_Wsg': _L0_ffn_in['Wsg'], 'L0_ffn_Wsu': _L0_ffn_in['Wsu'], 'L0_ffn_Wsd': _L0_ffn_in['Wsd'], 'L0_c': _L0_c, 'L0_wmod': _L0_wmod, 'L1_attn_wq_codes': _L1_attn_in['wq_codes'], 'L1_attn_wq_scales': _L1_attn_in['wq_scales'], 'L1_attn_bq': _L1_attn_in['bq'], 'L1_attn_wk_codes': _L1_attn_in['wk_codes'], 'L1_attn_wk_scales': _L1_attn_in['wk_scales'], 'L1_attn_bk': _L1_attn_in['bk'], 'L1_attn_wv_codes': _L1_attn_in['wv_codes'], 'L1_attn_wv_scales': _L1_attn_in['wv_scales'], 'L1_attn_bv': _L1_attn_in['bv'], 'L1_attn_wo_codes': _L1_attn_in['wo_codes'], 'L1_attn_wo_scales': _L1_attn_in['wo_scales'], 'L1_attn_bo': _L1_attn_in['bo'], 'L1_ffn_router_w': _L1_ffn_in['router_w'], 'L1_ffn_down_w': _L1_ffn_in['down_w'], 'L1_ffn_up_w': _L1_ffn_in['up_w'], 'L1_c': _L1_c, 'L1_wmod': _L1_wmod}
    _x0 = _d['L0_attn_x']
    _d['L0_attn_x'] = jax.random.normal(jax.random.fold_in(jax.random.key(seed), 1), (8, 256, 256), dtype=_x0.dtype)
    del _x0
    return _d

def reference(L0_attn_x, L0_attn_Wq, L0_attn_Wk, L0_attn_Wv, L0_attn_Wo, L0_ffn_Wr, L0_ffn_Wg, L0_ffn_Wu, L0_ffn_Wd, L0_ffn_Wsg, L0_ffn_Wsu, L0_ffn_Wsd, L0_c, L0_wmod, L1_attn_wq_codes, L1_attn_wq_scales, L1_attn_bq, L1_attn_wk_codes, L1_attn_wk_scales, L1_attn_bk, L1_attn_wv_codes, L1_attn_wv_scales, L1_attn_bv, L1_attn_wo_codes, L1_attn_wo_scales, L1_attn_bo, L1_ffn_router_w, L1_ffn_down_w, L1_ffn_up_w, L1_c, L1_wmod):

    def _L0_attn_ref(x, Wq, Wk, Wv, Wo):
        import jax, jax.numpy as jnp
        import numpy as np
        H = 16
        KVH = 4
        G = H // KVH
        HD = 128
        D = 256
        BASE = 10000.0

        def _rope(x, cos, sin):
            half = HD // 2
            x1, x2 = (x[..., :half], x[..., half:])
            return jnp.concatenate([x1 * cos - x2 * sin, x1 * sin + x2 * cos], axis=-1)
        B, S, _ = x.shape
        scale = HD ** (-0.5)
        q = (x @ Wq).reshape(B, S, H, HD).transpose(0, 2, 1, 3)
        k = (x @ Wk).reshape(B, S, KVH, HD).transpose(0, 2, 1, 3)
        v = (x @ Wv).reshape(B, S, KVH, HD).transpose(0, 2, 1, 3)
        t = jnp.arange(S, dtype=x.dtype)
        inv_freq = 1.0 / BASE ** (jnp.arange(0, HD, 2, dtype=x.dtype) / HD)
        freqs = t[:, None] * inv_freq[None, :]
        cos, sin = (jnp.cos(freqs), jnp.sin(freqs))
        q = _rope(q, cos, sin)
        k = _rope(k, cos, sin)
        qg = q.reshape(B, KVH, G, S, HD)
        scores = jnp.einsum('bkgqd,bksd->bkgqs', qg, k) * scale
        causal = jnp.triu(jnp.full((S, S), -jnp.inf, dtype=x.dtype), k=1)
        scores = scores + causal
        attn = jax.nn.softmax(scores, axis=-1)
        out = jnp.einsum('bkgqs,bksd->bkgqd', attn, v)
        out = out.reshape(B, H, S, HD).transpose(0, 2, 1, 3).reshape(B, S, H * HD)
        return out @ Wo

    def _L0_ffn_ref(x, Wr, Wg, Wu, Wd, Wsg, Wsu, Wsd):
        import jax, jax.numpy as jnp
        import numpy as np
        D = 256
        F = 176
        E = 8
        K = 2
        FS = 352
        B, S = (2, 128)
        silu = jax.nn.silu
        sg = silu(jnp.einsum('bsd,fd->bsf', x, Wsg))
        su = jnp.einsum('bsd,fd->bsf', x, Wsu)
        shared_out = jnp.einsum('bsf,df->bsd', sg * su, Wsd)
        logits = jnp.einsum('bsd,ed->bse', x, Wr)
        scores = jax.nn.softmax(logits, axis=-1)
        topk_scores, topk_idx = jax.lax.top_k(scores, K)
        w_full = jnp.sum(jax.nn.one_hot(topk_idx, E, dtype=x.dtype) * topk_scores[..., None], axis=-2)
        g = silu(jnp.einsum('bsd,efd->bsef', x, Wg))
        u = jnp.einsum('bsd,efd->bsef', x, Wu)
        out_e = jnp.einsum('bsef,edf->bsed', g * u, Wd)
        routed_out = jnp.einsum('bsed,bse->bsd', out_e, w_full)
        return routed_out + shared_out

    def _L1_attn_ref(x, wq_codes, wq_scales, bq, wk_codes, wk_scales, bk, wv_codes, wv_scales, bv, wo_codes, wo_scales, bo):
        import jax, jax.numpy as jnp
        import numpy as np
        BLOCK = 32
        NUM_HEADS = 16
        HEAD_DIM = 128
        FP4_GRID = jnp.array([0.0, 0.5, 1.0, 1.5, 2.0, 3.0, 4.0, 6.0], dtype=jnp.float32)

        def quantize_to_mxfp4(w, block_size=BLOCK):
            D, F = w.shape
            blocks = w.reshape(D // block_size, block_size, F)
            amax = jnp.max(jnp.abs(blocks), axis=1)
            e = jnp.floor(jnp.log2(jnp.maximum(amax, 1e-12) / 6.0))
            scale = jnp.exp2(e)
            v = blocks / scale[:, None, :]
            idx = jnp.argmin(jnp.abs(jnp.abs(v)[..., None] - FP4_GRID), axis=-1)
            codes = jnp.sign(v) * FP4_GRID[idx]
            return (codes.reshape(D, F).astype(jnp.float32), scale.astype(jnp.float32))

        def _mxfp4_matmul(x, codes, scales, block_size=BLOCK):
            w = codes * jnp.repeat(scales, block_size, axis=0)
            return x @ w
        B, S, D = x.shape
        q = _mxfp4_matmul(x, wq_codes, wq_scales) + bq
        k = _mxfp4_matmul(x, wk_codes, wk_scales) + bk
        v = _mxfp4_matmul(x, wv_codes, wv_scales) + bv
        q = q.reshape(B, S, NUM_HEADS, HEAD_DIM)
        k = k.reshape(B, S, NUM_HEADS, HEAD_DIM)
        v = v.reshape(B, S, NUM_HEADS, HEAD_DIM)
        scores = jnp.einsum('bqhd,bkhd->bhqk', q, k) / jnp.sqrt(jnp.float32(HEAD_DIM))
        attn = jax.nn.softmax(scores, axis=-1)
        out = jnp.einsum('bhqk,bkhd->bqhd', attn, v).reshape(B, S, NUM_HEADS * HEAD_DIM)
        return _mxfp4_matmul(out, wo_codes, wo_scales) + bo

    def _L1_ffn_ref(x, router_w, down_w, up_w):
        import jax, jax.numpy as jnp
        import numpy as np
        H = 256
        E = 8
        K = 2
        I = 16
        logits = jnp.einsum('bth,eh->bte', x, router_w)
        weights = jax.nn.softmax(logits, axis=-1)
        top_w, top_idx = jax.lax.top_k(weights, K)
        topk_mask = jnp.sum(jax.nn.one_hot(top_idx, E, dtype=x.dtype), axis=-2)
        gate = weights * topk_mask
        h = jnp.einsum('bth,eih->beti', x, down_w)
        a = jax.nn.silu(h)
        expert_out = jnp.einsum('beti,ehi->beth', a, up_w)
        out = jnp.einsum('beth,bte->bth', expert_out, gate)
        return out
    x = L0_attn_x
    mod = (_silu(L0_c) @ L0_wmod).reshape(L0_c.shape[0], 6, 1, -1)
    sa, ca, ga, sb, cb, gb = (mod[:, 0], mod[:, 1], mod[:, 2], mod[:, 3], mod[:, 4], mod[:, 5])
    ga = (2 * (ga >= 0) - 1) * jnp.maximum(jnp.abs(ga), 0.25)
    gb = (2 * (gb >= 0) - 1) * jnp.maximum(jnp.abs(gb), 0.25)
    h = _layernorm(x, axis=-1) * (1 + ca) + sa
    x = x + ga * _L0_attn_ref(h, L0_attn_Wq, L0_attn_Wk, L0_attn_Wv, L0_attn_Wo)
    h = _layernorm(x, axis=-1) * (1 + cb) + sb
    x = x + gb * _L0_ffn_ref(h, L0_ffn_Wr, L0_ffn_Wg, L0_ffn_Wu, L0_ffn_Wd, L0_ffn_Wsg, L0_ffn_Wsu, L0_ffn_Wsd)
    mod = (_silu(L1_c) @ L1_wmod).reshape(L1_c.shape[0], 6, 1, -1)
    sa, ca, ga, sb, cb, gb = (mod[:, 0], mod[:, 1], mod[:, 2], mod[:, 3], mod[:, 4], mod[:, 5])
    ga = (2 * (ga >= 0) - 1) * jnp.maximum(jnp.abs(ga), 0.25)
    gb = (2 * (gb >= 0) - 1) * jnp.maximum(jnp.abs(gb), 0.25)
    h = _layernorm(x, axis=-1) * (1 + ca) + sa
    x = x + ga * _L1_attn_ref(h, L1_attn_wq_codes, L1_attn_wq_scales, L1_attn_bq, L1_attn_wk_codes, L1_attn_wk_scales, L1_attn_bk, L1_attn_wv_codes, L1_attn_wv_scales, L1_attn_bv, L1_attn_wo_codes, L1_attn_wo_scales, L1_attn_bo)
    h = _layernorm(x, axis=-1) * (1 + cb) + sb
    x = x + gb * _L1_ffn_ref(h, L1_ffn_router_w, L1_ffn_down_w, L1_ffn_up_w)
    return x

_drawn_inputs = setup_inputs


def setup_inputs(seed=0):
    import zlib

    import numpy as np

    out = dict(_drawn_inputs(seed))
    spreads = {'L1_attn_bq': (0.0, 0.8),
     'L1_attn_bk': (0.0, 2.0),
     'L1_attn_bv': (0.0, 0.304),
     'L1_attn_bo': (0.0, 2.0)}
    factors = {'L0_attn_Wq': 8.0,
     'L0_attn_Wk': 8.0,
     'L0_attn_Wv': 4.914,
     'L0_attn_Wo': 4.865,
     'L0_ffn_Wr': 8.0,
     'L0_ffn_Wg': 8.0,
     'L0_ffn_Wu': 8.0,
     'L0_ffn_Wd': 8.0,
     'L0_ffn_Wsg': 8.0,
     'L0_ffn_Wsu': 8.0,
     'L0_ffn_Wsd': 8.0,
     'L0_c': 4.453,
     'L0_wmod': 4.348,
     'L1_attn_wq_codes': 3.248,
     'L1_attn_wq_scales': 8.0,
     'L1_attn_wk_codes': 3.181,
     'L1_attn_wk_scales': 8.0,
     'L1_attn_wv_scales': 8.0,
     'L1_attn_wo_scales': 5.361,
     'L1_ffn_router_w': 8.0,
     'L1_ffn_down_w': 8.0,
     'L1_ffn_up_w': 8.0}
    for name, (base, spread) in spreads.items():
        noise = np.random.default_rng([zlib.crc32(name.encode()), seed]).standard_normal(out[name].shape)
        drawn = base * np.exp(spread * noise) if base else spread * noise
        out[name] = jnp.asarray(drawn.astype(out[name].dtype))
    for name, factor in factors.items():
        out[name] = (out[name] * factor).astype(out[name].dtype)
    return out
```

```python
from contextlib import ExitStack

import concourse.bass as bass
from concourse import mybir
from concourse.alu_op_type import AluOpType as ALU

F32 = mybir.dt.float32
F32R = mybir.dt.float32r
U32 = mybir.dt.uint32
ACT = mybir.ActivationFunctionType
AX = mybir.AxisListType

P = 128
B, S, D = 8, 256, 256
TOK = 2 * S
NP = B // 2
NT = TOK // P
NC = D // P
HEADS, HD = 16, 128
HG = 4
NG = HEADS // HG
E = 8
F0, FS = 176, 352
NR = E * F0 // P
NSH = -(-FS // P)
NJ = NR + NSH
LASTW = FS - (NSH - 1) * P
EPS = 1e-5
SCALE = float(HD) ** -0.5
MASKED = -1e30
SA, CA, GA, SB, CB, GB = range(6)
PASSES = ((1, 0), (0, 1), (0, 0))
PIECE = 512


def width(j):
    return LASTW if j == NJ - 1 else P


class Weights:

    def __init__(self, shared_kv):
        self.shared_kv = shared_kv
        self.pieces = 5 if shared_kv else 8

    def q(self, w, hl, c, h):
        return w[:, c, hl, h * HD:(h + 1) * HD]

    def k(self, w, hl, c, h):
        if self.shared_kv:
            return w[:, 2, hl, c * HD:(c + 1) * HD]
        return w[:, 2 + c, hl, h * HD:(h + 1) * HD]

    def v(self, w, hl, c):
        if self.shared_kv:
            return w[:, 2, hl, (2 + c) * HD:(3 + c) * HD]
        return w[:, 4 + c, hl, :]

    def o(self, w, hl, h, c):
        piece = (3 if self.shared_kv else 6) + h // 2
        return w[:, piece, hl, (h % 2) * D + c * P:(h % 2) * D + (c + 1) * P]


class NormSems:
    def __init__(self, sem, name, residual=True, norm=True):
        if residual:
            self.scaled = sem(name + "_branch_scaled")
            self.back = sem(name + "_branch_turned")
            self.x_new = sem(name + "_x_new")
        if not norm:
            return
        self.mod = sem(name + "_mod_copied")
        self.stats = sem(name + "_stats")
        self.aggr = sem(name + "_aggr")
        self.var = sem(name + "_var_eps")
        self.rstd = sem(name + "_rstd")
        self.xhat = sem(name + "_xhat")
        self.turned = sem(name + "_xhat_turned")
        self.h = sem(name + "_h")
        self.hi = sem(name + "_h_hi")
        self.lo = sem(name + "_h_lo")
        self.passed = sem(name + "_passed")


def scale_branch(act, s, p, y_of, gate, bias, ys, batches=2):
    for c in range(NC):
        for b in range(batches):
            kw = {} if bias is None else {"bias": bias[:, c, b:b + 1]}
            act.activation(ys[:, c, b * S:(b + 1) * S], y_of(c, b), ACT.Identity,
                           scale=gate[:, c, b:b + 1], **kw).then_inc(s.scaled, 1)


def turn_branch(pe, s, p, ys, ident, banks):
    pe.wait_ge(s.scaled, p * 4 + 4)
    for half in range(2):
        for t in (2 * half, 2 * half + 1):
            for c in range(NC):
                mm = pe.transpose(banks[half][:, (t % 2) * D + c * P:(t % 2) * D + (c + 1) * P],
                                  ys[:, c, t * P:(t + 1) * P], ident[:, :])
        mm.then_inc(s.back, 1)


def add_branch(dve, s, p, x, banks):
    for half in range(2):
        dve.wait_ge(s.back, p * 2 + half + 1)
        xs = x[:, 2 * half:2 * half + 2, :].rearrange("p t d -> p (t d)")
        dve.tensor_tensor(xs, xs, banks[half][:, :], ALU.add).then_inc(s.x_new, 1)


def norm_dve(dve, s, p, x, tmp):
    for t in range(NT):
        dve.bn_stats(tmp.stats[:, t, :], x[:, t, :]).then_inc(s.stats, 1)
    hold(dve, s.stats, p * 4 + 4, s.passed)
    for t in range(NT):
        dve.bn_aggr(tmp.mv[:, t, :], tmp.stats[:, t, :]).then_inc(s.aggr, 1)
    dve.wait_ge(s.aggr, p * 4 + 4)
    dve.tensor_scalar(tmp.var[:, :], tmp.mv[:, :, 1], EPS, None, ALU.add).then_inc(s.var, 1)
    dve.wait_ge(s.rstd, p + 1)
    for t in range(NT):
        dve.tensor_scalar(tmp.xhat[:, t, :], x[:, t, :], tmp.mv[:, t, 0:1], tmp.rstd[:, t:t + 1],
                          ALU.subtract, ALU.mult).then_inc(s.xhat, 1)


def norm_pool(pool, s, p, tmp, minus_half):
    pool.wait_ge(s.var, p + 1)
    pool.tensor_tensor(tmp.rstd[:, :], tmp.var[:, :], minus_half[:, :], ALU.pow).then_inc(s.rstd, 1)


def turn_norm(pe, s, p, tmp, ident, banks):
    pe.wait_ge(s.xhat, p * 4 + 4)
    for c in range(NC):
        for t in range(NT):
            mm = pe.transpose(banks[c][:, t * P:(t + 1) * P], tmp.xhat[:, t, c * P:(c + 1) * P],
                              ident[:, :])
        mm.then_inc(s.turned, 1)


def modulate(act, s, p, shift, scale1, tmp, banks):
    for c in range(NC):
        act.wait_ge(s.turned, p * 2 + c + 1)
        for b in range(2):
            act.activation(tmp.h[:, c, b * S:(b + 1) * S], banks[c][:, b * S:(b + 1) * S],
                           ACT.Identity, bias=shift[:, c, b:b + 1],
                           scale=scale1[:, c, b:b + 1]).then_inc(s.h, 1)


def split_h(dve, s, p, tmp, hT):
    for c in range(NC):
        dve.wait_ge(s.h, p * 4 + 2 * c + 2)
        dve.tensor_copy(hT[:, 0, c, :], tmp.h[:, c, :]).then_inc(s.hi, 1)
        dve.wait_ge(s.hi, p * 2 + c + 1)
        dve.tensor_tensor(hT[:, 1, c, :], tmp.h[:, c, :], hT[:, 0, c, :].bitcast(F32),
                          ALU.subtract).then_inc(s.lo, 1)


def copy_mod(dve, s, p, mod, cur):
    dve.tensor_copy(cur[:, :, :], mod[:, :, bass.ds(p * 2, 2)]).then_inc(s.mod, 1)


class NormTiles:
    def __init__(self, sb):
        self.stats = sb("stats", [P, NT, 6])
        self.mv = sb("mv", [P, NT, 2])
        self.var = sb("var", [P, NT])
        self.rstd = sb("rstd", [P, NT])
        self.xhat = sb("xhat", [P, NT, D])
        self.h = sb("h_full", [P, NC, TOK])


def kinds(cur, kind):
    return cur[:, kind * NC:(kind + 1) * NC, :]


class RouterSems:
    def __init__(self, sem, name):
        self.logits = sem(name + "_logits")
        self.step = sem(name + "_step")
        self.shifted = sem(name + "_shifted")
        self.exp = sem(name + "_exp")
        self.weights = sem(name + "_weights")
        self.turned = sem(name + "_turned")
        self.wT = sem(name + "_wT")
        self.passed = sem(name + "_passed")

    STEPS = 5 + 2 * NT + 5


class RouterTiles:
    def __init__(self, sb):
        self.nmax = sb("r_nmax", [P, NT])
        self.shifted = sb("r_shifted", [P, NT, E])
        self.exp = sb("r_exp", [P, NT, E])
        self.sum = sb("r_sum", [P, NT])
        self.inv = sb("r_inv", [P, NT])
        self.score = sb("r_score", [P, NT, E])
        self.top = sb("r_top", [P, NT, E])
        self.at = sb("r_at", [P, NT, E], U32)
        self.first = sb("r_first", [P, NT, E])
        self.second = sb("r_second", [P, NT, E])
        self.w = sb("r_w", [P, NT, E])
        self.whl = sb("r_whl", [P, NT, 2 * E], F32R)
        self.wT = sb("r_wT", [2 * E, TOK], F32R)


def router_pe(pe, s, p, hT, wr, bank):
    for t in range(NT):
        for n, (c, (a, m)) in enumerate((c, pm) for c in range(NC) for pm in PASSES):
            mm = pe.matmul(bank[:, t * E:(t + 1) * E], hT[:, a, c, t * P:(t + 1) * P],
                           wr[:, m, c, :], start=(n == 0), stop=(n == NC * len(PASSES) - 1))
    mm.then_inc(s.logits, 1)


def router_turn(pe, s, p, r, ident, bank):
    pe.wait_ge(s.weights, p + 1)
    for t in range(NT):
        mm = pe.transpose(bank[0:2 * E, t * P:(t + 1) * P], r.whl[:, t, :].bitcast(F32), ident[:, :])
    mm.then_inc(s.turned, 1)


def router_exp(act, s, p, r):
    act.wait_ge(s.shifted, p + 1)
    act.activation(r.exp[:, :, :], r.shifted[:, :, :], ACT.Exp).then_inc(s.exp, 1)


def router_copy(act, s, p, r, bank):
    act.wait_ge(s.turned, p + 1)
    act.activation(r.wT[:, :], bank[0:2 * E, :], ACT.Identity).then_inc(s.wT, 1)


def router_dve(dve, s, p, r, iota8, bank):
    base = p * RouterSems.STEPS
    n = 0

    def link(ins):
        nonlocal n
        n += 1
        ins.then_inc(s.step, 1)
        hold(dve, s.step, base + n, s.passed)

    def rows(v):
        return v.broadcast_to([P, NT, E])

    logits = bank[:, 0:NT * E].rearrange("p (t e) -> p t e", e=E)
    dve.wait_ge(s.logits, p + 1)
    link(dve.tensor_reduce(r.nmax[:, :], logits, AX.X, ALU.max, negate=True))
    dve.tensor_tensor(r.shifted[:, :, :], logits, rows(r.nmax[:, :, None]), ALU.add).then_inc(s.shifted, 1)
    dve.wait_ge(s.exp, p + 1)
    link(dve.tensor_reduce(r.sum[:, :], r.exp[:, :, :], AX.X, ALU.add))
    link(dve.reciprocal(r.inv[:, :], r.sum[:, :]))
    link(dve.tensor_tensor(r.score[:, :, :], r.exp[:, :, :], rows(r.inv[:, :, None]), ALU.mult))
    for t in range(NT):
        link(dve.max(r.top[:, t, :], r.score[:, t, :]))
        link(dve.max_index(r.at[:, t, :], r.top[:, t, :], r.score[:, t, :]))
    places = iota8[:, None, :].broadcast_to([P, NT, E])
    link(dve.tensor_tensor(r.first[:, :, :], places, rows(r.at[:, :, 0:1]), ALU.is_equal))
    link(dve.tensor_tensor(r.second[:, :, :], places, rows(r.at[:, :, 1:2]), ALU.is_equal))
    link(dve.tensor_tensor(r.first[:, :, :], r.first[:, :, :], r.second[:, :, :], ALU.add))
    link(dve.tensor_tensor(r.w[:, :, :], r.score[:, :, :], r.first[:, :, :], ALU.mult))
    link(dve.tensor_copy(r.whl[:, :, 0:E], r.w[:, :, :]))
    link(dve.tensor_tensor(r.whl[:, :, E:2 * E], r.w[:, :, :], r.whl[:, :, 0:E].bitcast(F32), ALU.subtract))
    dve.nop().then_inc(s.weights, 1)
    assert n == RouterSems.STEPS


def ge(eng, sem, value):
    if not isinstance(value, int) or value > 0:
        eng.wait_ge(sem, value)


def hold(eng, sem, value, passed):
    eng.wait_ge(sem, value)
    eng.sem_inc(passed)


def over_pairs(eng, group, body):
    body(group, 0)
    with eng.Fori(1, NP - 1) as p:
        body(group, p)
    body(group, NP - 1)


def step_of(group, pair):
    return pair + group * NP


def split_matmuls(pe, out, pairs):
    total = len(pairs) * len(PASSES)
    for i, (pair, (a, m)) in enumerate((pair, pm) for pair in pairs for pm in PASSES):
        mm = pe.matmul(out, pair[0](a), pair[1](m), start=(i == 0), stop=(i == total - 1))
    return mm


class Attention:

    def __init__(self, nc, ctx, held, layer, nq, nk, vcols, score_cols, depth):
        def sb(n, shape, dt=F32):
            return ctx.enter_context(nc.sbuf_tensor(f"a{layer}_{n}", shape, dt))

        def sem(n):
            held.append(nc.alloc_semaphore(f"a{layer}_{n}"))
            return held[-1]

        self.hT = sb("hT", [P, 2, NC, TOK], F32R)
        self.qT = sb("qT", [P, nq, 2, TOK], F32R)
        self.kT = sb("kT", [P, nk, 2, TOK], F32R)
        self.v = sb("v", [P, 2, NT, vcols], F32R)
        self.depth = depth
        self.prob = sb("prob", [P, depth, 2, score_cols])
        self.probT = sb("probT", [P, 2, 2, score_cols], F32R)
        self.oT = sb("oT", [P, 2, 2, TOK], F32R)
        self.nmax = sb("nmax", [P, 2, 2])
        self.total = sb("total", [P, depth, 2, 2])
        self.inv = sb("inv", [P, depth, 2, 2])
        self.h_loaded = sem("h_loaded")
        self.w_loaded = sem("w_loaded")
        self.q_mm, self.k_mm, self.v_mm = sem("q_mm"), sem("k_mm"), sem("v_mm")
        self.v_hi, self.v_lo = sem("v_hi"), sem("v_lo")
        self.s_mm, self.t_mm, self.pv_mm = sem("s_mm"), sem("t_mm"), sem("pv_mm")
        self.o_mm = sem("o_mm")
        self.max_done, self.exp_done = sem("max"), sem("exp")
        self.inv_done, self.norm_done = sem("inv"), sem("norm")
        self.t_hi, self.t_lo = sem("t_hi"), sem("t_lo")
        self.o_hi, self.o_lo = sem("o_hi"), sem("o_lo")
        self.y_done = sem("y_done")
        self.sb, self.sem = sb, sem

    def scores(self, pe, n, b, k, parts, banks, par, mask=None):
        ge(pe, self.exp_done, n * 2 + (b - 1))
        for qt, (col, keys) in enumerate(parts):
            out = banks[b][:, col:col + keys]
            for i, (a, m) in enumerate(PASSES):
                mm = pe.matmul(out, self.qT[:, par, a, b * S + qt * P:b * S + (qt + 1) * P],
                               k(m)[:, b * S:b * S + keys], start=(i == 0),
                               stop=(mask is None and i == len(PASSES) - 1))
            if mask is not None:
                mm = pe.matmul(banks[b][:, col + keys - P:col + keys], mask[0][:, :],
                               mask[1][:, :], start=False, stop=True)
        mm.then_inc(self.s_mm, 1)

    def turn_probs(self, pe, n, h, b, parts, bank, ident):
        pe.wait_ge(self.norm_done, n * 2 + (b + 1))
        ge(pe, self.t_lo, n * 2 + b)
        for src, dst in parts:
            mm = pe.transpose(bank[:, dst:dst + P], self.prob[:, h % self.depth, b, src:src + P], ident[:, :])
        mm.then_inc(self.t_mm, 1)

    def times_v(self, pe, n, vcol, parts, bank, score_cols):
        ge(pe, self.o_lo, n)
        for b in range(2):
            pe.wait_ge(self.t_lo, n * 2 + (b + 1))
            total = len(parts) * len(PASSES)
            for i, ((kt, col, w, q0), (a, m)) in enumerate((x, pm) for x in parts for pm in PASSES):
                mm = pe.matmul(bank[:, b * S + q0:b * S + q0 + w],
                               self.v[:, a, 2 * b + kt, vcol:vcol + HD],
                               self.probT[:, b, m, col:col + w], start=(i == 0), stop=(i == total - 1))
            mm.then_inc(self.pv_mm, 1)

    def project_out(self, pe, n, h, step, wts, w, banks):
        pe.wait_ge(self.o_lo, n + 1)
        if h == 0:
            ge(pe, self.y_done, step * 2)
        for c in range(NC):
            for i, (a, m) in enumerate(PASSES):
                mm = pe.matmul(banks[c][:, :], wts.o(w, a, h, c), self.oT[:, h % 2, m, :],
                               start=(h == 0 and i == 0), stop=(h == HG - 1 and i == len(PASSES) - 1))
        mm.then_inc(self.o_mm, 1)

    def exponentials(self, act, n, h, b, parts, banks):
        act.wait_ge(self.max_done, n * 2 + (b + 1))
        ge(act, self.t_mm, n * 2 + (b + 1 - 2 * self.depth))
        for qt, (col, keys) in enumerate(parts):
            ins = act.activation(self.prob[:, h % self.depth, b, col:col + keys], banks[b][:, col:col + keys],
                                 ACT.Exp, bias=self.nmax[:, b, qt:qt + 1],
                                 accum_out=self.total[:, h % self.depth, b, qt:qt + 1])
        ins.then_inc(self.exp_done, 1)

    def probs_hi(self, act, n, b, bank, cols):
        act.wait_ge(self.t_mm, n * 2 + (b + 1))
        ge(act, self.pv_mm, n * 2 + (b - 1))
        act.activation(self.probT[:, b, 0, :], bank[:, 0:cols], ACT.Identity).then_inc(self.t_hi, 1)

    def out_hi(self, act, n, h, bank, bias):
        act.wait_ge(self.pv_mm, n * 2 + 2)
        ge(act, self.o_mm, n - 1)
        kw = {} if bias is None else {"bias": bias}
        act.activation(self.oT[:, h % 2, 0, :], bank[:, :], ACT.Identity, **kw).then_inc(self.o_hi, 1)

    def maxima(self, dve, n, b, parts, banks):
        dve.wait_ge(self.s_mm, n * 2 + (b + 1))
        if len({keys for _, keys in parts}) == 1:
            cols = sum(keys for _, keys in parts)
            ins = dve.tensor_reduce(self.nmax[:, b, :], banks[b][:, 0:cols].rearrange(
                "p (q k) -> p q k", q=len(parts)), AX.X, ALU.max, negate=True)
        else:
            for qt, (col, keys) in enumerate(parts):
                ins = dve.tensor_reduce(self.nmax[:, b, qt:qt + 1], banks[b][:, col:col + keys],
                                        AX.X, ALU.max, negate=True)
        ins.then_inc(self.max_done, 1)

    def inverses(self, dve, n, h, b):
        dve.wait_ge(self.exp_done, n * 2 + (b + 1))
        dve.reciprocal(self.inv[:, h % self.depth, b, :],
                       self.total[:, h % self.depth, b, :]).then_inc(self.inv_done, 1)

    def normalize(self, eng, n, h, b, parts):
        eng.wait_ge(self.inv_done, n * 2 + (b + 1))
        for qt, (col, keys) in enumerate(parts):
            pr = self.prob[:, h % self.depth, b, col:col + keys]
            inv = self.inv[:, h % self.depth, b, qt:qt + 1]
            if self.depth == 1:
                ins = eng.tensor_scalar(pr, pr, inv, None, ALU.mult)
            else:
                ins = eng.activation(pr, pr, ACT.Identity, scale=inv)
        ins.then_inc(self.norm_done, 1)

    def probs_lo(self, dve, n, b, bank, cols):
        dve.wait_ge(self.t_hi, n * 2 + (b + 1))
        dve.tensor_tensor(self.probT[:, b, 1, :], bank[:, 0:cols],
                          self.probT[:, b, 0, :].bitcast(F32), ALU.subtract).then_inc(self.t_lo, 1)

    def out_lo(self, dve, n, h, bank, bias):
        dve.wait_ge(self.o_hi, n + 1)
        o = self.oT[:, h % 2, :, :]
        if bias is None:
            ins = dve.tensor_tensor(o[:, 1, :], bank[:, :], o[:, 0, :].bitcast(F32), ALU.subtract)
        else:
            ins = dve.scalar_tensor_tensor(out=o[:, 1, :], in0=bank[:, :], scalar=bias,
                                           in1=o[:, 0, :].bitcast(F32), op0=ALU.add, op1=ALU.subtract)
        ins.then_inc(self.o_lo, 1)

    def take_sums(self, dve, step, group, pair, yacc, banks):
        dve.wait_ge(self.o_mm, step * HG + HG)
        for c in range(NC):
            y = yacc[:, c, bass.ds(pair * TOK, TOK)]
            if group == 0:
                ins = dve.tensor_copy(y, banks[c][:, :])
            else:
                ins = dve.tensor_tensor(y, banks[c][:, :], y, ALU.add)
            ins.then_inc(self.y_done, 1)


def before(group, pair):
    if isinstance(pair, int) and pair == 0:
        return (group - 1, NP - 1) if group else None
    return group, pair - 1


def after(group, pair):
    if isinstance(pair, int) and pair == NP - 1:
        return (group + 1, 0) if group < NG - 1 else None
    return group, pair + 1


def back(group, pair, h, by):
    if h >= by:
        return group, pair, h - by
    prev = before(group, pair)
    return None if prev is None else (*prev, h - by + HG)


def ahead(group, pair, h, by):
    if h + by < HG:
        return group, pair, h + by
    nxt = after(group, pair)
    return None if nxt is None else (*nxt, h + by - HG)


def slot_of(where):
    group, pair, h = where
    return pair * HG + (group * NP * HG + h)


def load_steps(sp, a, h_dram, w_dram, wbuf, used, per_step):
    def weights(group):
        sp.dma_start(wbuf[group % 2].bitcast(F32).rearrange("p n a w -> p (n a w)"),
                     w_dram[group]).then_inc(a.w_loaded, 16)

    weights(0)
    for it in range(NG * NP):
        ge(sp, used, it * per_step)
        sp.dma_start(a.hT[:, :, :, :].bitcast(F32).rearrange("p a c t -> p (a c t)"),
                     h_dram[it % NP]).then_inc(a.h_loaded, 16)
        group = it // NP + 1
        if it % NP == 1 and group < NG:
            ge(sp, a.o_mm, (group - 1) * NP * HG)
            weights(group)


def attention0(nc, held, wbuf, h_dram, w_dram, yacc, bank, const):
    wts = Weights(True)
    s_parts = ((0, P), (P, 2 * P))
    t_parts = ((0, 0), (P, P), (2 * P, 2 * P))
    pv_parts = ((0, 0, 2 * P, 0), (1, 2 * P, P, P))
    cols = 3 * P
    b_q, b_k, b_s, b_t, b_o, b_y = bank[0], bank[1], bank[2:4], bank[4], bank[5], bank[6:8]
    ROT = HG + 1

    def q_turn(where):
        group, pair, h = where
        return pair * ROT + (group * NP * ROT + (h + 1))

    def k_turn(step):
        return step * ROT

    def k_buf(pair):
        return (pair + 1) % 2 if isinstance(pair, int) else pair - 1

    def k_buf_after(group, pair):
        return pair % 2 if isinstance(pair, int) else pair * -1 + 2

    with ExitStack() as ctx:
        a = Attention(nc, ctx, held, 0, HG, 2, HD, cols, 2)
        turned, direct, full = a.sb("turned", [P, TOK]), a.sb("direct", [P, TOK]), a.sb("full", [P, TOK])
        rot_half = a.sem("rot_half")
        rot_direct, rot_sin = a.sem("rot_direct"), a.sem("rot_sin")
        rot_hi, rot_full, rot_lo = a.sem("rot_hi"), a.sem("rot_full"), a.sem("rot_lo")
        first, last_slot = (0, 0, 0), (NG - 1, NP - 1, HG - 1)
        block = ctx.enter_context(nc.Block())


        @block.sync
        def _(sp):
            load_steps(sp, a, h_dram, w_dram, wbuf, a.q_mm, HG)

        @block.tensor
        def _(pe):
            def project(bank_, w_of, mm_done):
                split_matmuls(pe, bank_[:, :], [(lambda hl, c=c: w_of(hl, c), lambda hl, c=c: a.hT[:, hl, c, :])
                                                for c in range(NC)]).then_inc(mm_done, 1)

            def q(where):
                group, pair, h = where
                ge(pe, rot_direct, q_turn(where) - (0 if h else 1))
                project(b_q, lambda hl, c: wts.q(wbuf[group % 2], hl, c, h), a.q_mm)

            def k(group, pair):
                step = step_of(group, pair)
                pe.wait_ge(a.h_loaded, step * 16 + 16)
                if isinstance(pair, int) and pair == 0:
                    pe.wait_ge(a.w_loaded, group * 16 + 16)
                ge(pe, a.v_lo, step)
                project(b_k, lambda hl, c: wts.k(wbuf[group % 2], hl, c, 0), a.k_mm)

            def v(group, pair):
                pe.wait_ge(rot_direct, k_turn(step_of(group, pair)) + 1)
                for t in range(NT):
                    mm = split_matmuls(pe, b_k[:, t * HD:(t + 1) * HD],
                                       [(lambda hl, c=c: a.hT[:, hl, c, t * P:(t + 1) * P],
                                         lambda hl, c=c: wts.v(wbuf[group % 2], hl, c)) for c in range(NC)])
                mm.then_inc(a.v_mm, 1)

            def scores(where, b, kb):
                group, pair, h = where
                pe.wait_ge(rot_lo, q_turn(where) + 1)
                a.scores(pe, slot_of(where), b, lambda hl: a.kT[:, kb, hl, :], s_parts, b_s, h,
                         (const.ident_r, const.mask_r))

            def pv(where):
                group, pair, h = where
                if h == 0:
                    pe.wait_ge(a.v_lo, step_of(group, pair) + 1)
                a.times_v(pe, slot_of(where), 0, pv_parts, b_o, cols)

            def out(where):
                group, pair, h = where
                a.project_out(pe, slot_of(where), h, step_of(group, pair), wts, wbuf[group % 2], b_y)

            def body(group, pair):
                nxt = after(group, pair)
                for h in range(HG):
                    n = slot_of((group, pair, h))
                    head, last, last2 = (ahead(group, pair, h, 1), back(group, pair, h, 1),
                                         back(group, pair, h, 2))
                    kb = k_buf(pair) if h < HG - 1 else k_buf_after(group, pair)
                    if h == HG - 1:
                        if last2 is not None:
                            out(last2)
                    elif head is not None:
                        scores(head, 0, kb)
                    if last is not None:
                        pv(last)
                    a.turn_probs(pe, n, h, 0, t_parts, b_t, const.ident)
                    if h == HG - 1 and head is not None:
                        scores(head, 0, kb)
                    if head is not None:
                        scores(head, 1, kb)
                    if h == 0:
                        v(group, pair)
                        q((group, pair, 3))
                    if h < HG - 1 and last2 is not None:
                        out(last2)
                    if h == 1 and nxt is not None:
                        k(*nxt)
                        q((*nxt, 0))
                    a.turn_probs(pe, n, h, 1, t_parts, b_t, const.ident)
                    if h >= 2 and nxt is not None:
                        q((*nxt, h - 1))

            k(0, 0)
            for h in range(3):
                q((0, 0, h))
            for b in range(2):
                scores(first, b, k_buf(0))
            for group in range(NG):
                over_pairs(pe, group, body)
            pv(last_slot)
            out((NG - 1, NP - 1, HG - 2))
            out(last_slot)

        @block.scalar
        def _(act):
            def halves(turn, b, mm_done, count):
                act.wait_ge(mm_done, count)
                ge(act, rot_hi, turn)
                ge(act, rot_full, turn)
                H = HD // 2
                act.activation(turned[0:H, :], b[H:HD, :], ACT.Identity).then_inc(rot_half, 1)
                act.activation(turned[H:HD, :], b[0:H, :], ACT.Identity).then_inc(rot_half, 1)

            def q(where):
                halves(q_turn(where), b_q, a.q_mm, slot_of(where) + 1)

            def k(group, pair):
                step = step_of(group, pair)
                halves(k_turn(step), b_k, a.k_mm, step + 1)

            def normalize(where):
                group, pair, h = where
                for b in range(2):
                    a.normalize(act, slot_of(where), h, b, s_parts)

            def body(group, pair):
                step = step_of(group, pair)
                nxt = after(group, pair)
                for h in range(HG):
                    n = slot_of((group, pair, h))
                    head, last = ahead(group, pair, h, 1), back(group, pair, h, 1)
                    if last is not None:
                        a.out_hi(act, slot_of(last), last[2], b_o, None)
                    a.probs_hi(act, n, 0, b_t, cols)
                    if h == 2 and nxt is not None:
                        q((*nxt, 0))
                    if head is not None:
                        for b in range(2):
                            a.exponentials(act, slot_of(head), head[2], b, s_parts, b_s)
                    if h == 0:
                        act.wait_ge(a.v_mm, step + 1)
                        ge(act, a.pv_mm, step * HG * 2)
                        act.activation(a.v[:, 0, :, :].rearrange("p t d -> p (t d)"), b_k[:, :],
                                       ACT.Identity).then_inc(a.v_hi, 1)
                    if h == 1 and nxt is not None:
                        k(*nxt)
                    a.probs_hi(act, n, 1, b_t, cols)
                    if head is not None:
                        normalize(head)
                    if h == 0:
                        q((group, pair, 3))
                    if h >= 2 and nxt is not None:
                        q((*nxt, h - 1))

            k(0, 0)
            for h in range(3):
                q((0, 0, h))
            for b in range(2):
                a.exponentials(act, 0, 0, b, s_parts, b_s)
            normalize(first)
            for group in range(NG):
                over_pairs(act, group, body)
            a.out_hi(act, slot_of(last_slot), HG - 1, b_o, None)

        @block.vector
        def _(dve):
            def turn_direct(turn, b, cos):
                dve.wait_ge(rot_half, turn * 2 + 2)
                ge(dve, rot_full, turn)
                for i in range(2):
                    ins = dve.tensor_tensor(direct[:, i * S:(i + 1) * S], b[:, i * S:(i + 1) * S],
                                            cos[:, :], ALU.mult)
                ins.then_inc(rot_direct, 1)

            def turn_hi(turn, dst, reader):
                ge(dve, a.s_mm, reader)
                dve.wait_ge(rot_direct, turn + 1)
                dve.wait_ge(rot_sin, turn + 1)
                dve.tensor_tensor(dst, direct[:, :], turned[:, :], ALU.add).then_inc(rot_hi, 1)

            def q_direct(where):
                turn_direct(q_turn(where), b_q, const.cos_q)

            def q_hi(where):
                turn_hi(q_turn(where), a.qT[:, where[2], 0, :], slot_of(where) * 2 - 2 * (HG - 1))

            def k_direct(group, pair):
                turn_direct(k_turn(step_of(group, pair)), b_k, const.cos_k)

            def k_hi(group, pair, buf):
                step = step_of(group, pair)
                turn_hi(k_turn(step), a.kT[:, buf, 0, :], (step - 1) * HG * 2)

            def body(group, pair):
                step = step_of(group, pair)
                nxt, prev = after(group, pair), before(group, pair)
                for h in range(HG):
                    n = slot_of((group, pair, h))
                    head, last = ahead(group, pair, h, 1), back(group, pair, h, 1)
                    late = h == HG - 1
                    turning = (group, pair, h + 2) if h < 2 else (*nxt, 1) if late and nxt is not None else None
                    if h == 2 and nxt is not None:
                        k_direct(*nxt)
                    if head is not None and not late:
                        a.maxima(dve, slot_of(head), 0, s_parts, b_s)
                    if turning is not None:
                        q_direct(turning)
                    if h == 2 and nxt is not None:
                        k_hi(*nxt, k_buf_after(group, pair))
                    if last is not None:
                        a.out_lo(dve, slot_of(last), last[2], b_o, None)
                    a.probs_lo(dve, n, 0, b_t, cols)
                    if h == 2 and nxt is not None:
                        q_direct((*nxt, 0))
                    if head is not None:
                        if late:
                            a.maxima(dve, slot_of(head), 0, s_parts, b_s)
                        a.maxima(dve, slot_of(head), 1, s_parts, b_s)
                    if turning is not None:
                        q_hi(turning)
                    if h == 2 and nxt is not None:
                        q_hi((*nxt, 0))
                    if h == 0:
                        dve.wait_ge(a.v_hi, step + 1)
                        dve.tensor_tensor(a.v[:, 1, :, :].rearrange("p t d -> p (t d)"), b_k[:, :],
                                          a.v[:, 0, :, :].bitcast(F32).rearrange("p t d -> p (t d)"),
                                          ALU.subtract).then_inc(a.v_lo, 1)
                    if head is not None:
                        for b in range(2):
                            a.inverses(dve, slot_of(head), head[2], b)
                    if h == 1 and prev is not None:
                        a.take_sums(dve, step_of(*prev), *prev, yacc, b_y)
                    a.probs_lo(dve, n, 1, b_t, cols)

            k_direct(0, 0)
            k_hi(0, 0, k_buf(0))
            for h in range(2):
                q_direct((0, 0, h))
                q_hi((0, 0, h))
            for b in range(2):
                a.maxima(dve, 0, b, s_parts, b_s)
            for b in range(2):
                a.inverses(dve, 0, 0, b)
            for group in range(NG):
                over_pairs(dve, group, body)
            a.out_lo(dve, slot_of(last_slot), HG - 1, b_o, None)
            a.take_sums(dve, NG * NP - 1, NG - 1, NP - 1, yacc, b_y)

        @block.gpsimd
        def _(pool):
            def rotate(turn, sin, dst):
                pool.wait_ge(rot_half, turn * 2 + 2)
                for i in range(2):
                    half = turned[:, i * S:(i + 1) * S]
                    ins = pool.tensor_tensor(half, half, sin[:, :], ALU.mult)
                ins.then_inc(rot_sin, 1)
                pool.wait_ge(rot_direct, turn + 1)
                pool.wait_ge(rot_sin, turn + 1)
                ge(pool, rot_lo, turn)
                pool.tensor_tensor(full[:, :], direct[:, :], turned[:, :], ALU.add).then_inc(rot_full, 1)
                pool.wait_ge(rot_full, turn + 1)
                pool.wait_ge(rot_hi, turn + 1)
                pool.tensor_tensor(dst[:, 1, :], full[:, :], dst[:, 0, :].bitcast(F32),
                                   ALU.subtract).then_inc(rot_lo, 1)

            def q(where):
                rotate(q_turn(where), const.sin_q, a.qT[:, where[2], :, :])

            def k(group, pair, buf):
                rotate(k_turn(step_of(group, pair)), const.sin_k, a.kT[:, buf, :, :])

            def body(group, pair):
                nxt = after(group, pair)
                q((group, pair, 3))
                if nxt is not None:
                    k(*nxt, k_buf_after(group, pair))
                    for h in range(3):
                        q((*nxt, h))

            k(0, 0, k_buf(0))
            for h in range(3):
                q((0, 0, h))
            for group in range(NG):
                over_pairs(pool, group, body)


def attention1(nc, held, wbuf, h_dram, w_dram, yacc, bank, const):
    wts = Weights(False)
    s_parts = ((0, 2 * P), (2 * P, 2 * P))
    t_parts = tuple((qt * 2 * P + kt * P, kt * 2 * P + qt * P) for kt in range(2) for qt in range(2))
    pv_parts = ((0, 0, 2 * P, 0), (1, 2 * P, 2 * P, 0))
    cols = 4 * P
    b_qk, b_s, b_t, b_o, b_y = bank[0:2], bank[2:4], bank[4], bank[5], bank[6:8]

    def bias(kind, where):
        col = kind * HEADS + where[0] * HG + where[2]
        return const.biasT[:, col:col + 1]

    with ExitStack() as ctx:
        a = Attention(nc, ctx, held, 1, 2, 2, HG * HD, cols, 1)
        buf = (a.qT, a.kT)
        mm_done = (a.q_mm, a.k_mm)
        hi_done, lo_done = (a.sem("q_hi"), a.sem("k_hi")), (a.sem("q_lo"), a.sem("k_lo"))
        block = ctx.enter_context(nc.Block())

        @block.sync
        def _(sp):
            load_steps(sp, a, h_dram, w_dram, wbuf, a.k_mm, HG)

        @block.tensor
        def _(pe):
            def qk(where):
                group, pair, h = where
                n = slot_of(where)
                if h == 0:
                    pe.wait_ge(a.h_loaded, step_of(group, pair) * 16 + 16)
                    if isinstance(pair, int) and pair == 0:
                        pe.wait_ge(a.w_loaded, group * 16 + 16)
                for i in range(2):
                    if h == 2:
                        pe.wait_ge(a.v_lo, step_of(group, pair) * NT + (i + 3))
                    else:
                        ge(pe, lo_done[i], n)
                    w_of = (wts.q, wts.k)[i]
                    split_matmuls(pe, b_qk[i][:, :],
                                  [(lambda hl, c=c: w_of(wbuf[group % 2], hl, c, h),
                                    lambda hl, c=c: a.hT[:, hl, c, :]) for c in range(NC)]
                                  ).then_inc(mm_done[i], 1)

            def v(group, pair, t):
                step = step_of(group, pair)
                if t < 2:
                    pe.wait_ge(lo_done[t], step * HG + 2)
                else:
                    pe.wait_ge(a.v_lo, step * NT + (t - 1))
                split_matmuls(pe, b_qk[t % 2][:, :],
                              [(lambda hl, c=c: a.hT[:, hl, c, t * P:(t + 1) * P],
                                lambda hl, c=c: wts.v(wbuf[group % 2], hl, c)) for c in range(NC)]
                              ).then_inc(a.v_mm, 1)

            def pv(where):
                group, pair, h = where
                if h == 0:
                    pe.wait_ge(a.v_lo, step_of(group, pair) * NT + NT)
                a.times_v(pe, slot_of(where), h * HD, pv_parts, b_o, cols)

            def out(where):
                group, pair, h = where
                a.project_out(pe, slot_of(where), h, step_of(group, pair), wts, wbuf[group % 2], b_y)

            def body(group, pair):
                for h in range(HG):
                    n = slot_of((group, pair, h))
                    pe.wait_ge(lo_done[0], n + 1)
                    pe.wait_ge(lo_done[1], n + 1)
                    for b in range(2):
                        a.scores(pe, n, b, lambda hl: a.kT[:, h % 2, hl, :], s_parts, b_s, h % 2)
                    fetch, last, last2 = (ahead(group, pair, h, 1), back(group, pair, h, 1),
                                          back(group, pair, h, 2))
                    if fetch is not None:
                        qk(fetch)
                    if last is not None:
                        pv(last)
                    if h == 0:
                        v(group, pair, 0)
                        v(group, pair, 1)
                    a.turn_probs(pe, n, h, 0, t_parts, b_t, const.ident)
                    if h == 0:
                        v(group, pair, 2)
                    if last2 is not None:
                        out(last2)
                    if h == 0:
                        v(group, pair, 3)
                    a.turn_probs(pe, n, h, 1, t_parts, b_t, const.ident)

            qk((0, 0, 0))
            for group in range(NG):
                over_pairs(pe, group, body)
            pv((NG - 1, NP - 1, HG - 1))
            out((NG - 1, NP - 1, HG - 2))
            out((NG - 1, NP - 1, HG - 1))

        @block.scalar
        def _(act):
            def qk(where):
                n = slot_of(where)
                for i in range(2):
                    act.wait_ge(mm_done[i], n + 1)
                    ge(act, a.s_mm, n * 2 - 2)
                    act.activation(buf[i][:, where[2] % 2, 0, :], b_qk[i][:, :], ACT.Identity,
                                   bias=bias(i, where)).then_inc(hi_done[i], 1)

            def v(step, t):
                act.wait_ge(a.v_mm, step * NT + (t + 1))
                ge(act, a.pv_mm, step * HG * 2)
                act.activation(a.v[:, 0, t, :], b_qk[t % 2][:, :], ACT.Identity).then_inc(a.v_hi, 1)

            def body(group, pair):
                step = step_of(group, pair)
                for h in range(HG):
                    n = slot_of((group, pair, h))
                    for b in range(2):
                        a.exponentials(act, n, h, b, s_parts, b_s)
                    fetch, last = ahead(group, pair, h, 1), back(group, pair, h, 1)
                    if fetch is not None:
                        qk(fetch)
                    if last is not None:
                        a.out_hi(act, slot_of(last), last[2], b_o, bias(2, last))
                    if h == 0:
                        v(step, 0)
                        v(step, 1)
                    a.probs_hi(act, n, 0, b_t, cols)
                    if h == 0:
                        v(step, 2)
                        v(step, 3)
                    a.probs_hi(act, n, 1, b_t, cols)

            qk((0, 0, 0))
            for group in range(NG):
                over_pairs(act, group, body)
            last = (NG - 1, NP - 1, HG - 1)
            a.out_hi(act, slot_of(last), HG - 1, b_o, bias(2, last))

        @block.vector
        def _(dve):
            def qk(where):
                n = slot_of(where)
                for i in range(2):
                    dve.wait_ge(hi_done[i], n + 1)
                    dst = buf[i][:, where[2] % 2, :, :]
                    dve.scalar_tensor_tensor(out=dst[:, 1, :], in0=b_qk[i][:, :], scalar=bias(i, where),
                                             in1=dst[:, 0, :].bitcast(F32), op0=ALU.add,
                                             op1=ALU.subtract).then_inc(lo_done[i], 1)

            def v(step, t):
                dve.wait_ge(a.v_hi, step * NT + (t + 1))
                dve.tensor_tensor(a.v[:, 1, t, :], b_qk[t % 2][:, :], a.v[:, 0, t, :].bitcast(F32),
                                  ALU.subtract).then_inc(a.v_lo, 1)

            def body(group, pair):
                step = step_of(group, pair)
                for h in range(HG):
                    n = slot_of((group, pair, h))
                    if h == 2 and before(group, pair) is not None:
                        prev = before(group, pair)
                        a.take_sums(dve, step_of(*prev), *prev, yacc, b_y)
                    for b in range(2):
                        a.maxima(dve, n, b, s_parts, b_s)
                    for b in range(2):
                        a.inverses(dve, n, h, b)
                        a.normalize(dve, n, h, b, s_parts)
                    fetch, last = ahead(group, pair, h, 1), back(group, pair, h, 1)
                    if fetch is not None:
                        qk(fetch)
                    if last is not None:
                        a.out_lo(dve, slot_of(last), last[2], b_o, bias(2, last))
                    if h == 0:
                        v(step, 0)
                        v(step, 1)
                    a.probs_lo(dve, n, 0, b_t, cols)
                    if h == 0:
                        v(step, 2)
                        v(step, 3)
                    a.probs_lo(dve, n, 1, b_t, cols)

            qk((0, 0, 0))
            for group in range(NG):
                over_pairs(dve, group, body)
            last = (NG - 1, NP - 1, HG - 1)
            a.out_lo(dve, slot_of(last), HG - 1, b_o, bias(2, last))
            a.take_sums(dve, NG * NP - 1, NG - 1, NP - 1, yacc, b_y)

STAGES = 3


def piece0(ins, group, i):
    wq, wk, wv, wo = (ins[f"L0_attn_W{n}"] for n in "qkvo")
    if i < 2:
        return [(0, PIECE, wq[i * P:(i + 1) * P, group * PIECE:(group + 1) * PIECE])]
    if i == 2:
        return [(at, D, w.rearrange("(c p) n -> p c n", p=P)[:, :, group * HD:(group + 1) * HD])
                for at, w in ((0, wk), (D, wv))]
    h = group * HG + (i - 3) * 2
    return [(0, PIECE, wo[h * HD:(h + 2) * HD, :].rearrange("(h p) n -> p h n", p=P))]


def start(nc, held, ins, persistent, x_all, h_dram, w_dram, bank):
    rb_gu, rb_d, dd, wr, mod, gbo, const = (persistent[k] for k in
                                            ("gu", "down", "small", "routers", "mod", "gbo", "const"))
    with ExitStack() as ctx:
        def sb(n, shape, dt=F32):
            return ctx.enter_context(nc.sbuf_tensor("s_" + n, shape, dt))

        def sem(n):
            held.append(nc.alloc_semaphore("s_" + n))
            return held[-1]

        c_rows = sb("c_rows", [B, 2, D])
        c_silu = sb("c_silu", [B, 2, D])
        c_T = sb("c_T", [P, 2 * NC * B])
        wmod = sb("wmod", [P, NC, 6 * D])
        rows = sb("rows", [3 * HEADS + NC, P])
        r_rows = sb("r_rows", [E, 2, D])
        raw_g = sb("raw_g", [P, NR, D])
        raw_u = sb("raw_u", [P, NR, D])
        raw_d = sb("raw_d", [P, NC, NR * P])
        raw_s = sb("raw_s", [P, 2, NSH, D])
        raw_sd = sb("raw_sd", [P, NC, FS])
        raw_small = sb("raw_small", [P, D])
        raw_up = sb("raw_up", [P, NC, P])
        mask = sb("mask", [P, P])
        sel = sb("sel", [2 * E, NR * P + P])
        mag, sign = sb("mag", [P, 2, NC * B]), sb("sign", [P, 2, NC * B])
        stage = sb("stage", [P, STAGES, PIECE])
        split = sb("split", [P, STAGES, 2, PIECE], F32R)
        hT = sb("hT", [P, 2, NC, TOK], F32R)
        cur = sb("cur", [P, 6 * NC, 2])
        tmp = NormTiles(lambda n, s: sb(n, s))

        s_ident, s_const, s_c, s_rows = sem("ident_loaded"), sem("const_loaded"), sem("c_loaded"), sem("rows_loaded")
        s_mod = [sem(f"wmod{i}_loaded") for i in range(2)]
        s_x, s_gu, s_dn, s_small = sem("x_loaded"), sem("gu_loaded"), sem("down_loaded"), sem("small_loaded")
        s_silu, s_cT, s_cTs = sem("silu"), sem("c_turned"), sem("c_T")
        s_modmm, s_modraw, s_modstep = sem("mod_mm"), sem("mod_raw"), sem("mod_step")
        s_modready = sem("mod_ready")
        s_rowsT, s_bias, s_rhi, s_rlo = sem("rows_turned"), sem("bias"), sem("router_hi"), sem("router_lo")
        s_wT, s_whi, s_wlo = sem("w_turned"), sem("w_hi"), sem("w_lo")
        s_stage = [sem(f"stage{i}_loaded") for i in range(STAGES)]
        s_pout = [sem(f"piece{i}_stored") for i in range(STAGES)]
        s_phi, s_plo = sem("piece_hi"), sem("piece_lo")
        s_cast = sem("consts_cast")
        n_ = NormSems(sem, "n", residual=False)
        s_hout = sem("h_stored")
        PIECES = [(g, i) for g in range(NG) for i in range(5)]
        SOURCES = [2 if i == 2 else 1 for _, i in PIECES]
        block = ctx.enter_context(nc.Block())

        @block.sync
        def _(sp):
            sp.dma_start(const.ident[:, :], ins["k_ident"]).then_inc(s_ident, 16)
            for l in range(2):
                sp.dma_start(c_rows[:, l, :], ins[f"L{l}_c"]).then_inc(s_c, 16)
            sp.dma_start(wmod[:, :, :], ins["L0_wmod"].rearrange("(c p) n -> p c n", p=P)).then_inc(s_mod[0], 16)
            sp.dma_start(x_all[:, :, :], ins["L0_attn_x"].rearrange("b s d -> (b s) d").rearrange(
                "(t p) d -> p t d", p=P)).then_inc(s_x, 16)
            for i, k in enumerate(("bq", "bk", "bv", "bo")):
                k_rows = ins[f"L1_attn_{k}"].rearrange("(h d) -> h d", d=P)
                sp.dma_start(rows[i * HEADS:i * HEADS + k_rows.shape[0], :], k_rows).then_inc(s_rows, 16)
            sp.dma_start(r_rows[:, 0, :], ins["L0_ffn_Wr"]).then_inc(s_rows, 16)
            sp.dma_start(r_rows[:, 1, :], ins["L1_ffn_router_w"]).then_inc(s_rows, 16)
            for dst, key in ((const.cos_q, "k_cos_q"), (const.sin_q, "k_sin_q"), (const.cos_k, "k_cos_k"),
                             (const.sin_k, "k_sin_k"), (const.iota8, "k_iota"), (mask, "k_mask"), (sel, "k_sel")):
                sp.dma_start(dst[:, :], ins[key]).then_inc(s_const, 16)
            stored = 0

            def load_piece(n):
                if n >= STAGES:
                    sp.wait_ge(s_plo, n - STAGES + 1)
                for at, size, src in piece0(ins, *PIECES[n]):
                    dst = stage[:, n % STAGES, at:at + size]
                    if len(src.shape) == 3:
                        dst = dst.rearrange("p (c w) -> p c w", c=src.shape[1])
                    sp.dma_start(dst, src).then_inc(s_stage[n % STAGES], 16)

            def store_piece(n):
                g, i = PIECES[n]
                sp.wait_ge(s_plo, n + 1)
                sp.dma_start(w_dram[g][:, i * 2 * PIECE:(i + 1) * 2 * PIECE],
                             split[:, n % STAGES, :, :].bitcast(F32).rearrange("p a w -> p (a w)")
                             ).then_inc(s_pout[n % STAGES], 16)

            for n in range(STAGES):
                load_piece(n)
            for dst, key in ((raw_g, "L0_ffn_Wg"), (raw_u, "L0_ffn_Wu")):
                sp.dma_start(dst[:, :, :], ins[key].rearrange("e f d -> (e f) d").rearrange(
                    "(j p) d -> p j d", p=P)).then_inc(s_gu, 16)
            for i, key in enumerate(("L0_ffn_Wsg", "L0_ffn_Wsu")):
                full = (NSH - 1) * P
                sp.dma_start(raw_s[:, i, 0:NSH - 1, :], ins[key][0:full, :].rearrange(
                    "(j p) d -> p j d", p=P)).then_inc(s_gu, 16)
                sp.dma_start(raw_s[0:LASTW, i, NSH - 1, :], ins[key][full:FS, :]).then_inc(s_gu, 16)
            for c in range(NC):
                sp.dma_start(raw_d[:, c, :].rearrange("p (e f) -> p e f", e=E),
                             ins["L0_ffn_Wd"][:, c * P:(c + 1) * P, :].rearrange("e d f -> d e f")).then_inc(s_dn, 16)
            sp.dma_start(raw_sd[:, :, :], ins["L0_ffn_Wsd"].rearrange("(c p) f -> p c f", p=P)).then_inc(s_dn, 16)
            sp.dma_start(raw_small[:, :], ins["L1_ffn_down_w"].rearrange("e i h -> (e i) h")).then_inc(s_small, 16)
            for c in range(NC):
                sp.dma_start(raw_up[:, c, :].rearrange("p (e i) -> p e i", e=E),
                             ins["L1_ffn_up_w"][:, c * P:(c + 1) * P, :].rearrange("e h i -> h e i")
                             ).then_inc(s_small, 16)
            sp.wait_ge(s_modmm, 1)
            sp.dma_start(wmod[:, :, :], ins["L1_wmod"].rearrange("(c p) n -> p c n", p=P)).then_inc(s_mod[1], 16)
            for n in range(len(PIECES)):
                store_piece(n)
                if n + STAGES < len(PIECES):
                    load_piece(n + STAGES)
            for i in range(STAGES):
                sp.wait_ge(s_pout[i], 16 * len(PIECES[i::STAGES]))

        @block.tensor
        def _(pe):
            pe.wait_ge(s_ident, 16)
            pe.wait_ge(s_silu, 1)
            for l in range(2):
                for c in range(NC):
                    at = (l * NC + c) * B
                    mm = pe.transpose(bank[0][:, at:at + B], c_silu[:, l, c * P:(c + 1) * P],
                                      const.ident[0:B, 0:B])
            mm.then_inc(s_cT, 1)
            pe.wait_ge(s_rows, 16 * 6)
            mm = pe.transpose(bank[2][:, 0:3 * HEADS + NC], rows[:, :],
                              const.ident[0:3 * HEADS + NC, 0:3 * HEADS + NC])
            for l in range(2):
                for c in range(NC):
                    at = P + (l * NC + c) * E
                    mm = pe.transpose(bank[2][:, at:at + E], r_rows[:, l, c * P:(c + 1) * P],
                                      const.ident[0:E, 0:E])
            mm.then_inc(s_rowsT, 1)
            pe.wait_ge(s_cTs, 1)
            for l in range(2):
                pe.wait_ge(s_mod[l], 16)
                for j in range(6 * NC):
                    at = (l * 6 * NC + j) * B
                    for c in range(NC):
                        mm = pe.matmul(bank[1][:, at:at + B], wmod[:, c, j * P:(j + 1) * P],
                                       c_T[:, (l * NC + c) * B:(l * NC + c + 1) * B],
                                       start=(c == 0), stop=(c == NC - 1))
                mm.then_inc(s_modmm, 1)
            for n in range(NJ + NJ + 1):
                out = bank[3 + n % 2]
                if n >= 2:
                    pe.wait_ge(s_wlo, n - 1)
                if n < NJ:
                    if n == 0:
                        pe.wait_ge(s_gu, 16 * 6)
                    w = width(n)
                    for i, (raw, c) in enumerate((r, c) for r in range(2) for c in range(NC)):
                        if n < NR:
                            src = (raw_g, raw_u)[raw][:, n, c * P:(c + 1) * P]
                        else:
                            src = raw_s[0:w, raw, n - NR, c * P:(c + 1) * P]
                        mm = pe.transpose(out[:, i * P:i * P + w], src, const.ident[0:w, 0:w])
                elif n < 2 * NJ:
                    j = n - NJ
                    if j == 0:
                        pe.wait_ge(s_dn, 16 * 3)
                    w = width(j)
                    for c in range(NC):
                        src = raw_d[:, c, j * P:(j + 1) * P] if j < NR else \
                            raw_sd[:, c, (j - NR) * P:(j - NR) * P + w]
                        mm = pe.transpose(out[0:w, c * P:(c + 1) * P], src, const.ident[:, :])
                else:
                    pe.wait_ge(s_small, 16 * 3)
                    for c in range(NC):
                        pe.transpose(out[:, c * P:(c + 1) * P], raw_small[:, c * P:(c + 1) * P], const.ident[:, :])
                        mm = pe.transpose(out[:, (NC + c) * P:(NC + c + 1) * P], raw_up[:, c, :], const.ident[:, :])
                mm.then_inc(s_wT, 1)
            with pe.Fori(0, NP) as p:
                turn_norm(pe, n_, p, tmp, const.ident, bank[5:7])

        def weight_parts(n):
            src = bank[3 + n % 2]
            if n < NJ:
                w = width(n)
                view = src[:, :].rearrange("p (i w) -> p i w", i=4)[:, :, 0:w]
                return view, [rb_gu[:, n, hl, :, 0:w] for hl in range(2)]
            if n < 2 * NJ:
                j, w = n - NJ, width(n - NJ)
                return src[0:w, 0:D], [rb_d[0:w, hl, j, :] for hl in range(2)]
            return src[:, :], [dd[:, hl, :] for hl in range(2)]

        @block.scalar
        def _(act):
            act.wait_ge(s_c, 32)
            act.activation(c_silu[:, :, :], c_rows[:, :, :], ACT.Silu).then_inc(s_silu, 1)
            act.wait_ge(s_cT, 1)
            act.activation(c_T[:, :], bank[0][:, 0:2 * NC * B], ACT.Identity).then_inc(s_cTs, 1)
            act.wait_ge(s_rowsT, 1)
            act.activation(wr[:, :, 0, :], bank[2][:, P:P + 2 * NC * E].rearrange("p (l w) -> p l w", l=2),
                           ACT.Identity).then_inc(s_rhi, 1)
            for n in range(NJ + NJ + 1):
                act.wait_ge(s_wT, n + 1)
                src, (hi, _) = weight_parts(n)
                act.activation(hi, src, ACT.Identity).then_inc(s_whi, 1)
                if n < len(PIECES):
                    act.wait_ge(s_stage[n % STAGES], sum(SOURCES[n % STAGES:n + 1:STAGES]) * 16)
                    if n >= STAGES:
                        act.wait_ge(s_pout[n % STAGES], 16 * (n // STAGES))
                    act.activation(split[:, n % STAGES, 0, :], stage[:, n % STAGES, :], ACT.Identity).then_inc(s_phi, 1)
            with act.Fori(0, NP) as p:
                modulate(act, n_, p, kinds(cur, SA), kinds(cur, CA), tmp, bank[5:7])
                act.wait_ge(n_.lo, p * 2 + 2)
                act.dma_start(h_dram[p], hT[:, :, :, :].bitcast(F32).rearrange("p a c t -> p (a c t)")
                              ).then_inc(s_hout, 16)
            act.wait_ge(s_hout, 16 * NP)

        @block.vector
        def _(dve):
            dve.wait_ge(s_ident, 16)
            dve.wait_ge(s_const, 16 * 7)
            dve.tensor_copy(const.ident_r[:, :], const.ident[:, :]).then_inc(s_cast, 1)
            dve.tensor_copy(const.mask_r[:, :], mask[:, :]).then_inc(s_cast, 1)
            dve.tensor_copy(const.sel_r[:, :], sel[:, :]).then_inc(s_cast, 1)
            dve.memset(const.minus_half[:, :], -0.5).then_inc(s_cast, 1)
            dve.wait_ge(s_rhi, 1)
            dve.tensor_copy(const.biasT[:, :], bank[2][:, 0:3 * HEADS + NC]).then_inc(s_bias, 1)
            dve.wait_ge(s_bias, 1)
            dve.tensor_scalar(const.biasT[:, 0:HEADS], const.biasT[:, 0:HEADS], SCALE, None,
                              ALU.mult).then_inc(s_bias, 1)
            dve.tensor_tensor(wr[:, :, 1, :], bank[2][:, P:P + 2 * NC * E].rearrange("p (l w) -> p l w", l=2),
                              wr[:, :, 0, :].bitcast(F32), ALU.subtract).then_inc(s_rlo, 1)
            dve.wait_ge(s_modmm, 2)
            dve.tensor_copy(mod[:, :, :, :].rearrange("p l k b -> p (l k b)"),
                            bank[1][:, 0:2 * 6 * NC * B]).then_inc(s_modraw, 1)
            dve.wait_ge(s_modraw, 1)
            step = 0
            for c_kind, g_kind in ((CA, GA), (CB, GB)):
                scale = mod[:, :, c_kind * NC:(c_kind + 1) * NC, :]
                gate = mod[:, :, g_kind * NC:(g_kind + 1) * NC, :]
                m = mag[:, :, :].rearrange("p l (c b) -> p l c b", c=NC)
                sg = sign[:, :, :].rearrange("p l (c b) -> p l c b", c=NC)
                for l in range(2):
                    for ins_ in (
                            lambda: dve.tensor_scalar(scale[:, l], scale[:, l], 1.0, None, ALU.add),
                            lambda: dve.scalar_tensor_tensor(out=m[:, l], in0=gate[:, l], scalar=-1.0,
                                                             in1=gate[:, l], op0=ALU.mult, op1=ALU.max),
                            lambda: dve.tensor_scalar(sg[:, l], gate[:, l], 0.0, 2.0, ALU.is_ge, ALU.mult),
                            lambda: dve.tensor_scalar(sg[:, l], sg[:, l], -1.0, None, ALU.add),
                            lambda: dve.scalar_tensor_tensor(out=gate[:, l], in0=m[:, l], scalar=0.25,
                                                             in1=sg[:, l], op0=ALU.max, op1=ALU.mult)):
                        step += 1
                        ins_().then_inc(s_modstep, 1)
                        dve.wait_ge(s_modstep, step)
            for c in range(NC):
                ga1 = mod[:, 1, GA * NC + c, :]
                ins_ = dve.tensor_scalar(gbo[:, c, :], ga1, const.biasT[:, 3 * HEADS + c:3 * HEADS + c + 1],
                                         None, ALU.mult)
            ins_.then_inc(s_modready, 1)
            for n in range(NJ + NJ + 1):
                dve.wait_ge(s_whi, n + 1)
                src, (hi, lo) = weight_parts(n)
                dve.tensor_tensor(lo, src, hi.bitcast(F32), ALU.subtract).then_inc(s_wlo, 1)
            dve.wait_ge(s_x, 16)
            with dve.Fori(0, NP) as p:
                copy_mod(dve, n_, p, mod[:, 0], cur)
                x = x_all[:, bass.ds(p * NT, NT), :]
                norm_dve(dve, n_, p, x, tmp)
                ge(dve, s_hout, p * 16)
                split_h(dve, n_, p, tmp, hT)

        @block.gpsimd
        def _(pool):
            for n in range(len(PIECES)):
                pool.wait_ge(s_phi, n + 1)
                pool.tensor_tensor(split[:, n % STAGES, 1, :], stage[:, n % STAGES, :],
                                   split[:, n % STAGES, 0, :].bitcast(F32), ALU.subtract).then_inc(s_plo, 1)
            pool.wait_ge(s_cast, 4)
            with pool.Fori(0, NP) as p:
                norm_pool(pool, n_, p, tmp, const.minus_half)


def piece1(ins, group, i):
    if i < 6:
        w, c = "qkv"[i // 2], i % 2
        codes, scales = ins[f"L1_attn_w{w}_codes"], ins[f"L1_attn_w{w}_scales"]
        cols = bass.ds(group * PIECE, PIECE)
        return [(0, PIECE, codes[c * P:(c + 1) * P, cols])], [(0, PIECE, scales[c * 4:(c + 1) * 4, cols])]
    codes, scales = ins["L1_attn_wo_codes"], ins["L1_attn_wo_scales"]
    first = group * HG + (i - 6) * 2
    return ([(k * D, D, codes[bass.ds((first + k) * HD, HD), :]) for k in range(2)],
            [(k * D, D, scales[bass.ds((first + k) * 4, 4), :]) for k in range(2)])


def feed_forward0(nc, held, ins, persistent, yacc, h_dram, w_dram, x_dram, bank):
    gu, down, wr, mod, const = (persistent[k] for k in ("gu", "down", "routers", "mod", "const"))
    PIECES = 8
    with ExitStack() as ctx:
        def sb(n, shape, dt=F32):
            return ctx.enter_context(nc.sbuf_tensor("f0_" + n, shape, dt))

        def sem(n):
            held.append(nc.alloc_semaphore("f0_" + n))
            return held[-1]

        x = sb("x", [P, NT, D])
        ys = sb("ys", [P, NC, TOK])
        hT = sb("hT", [P, 2, NC, TOK], F32R)
        cur = sb("cur", [P, 2, 6 * NC, 2])
        tmp = NormTiles(lambda n, s: sb(n, s))
        r = RouterTiles(sb)
        silu = sb("silu", [P, 2, TOK])
        prod = sb("prod", [P, 2, TOK])
        act_hl = sb("act_hl", [P, 2, 2, TOK], F32R)
        codes = sb("codes", [P, 2, PIECE])
        scales = sb("scales", [P, 2, PIECE])
        split = sb("split", [P, 2, 2, PIECE], F32R)
        b_g, b_u, b_w, b_r, b_y = bank[0:2], bank[2:4], bank[4], bank[5], bank[6:8]

        n1, n2 = NormSems(sem, "n1"), NormSems(sem, "n2")
        rs = RouterSems(sem, "r")
        x_in, x_out, h_out = sem("x_loaded"), sem("x_stored"), sem("h_stored")
        gu_mm, w_mm, y_mm = sem("gu_mm"), sem("w_mm"), sem("y_mm")
        silu_done, mul_done, gated = sem("silu"), sem("mul"), sem("gated")
        a_hi, a_lo = sem("a_hi"), sem("a_lo")
        p_w, p_hi, p_lo = (sem("piece_" + k) for k in ("w", "hi", "lo"))
        p_in = [sem(f"piece{i}_loaded") for i in range(2)]
        p_out = [sem(f"piece{i}_stored") for i in range(2)]
        p_passed = sem("piece_passed")
        LOADS = 3 * 5 + 10
        block = ctx.enter_context(nc.Block())

        def store(sp, p, i):
            sp.wait_ge(p_lo, p * PIECES + i + 1)
            sp.dma_start(w_dram[p][:, i * 2 * PIECE:(i + 1) * 2 * PIECE],
                         split[:, i % 2, :, :].bitcast(F32).rearrange("p a w -> p (a w)")).then_inc(p_out[i % 2], 16)

        @block.sync
        def _(sp):
            with sp.Fori(0, NP) as p:
                ge(sp, x_out, p * 16)
                sp.dma_start(x[:, :, :], ins["L0_attn_x"].rearrange("b s d -> (b s) d").rearrange(
                    "(g t p) d -> g p t d", p=P, t=NT)[p]).then_inc(x_in, 16)
                for i in range(PIECES):
                    if i >= 2:
                        sp.wait_ge(p_lo, p * PIECES + i - 1)
                    code_src, scale_src = piece1(ins, p, i)
                    for at, size, src in code_src:
                        sp.dma_start(codes[:, i % 2, at:at + size], src).then_inc(p_in[i % 2], 16)
                    for at, size, src in scale_src:
                        for k in range(4):
                            sp.dma_start(scales[32 * k:32 * k + 32, i % 2, at:at + size],
                                         src[k:k + 1, :].broadcast_to([32, size])).then_inc(p_in[i % 2], 16)
                    if i:
                        store(sp, p, i - 1)
                store(sp, p, PIECES - 1)
                sp.wait_ge(n2.lo, p * 2 + 2)
                sp.dma_start(h_dram[p], hT[:, :, :, :].bitcast(F32).rearrange("p a c t -> p (a c t)")
                             ).then_inc(h_out, 16)
                sp.dma_start(x_dram[p], x[:, :, :].rearrange("p t d -> p (t d)")).then_inc(x_out, 16)
            sp.wait_ge(h_out, 16 * NP)
            sp.wait_ge(x_out, 16 * NP)
            for i in range(2):
                sp.wait_ge(p_out[i], 16 * NP * PIECES // 2)

        @block.gpsimd
        def _(pool):
            with pool.Fori(0, NP) as p:
                norm_pool(pool, n1, p, tmp, const.minus_half)
                loads = [0, 0]
                for i in range(PIECES):
                    loads[i % 2] += 5 if i < 6 else 10
                    hold(pool, p_in[i % 2], p * (LOADS * 16) + loads[i % 2] * 16, p_passed)
                    w, s_ = codes[:, i % 2, :], scales[:, i % 2, :]
                    if i < 2:
                        pool.tensor_scalar(s_, s_, SCALE, 1.0, ALU.mult, ALU.mult).then_inc(p_hi, 1)
                        pool.wait_ge(p_hi, p * (PIECES + 2) + 2 * i + 1)
                    pool.wait_ge(p_out[i % 2], p * (PIECES // 2 * 16) + i // 2 * 16)
                    pool.tensor_tensor(split[:, i % 2, 0, :], w, s_, ALU.mult).then_inc(p_hi, 1)
                    pool.wait_ge(p_hi, p * (PIECES + 2) + (2 * i + 2 if i < 2 else i + 3))
                    pool.tensor_tensor(w, w, s_, ALU.mult).then_inc(p_w, 1)
                    pool.wait_ge(p_w, p * PIECES + i + 1)
                    pool.tensor_tensor(split[:, i % 2, 1, :], w, split[:, i % 2, 0, :].bitcast(F32),
                                       ALU.subtract).then_inc(p_lo, 1)
                norm_pool(pool, n2, p, tmp, const.minus_half)

        @block.tensor
        def _(pe):
            with pe.Fori(0, NP) as p:
                turn_branch(pe, n1, p, ys, const.ident, b_g)
                turn_norm(pe, n1, p, tmp, const.ident, b_u)
                pe.wait_ge(n1.lo, p * 2 + 2)
                router_pe(pe, rs, p, hT, wr[:, 0], b_r)
                for j in range(NJ + 1):
                    if j < NJ:
                        w = width(j)
                        if j >= 2:
                            pe.wait_ge(mul_done, p * NJ + j - 1)
                        for i, bk in ((0, b_g[j % 2]), (2, b_u[j % 2])):
                            mm = split_matmuls(pe, bk[0:w, :], [
                                (lambda hl, c=c, i=i: gu[:, j, hl, i + c, 0:w], lambda hl, c=c: hT[:, hl, c, :])
                                for c in range(NC)])
                        mm.then_inc(gu_mm, 1)
                        if j == 0:
                            router_turn(pe, rs, p, r, const.ident, b_r)
                        if j < NR:
                            if j == 0:
                                pe.wait_ge(rs.wT, p + 1)
                            else:
                                pe.wait_ge(gated, p * NR + j)
                            pe.matmul(b_w[:, :], const.sel_r[:, j * P:(j + 1) * P], r.wT[:, :],
                                      start=True, stop=True).then_inc(w_mm, 1)
                    if j:
                        w = width(j - 1)
                        pe.wait_ge(a_lo, p * NJ + j)
                        for c in range(NC):
                            for i, (a, m) in enumerate(PASSES):
                                mm = pe.matmul(b_y[c][:, :], down[0:w, a, j - 1, c * P:(c + 1) * P],
                                               act_hl[0:w, (j - 1) % 2, m, :], start=(j == 1 and i == 0),
                                               stop=(j == NJ and i == len(PASSES) - 1))
                        mm.then_inc(y_mm, 1)
                turn_branch(pe, n2, p, ys, const.ident, b_g)
                turn_norm(pe, n2, p, tmp, const.ident, b_u)

        @block.scalar
        def _(act):
            with act.Fori(0, NP) as p:
                act.wait_ge(n1.mod, p + 1)
                scale_branch(act, n1, p, lambda c, b: yacc[:, c, bass.ds(p * TOK + b * S, S)],
                             kinds(cur[:, 0], GA), None, ys)
                modulate(act, n1, p, kinds(cur[:, 0], SB), kinds(cur[:, 0], CB), tmp, b_u)
                router_exp(act, rs, p, r)
                router_copy(act, rs, p, r, b_r)
                for j in range(NJ + 1):
                    if j < NJ:
                        w = width(j)
                        act.wait_ge(gu_mm, p * NJ + j + 1)
                        act.activation(silu[0:w, j % 2, :], b_g[j % 2][0:w, :], ACT.Silu).then_inc(silu_done, 1)
                    if j:
                        w = width(j - 1)
                        act.wait_ge(mul_done, p * NJ + j)
                        if j - 1 < NR:
                            act.wait_ge(gated, p * NR + j)
                        if j >= 3:
                            act.wait_ge(y_mm, p * NJ + j - 2)
                        act.activation(act_hl[0:w, (j - 1) % 2, 0, :], prod[0:w, (j - 1) % 2, :],
                                       ACT.Identity).then_inc(a_hi, 1)
                act.wait_ge(y_mm, p * NJ + NJ)
                scale_branch(act, n2, p, lambda c, b: b_y[c][:, b * S:(b + 1) * S], kinds(cur[:, 0], GB), None, ys)
                modulate(act, n2, p, kinds(cur[:, 1], SA), kinds(cur[:, 1], CA), tmp, b_u)

        @block.vector
        def _(dve):
            with dve.Fori(0, NP) as p:
                copy_mod(dve, n1, p, mod[:, 0], cur[:, 0])
                copy_mod(dve, n2, p, mod[:, 1], cur[:, 1])
                dve.wait_ge(x_in, p * 16 + 16)
                add_branch(dve, n1, p, x, b_g)
                dve.wait_ge(n1.x_new, p * 2 + 2)
                norm_dve(dve, n1, p, x, tmp)
                dve.wait_ge(h_out, p * 16)
                split_h(dve, n1, p, tmp, hT)
                router_dve(dve, rs, p, r, const.iota8, b_r)
                for j in range(NJ):
                    w = width(j)
                    pr = prod[0:w, j % 2, :]
                    dve.wait_ge(silu_done, p * NJ + j + 1)
                    if j >= 2:
                        dve.wait_ge(a_hi, p * NJ + j - 1)
                    dve.tensor_tensor(pr, b_u[j % 2][0:w, :], silu[0:w, j % 2, :], ALU.mult).then_inc(mul_done, 1)
                    if j < NR:
                        dve.wait_ge(mul_done, p * NJ + j + 1)
                        dve.wait_ge(w_mm, p * NR + j + 1)
                        dve.tensor_tensor(pr, b_w[0:w, :], pr, ALU.mult).then_inc(gated, 1)
                    dve.wait_ge(a_hi, p * NJ + j + 1)
                    dve.tensor_tensor(act_hl[0:w, j % 2, 1, :], pr, act_hl[0:w, j % 2, 0, :].bitcast(F32),
                                      ALU.subtract).then_inc(a_lo, 1)
                add_branch(dve, n2, p, x, b_g)
                dve.wait_ge(n2.x_new, p * 2 + 2)
                norm_dve(dve, n2, p, x, tmp)
                split_h(dve, n2, p, tmp, hT)


def feed_forward1(nc, held, persistent, yacc, x_dram, out, bank):
    small, wr, mod, gbo, const = (persistent[k] for k in ("small", "routers", "mod", "gbo", "const"))
    with ExitStack() as ctx:
        def sb(n, shape, dt=F32):
            return ctx.enter_context(nc.sbuf_tensor("f1_" + n, shape, dt))

        def sem(n):
            held.append(nc.alloc_semaphore("f1_" + n))
            return held[-1]

        x = sb("x", [P, NT, D])
        ys = sb("ys", [P, NC, TOK])
        hT = sb("hT", [P, 2, NC, TOK], F32R)
        cur = sb("cur", [P, 6 * NC, 2])
        bo = sb("bo", [P, NC, 2])
        tmp = NormTiles(lambda n, s: sb(n, s))
        r = RouterTiles(sb)
        silu = sb("silu", [P, TOK])
        act_hl = sb("act_hl", [P, 2, TOK], F32R)
        b_h, b_w, b_r, b_y = bank[4], bank[1], bank[5], bank[6:8]
        n1, n2 = NormSems(sem, "n1"), NormSems(sem, "n2", norm=False)
        rs = RouterSems(sem, "r")
        x_in, x_out = sem("x_loaded"), sem("x_stored")
        d_mm, w_mm, y_mm = sem("down_mm"), sem("w_mm"), sem("y_mm")
        silu_done, gated, a_hi, a_lo = sem("silu"), sem("gated"), sem("a_hi"), sem("a_lo")
        bo_done = sem("bo")
        block = ctx.enter_context(nc.Block())

        @block.sync
        def _(sp):
            with sp.Fori(0, NP) as p:
                ge(sp, x_out, p * 16)
                sp.dma_start(x[:, :, :].rearrange("p t d -> p (t d)"), x_dram[p]).then_inc(x_in, 16)
                sp.wait_ge(n2.x_new, p * 2 + 2)
                sp.dma_start(out.rearrange("b s d -> (b s) d").rearrange("(g t p) d -> g p t d", p=P, t=NT)[p],
                             x[:, :, :]).then_inc(x_out, 16)
            sp.wait_ge(x_out, 16 * NP)

        @block.gpsimd
        def _(pool):
            with pool.Fori(0, NP) as p:
                norm_pool(pool, n1, p, tmp, const.minus_half)

        @block.tensor
        def _(pe):
            with pe.Fori(0, NP) as p:
                turn_branch(pe, n1, p, ys, const.ident, bank[0:2])
                turn_norm(pe, n1, p, tmp, const.ident, bank[2:4])
                pe.wait_ge(n1.lo, p * 2 + 2)
                router_pe(pe, rs, p, hT, wr[:, 1], b_r)
                split_matmuls(pe, b_h[:, :], [(lambda hl, c=c: small[:, hl, c * P:(c + 1) * P],
                                               lambda hl, c=c: hT[:, hl, c, :]) for c in range(NC)]
                              ).then_inc(d_mm, 1)
                router_turn(pe, rs, p, r, const.ident, b_r)
                pe.wait_ge(rs.wT, p + 1)
                pe.matmul(b_w[:, :], const.sel_r[:, NR * P:(NR + 1) * P], r.wT[:, :],
                          start=True, stop=True).then_inc(w_mm, 1)
                pe.wait_ge(a_lo, p + 1)
                for c in range(NC):
                    mm = split_matmuls(pe, b_y[c][:, :], [(lambda hl: small[:, hl, (NC + c) * P:(NC + c + 1) * P],
                                                           lambda hl: act_hl[:, hl, :])])
                mm.then_inc(y_mm, 1)
                turn_branch(pe, n2, p, ys, const.ident, bank[0:2])

        @block.scalar
        def _(act):
            with act.Fori(0, NP) as p:
                act.wait_ge(n1.mod, p + 1)
                act.wait_ge(bo_done, p + 1)
                scale_branch(act, n1, p, lambda c, b: yacc[:, c, bass.ds(p * TOK + b * S, S)],
                             kinds(cur, GA), bo, ys)
                modulate(act, n1, p, kinds(cur, SB), kinds(cur, CB), tmp, bank[2:4])
                router_exp(act, rs, p, r)
                router_copy(act, rs, p, r, b_r)
                act.wait_ge(d_mm, p + 1)
                act.activation(silu[:, :], b_h[:, :], ACT.Silu).then_inc(silu_done, 1)
                act.wait_ge(gated, p + 1)
                act.activation(act_hl[:, 0, :], silu[:, :], ACT.Identity).then_inc(a_hi, 1)
                act.wait_ge(y_mm, p + 1)
                scale_branch(act, n2, p, lambda c, b: b_y[c][:, b * S:(b + 1) * S], kinds(cur, GB), None, ys)

        @block.vector
        def _(dve):
            with dve.Fori(0, NP) as p:
                copy_mod(dve, n1, p, mod[:, 1], cur)
                dve.tensor_copy(bo[:, :, :], gbo[:, :, bass.ds(p * 2, 2)]).then_inc(bo_done, 1)
                dve.wait_ge(x_in, p * 16 + 16)
                add_branch(dve, n1, p, x, bank[0:2])
                dve.wait_ge(n1.x_new, p * 2 + 2)
                norm_dve(dve, n1, p, x, tmp)
                split_h(dve, n1, p, tmp, hT)
                router_dve(dve, rs, p, r, const.iota8, b_r)
                dve.wait_ge(silu_done, p + 1)
                dve.wait_ge(w_mm, p + 1)
                dve.tensor_tensor(silu[:, :], b_w[:, :], silu[:, :], ALU.mult).then_inc(gated, 1)
                dve.wait_ge(a_hi, p + 1)
                dve.tensor_tensor(act_hl[:, 1, :], silu[:, :], act_hl[:, 0, :].bitcast(F32),
                                  ALU.subtract).then_inc(a_lo, 1)
                add_branch(dve, n2, p, x, bank[0:2])


class Constants:
    def __init__(self, sb):
        self.ident = sb("ident", [P, P])
        self.ident_r = sb("ident_r", [P, P], F32R)
        self.mask_r = sb("mask_r", [P, P], F32R)
        self.sel_r = sb("sel_r", [2 * E, (NR + 1) * P], F32R)
        self.cos_q, self.sin_q = sb("cos_q", [P, S]), sb("sin_q", [P, S])
        self.cos_k, self.sin_k = sb("cos_k", [P, S]), sb("sin_k", [P, S])
        self.iota8 = sb("iota8", [P, E])
        self.minus_half = sb("minus_half", [P, NT])
        self.biasT = sb("biasT", [P, 3 * HEADS + NC])


def release(nc, held):
    nc.clear_and_free_semaphores(held)
    nc.all_engine_barrier()


def program(nc, ins, out):
    def dram(name, shape):
        return nc.dram_tensor(name, shape, F32, kind="Internal").ap()

    h0_dram, h1_dram = dram("h0", [NP, P, 2 * NC * TOK]), dram("h1", [NP, P, 2 * NC * TOK])
    w0_dram, w1_dram = dram("w0", [NG, P, 5 * 2 * PIECE]), dram("w1", [NG, P, 8 * 2 * PIECE])
    x_dram = dram("x2", [NP, P, NT * D])
    with ExitStack() as ctx:
        def sb(n, shape, dt=F32):
            return ctx.enter_context(nc.sbuf_tensor(n, shape, dt))

        bank = [ctx.enter_context(nc.psum_tensor(f"bank{i}", [P, 512], F32)) for i in range(8)]
        rb = sb("ff_weights", [P, NJ * 8 * P + 2 * NJ * D], F32R)
        persistent = {
            "gu": rb[:, 0:NJ * 8 * P].rearrange("p (j a i w) -> p j a i w", j=NJ, a=2, i=4),
            "down": rb[:, NJ * 8 * P:NJ * 8 * P + 2 * NJ * D].rearrange("p (a j d) -> p a j d", a=2, j=NJ),
            "small": sb("ff1_weights", [P, 2, 4 * P], F32R),
            "routers": sb("routers", [P, 2, 2, NC * E], F32R),
            "mod": sb("mod", [P, 2, 6 * NC, B]),
            "gbo": sb("gbo", [P, NC, B]),
            "const": Constants(sb),
        }
        yacc = sb("yacc", [P, NC, NP * TOK])
        x_all = yacc[:, :, :].rearrange("p c t -> p (c t)").rearrange("p (t d) -> p t d", d=D)
        routers = persistent["routers"][:, :, :, :].rearrange("p l a (c e) -> p l a c e", c=NC)
        held = []
        start(nc, held, ins, persistent, x_all, h0_dram, w0_dram, bank)
        release(nc, held)
        persistent["routers"] = routers
        ra = sb("attn_weights", [P, 2 * 5 * 2 * PIECE], F32R)

        def pieces(t, at, n):
            return t[:, at:at + n * 2 * PIECE].rearrange("p (n a w) -> p n a w", n=n, a=2)

        const = persistent["const"]
        held = []
        attention0(nc, held, [pieces(ra, 0, 5), pieces(ra, 5 * 2 * PIECE, 5)], h0_dram, w0_dram, yacc, bank, const)
        release(nc, held)
        held = []
        feed_forward0(nc, held, ins, persistent, yacc, h1_dram, w1_dram, x_dram, bank)
        release(nc, held)
        held = []
        attention1(nc, held, [pieces(ra, 0, 8), pieces(rb, 0, 8)], h1_dram, w1_dram, yacc, bank, const)
        release(nc, held)
        held = []
        feed_forward1(nc, held, persistent, yacc, x_dram, out, bank)
        release(nc, held)


_INS = ["L0_attn_x", "L0_attn_Wq", "L0_attn_Wk", "L0_attn_Wv", "L0_attn_Wo", "L0_ffn_Wr", "L0_ffn_Wg",
        "L0_ffn_Wu", "L0_ffn_Wd", "L0_ffn_Wsg", "L0_ffn_Wsu", "L0_ffn_Wsd", "L0_c", "L0_wmod",
        "L1_attn_wq_codes", "L1_attn_wq_scales", "L1_attn_bq", "L1_attn_wk_codes", "L1_attn_wk_scales",
        "L1_attn_bk", "L1_attn_wv_codes", "L1_attn_wv_scales", "L1_attn_bv", "L1_attn_wo_codes",
        "L1_attn_wo_scales", "L1_attn_bo", "L1_ffn_router_w", "L1_ffn_down_w", "L1_ffn_up_w", "L1_c",
        "L1_wmod"]


def tables():
    import numpy as np
    f = np.float32
    half = HD // 2
    inv_freq = (f(1.0) / f(10000.0) ** (np.arange(0, HD, 2, dtype=f) / f(HD))).astype(f)
    angle = (inv_freq[:, None] * np.arange(S, dtype=f)[None, :]).astype(f)
    cos, sin = np.cos(angle).astype(f), np.sin(angle).astype(f)
    cos, sin = np.concatenate([cos, cos]), np.concatenate([-sin, sin])
    assert cos.shape == (2 * half, S)
    sel = np.zeros((2 * E, (NR + 1) * P), f)
    for j in range(NR * P):
        sel[[j // F0, E + j // F0], j] = 1
    for j in range(P):
        sel[[j // (P // E), E + j // (P // E)], NR * P + j] = 1
    mask = np.where(np.arange(P)[None, :] > np.arange(P)[:, None], f(MASKED), f(0)).astype(f)
    return {"k_ident": np.eye(P, dtype=f), "k_mask": mask, "k_sel": sel,
            "k_cos_q": (cos * f(SCALE)).astype(f), "k_sin_q": (sin * f(SCALE)).astype(f),
            "k_cos_k": cos, "k_sin_k": sin,
            "k_iota": np.tile(np.arange(E, dtype=f), (P, 1))}


def kernel(**inputs):
    import numpy as np
    import concourse.bacc as bacc
    from concourse.bass_utils import run_bass_kernel_spmd as run

    nc = bacc.Bacc("TRN2", target_bir_lowering=False, num_devices=1, dynamic_dma_scratch_size=1024)
    given = {name: np.ascontiguousarray(inputs[name]) for name in _INS}
    given.update(tables())
    arrays, ins = {}, {}
    for name, a in given.items():
        arrays[f"in_{name}"] = a
        ins[name] = nc.dram_tensor(f"in_{name}", a.shape, mybir.dt.from_np(a.dtype), kind="ExternalInput").ap()
    out = nc.dram_tensor("out_0", (B, S, D), F32, kind="ExternalOutput").ap()
    program(nc, ins, out)
    r = run(nc, [arrays], core_ids=[0])
    return r.results[0]["out_0"]
```

```python
from contextlib import ExitStack

import concourse.bass as bass
from concourse import mybir
from concourse.alu_op_type import AluOpType as ALU

F32 = mybir.dt.float32
F32R = mybir.dt.float32r
U32 = mybir.dt.uint32
ACT = mybir.ActivationFunctionType
AX = mybir.AxisListType

P = 128
B, S, D = 8, 256, 256
TOK = 2 * S
NP = B // 2
NT = TOK // P
NC = D // P
HEADS, HD = 16, 128
HG = 4
NG = HEADS // HG
E = 8
F0, FS = 176, 352
NR = E * F0 // P
NSH = -(-FS // P)
NJ = NR + NSH
CHUNKS = [*range(NR, NJ), *range(NR)]
LASTW = FS - (NSH - 1) * P
EPS = 1e-5
SCALE = float(HD) ** -0.5
MASKED = -1e30
SA, CA, GA, SB, CB, GB = range(6)
PASSES = ((1, 0), (0, 1), (0, 0))
PIECE = 512


def width(j):
    return LASTW if j == NJ - 1 else P


class Weights:

    def __init__(self, shared_kv):
        self.shared_kv = shared_kv
        self.pieces = 5 if shared_kv else 8

    def q(self, w, hl, c, h):
        return w[:, c, hl, h * HD:(h + 1) * HD]

    def k(self, w, hl, c, h):
        if self.shared_kv:
            return w[:, 2, hl, c * HD:(c + 1) * HD]
        return w[:, 2 + c, hl, h * HD:(h + 1) * HD]

    def v(self, w, hl, c):
        if self.shared_kv:
            return w[:, 2, hl, (2 + c) * HD:(3 + c) * HD]
        return w[:, 4 + c, hl, :]

    def o(self, w, hl, h, c):
        piece = (3 if self.shared_kv else 6) + h // 2
        return w[:, piece, hl, (h % 2) * D + c * P:(h % 2) * D + (c + 1) * P]


class NormSems:
    def __init__(self, sem, name, residual=True, norm=True):
        self.residual = residual
        if residual:
            self.scaled = sem(name + "_branch_scaled")
            self.back = sem(name + "_branch_turned")
            self.x_new = sem(name + "_x_new")
        if not norm:
            return
        self.mod = sem(name + "_mod_copied")
        self.stats = sem(name + "_stats")
        self.aggr = sem(name + "_aggr")
        self.var = sem(name + "_var_eps")
        self.rstd = sem(name + "_rstd")
        self.xhat = sem(name + "_xhat")
        self.turned = sem(name + "_xhat_turned")
        self.h = sem(name + "_h")
        self.hi = sem(name + "_h_hi")
        self.lo = sem(name + "_h_lo")
        self.passed = sem(name + "_passed")


def scale_branch(act, s, p, y_of, gate, bias, ys, batches=2):
    for c in range(NC):
        for b in range(batches):
            kw = {} if bias is None else {"bias": bias[:, c, b:b + 1]}
            act.activation(ys[:, c, b * S:(b + 1) * S], y_of(c, b), ACT.Identity,
                           scale=gate[:, c, b:b + 1], **kw).then_inc(s.scaled, 1)


def turn_half(pe, s, half, ys, ident, bank):
    for t in (2 * half, 2 * half + 1):
        for c in range(NC):
            mm = pe.transpose(bank[:, (t % 2) * D + c * P:(t % 2) * D + (c + 1) * P],
                              ys[:, c, t * P:(t + 1) * P], ident[:, :])
    mm.then_inc(s.back, 1)


def turn_branch(pe, s, p, ys, ident, banks):
    pe.wait_ge(s.scaled, p * 4 + 4)
    for half in range(2):
        turn_half(pe, s, half, ys, ident, banks[half])


def add_half(dve, s, p, half, x, bank):
    dve.wait_ge(s.back, p * 2 + (half + 1))
    xs = x[:, 2 * half:2 * half + 2, :].rearrange("p t d -> p (t d)")
    dve.tensor_tensor(xs, xs, bank[:, :], ALU.add).then_inc(s.x_new, 1)


def add_branch(dve, s, p, x, banks):
    for half in range(2):
        add_half(dve, s, p, half, x, banks[half])


def tile_stats(dve, s, p, half, x, tmp):
    if s.residual:
        hold(dve, s.x_new, p * 2 + (half + 1), s.passed)
    for t in (2 * half, 2 * half + 1):
        dve.bn_stats(tmp.stats[:, t, :], x[:, t, :]).then_inc(s.stats, 1)


def mean_and_var(dve, s, p, tmp):
    hold(dve, s.stats, p * 4 + 4, s.passed)
    for t in range(NT):
        dve.bn_aggr(tmp.mv[:, t, :], tmp.stats[:, t, :]).then_inc(s.aggr, 1)
    dve.wait_ge(s.aggr, p * 4 + 4)
    dve.tensor_scalar(tmp.var[:, :], tmp.mv[:, :, 1], EPS, None, ALU.add).then_inc(s.var, 1)


def norm_stats(dve, s, p, x, tmp):
    for half in range(2):
        tile_stats(dve, s, p, half, x, tmp)
    mean_and_var(dve, s, p, tmp)


def norm_pool(pool, s, p, tmp, minus_half):
    pool.wait_ge(s.var, p + 1)
    pool.tensor_tensor(tmp.rstd[:, :], tmp.var[:, :], minus_half[:, :], ALU.pow).then_inc(s.rstd, 1)


def norm_scale(dve, s, p, x, tmp):
    dve.wait_ge(s.rstd, p + 1)
    for t in range(NT):
        dve.tensor_scalar(tmp.xhat[:, t, :], x[:, t, :], tmp.mv[:, t, 0:1], tmp.rstd[:, t:t + 1],
                          ALU.subtract, ALU.mult).then_inc(s.xhat, 1)


def norm_dve(dve, s, p, x, tmp):
    norm_stats(dve, s, p, x, tmp)
    norm_scale(dve, s, p, x, tmp)


def turn_chunk(pe, s, c, tmp, ident, bank):
    for t in range(NT):
        mm = pe.transpose(bank[:, t * P:(t + 1) * P], tmp.xhat[:, t, c * P:(c + 1) * P], ident[:, :])
    mm.then_inc(s.turned, 1)


def turn_norm(pe, s, p, tmp, ident, banks):
    pe.wait_ge(s.xhat, p * 4 + 4)
    for c in range(NC):
        turn_chunk(pe, s, c, tmp, ident, banks[c])


def modulate_chunk(act, s, p, c, shift, scale1, tmp, bank):
    act.wait_ge(s.turned, p * 2 + (c + 1))
    for b in range(2):
        act.activation(tmp.h[:, c, b * S:(b + 1) * S], bank[:, b * S:(b + 1) * S],
                       ACT.Identity, bias=shift[:, c, b:b + 1],
                       scale=scale1[:, c, b:b + 1]).then_inc(s.h, 1)


def modulate(act, s, p, shift, scale1, tmp, banks):
    for c in range(NC):
        modulate_chunk(act, s, p, c, shift, scale1, tmp, banks[c])


def split_chunk(dve, s, p, c, tmp, hT):
    hold(dve, s.h, p * 4 + (2 * c + 2), s.passed)
    dve.tensor_copy(hT[:, 0, c, :], tmp.h[:, c, :]).then_inc(s.hi, 1)
    dve.wait_ge(s.hi, p * 2 + (c + 1))
    dve.tensor_tensor(hT[:, 1, c, :], tmp.h[:, c, :], hT[:, 0, c, :].bitcast(F32),
                      ALU.subtract).then_inc(s.lo, 1)


def split_h(dve, s, p, tmp, hT):
    for c in range(NC):
        split_chunk(dve, s, p, c, tmp, hT)


def copy_mod(dve, s, p, mod, cur):
    dve.tensor_copy(cur[:, :, :], mod[:, :, bass.ds(p * 2, 2)]).then_inc(s.mod, 1)


class NormTiles:
    def __init__(self, sb):
        self.stats = sb("stats", [P, NT, 6])
        self.mv = sb("mv", [P, NT, 2])
        self.var = sb("var", [P, NT])
        self.rstd = sb("rstd", [P, NT])
        self.xhat = sb("xhat", [P, NT, D])
        self.h = sb("h_full", [P, NC, TOK])


def kinds(cur, kind):
    return cur[:, kind * NC:(kind + 1) * NC, :]


class RouterSems:
    def __init__(self, sem, name):
        self.logits = sem(name + "_logits")
        self.copied = sem(name + "_copied")
        self.lturned = sem(name + "_lturned")
        self.step = sem(name + "_step")
        self.shifted = sem(name + "_shifted")
        self.exp = sem(name + "_exp")
        self.weights = sem(name + "_weights")
        self.turned = sem(name + "_turned")
        self.wT = sem(name + "_wT")
        self.passed, self.pe_passed = sem(name + "_passed"), sem(name + "_pe_passed")

    STEPS = 4 + 2 * NT + 6


class RouterTiles:
    def __init__(self, sb):
        self.logits = sb("r_logits", [E, TOK])
        self.nmax = sb("r_nmax", [P, NT])
        self.shifted = sb("r_shifted", [P, NT, E])
        self.exp = sb("r_exp", [P, NT, E])
        self.sum = sb("r_sum", [P, NT])
        self.inv = sb("r_inv", [P, NT])
        self.score = sb("r_score", [P, NT, E])
        self.top = sb("r_top", [P, NT, E])
        self.at = sb("r_at", [P, NT, E], U32)
        self.first = sb("r_first", [P, NT, E])
        self.second = sb("r_second", [P, NT, E])
        self.w = sb("r_w", [P, NT, E])
        self.whl = sb("r_whl", [P, NT, 2 * E], F32R)
        self.wT = sb("r_wT", [2 * E, TOK], F32R)


def router_logits(pe, s, hT, wr, bank):
    split_matmuls(pe, bank[0:E, :], [(lambda hl, c=c: wr[:, hl, c, :], lambda hl, c=c: hT[:, hl, c, :])
                                     for c in range(NC)]).then_inc(s.logits, 1)


def router_logits_turn(pe, s, p, r, ident, bank):
    hold(pe, s.copied, p + 1, s.pe_passed)
    for t in range(NT):
        mm = pe.transpose(bank[:, t * E:(t + 1) * E], r.logits[:, t * P:(t + 1) * P], ident[0:E, 0:E])
    mm.then_inc(s.lturned, 1)


def router_turn(pe, s, p, r, ident, bank):
    pe.wait_ge(s.weights, p + 1)
    for t in range(NT):
        mm = pe.transpose(bank[0:2 * E, t * P:(t + 1) * P], r.whl[:, t, :].bitcast(F32), ident[:, :])
    mm.then_inc(s.turned, 1)


def router_logits_copy(act, s, p, r, bank):
    act.wait_ge(s.logits, p + 1)
    act.activation(r.logits[:, :], bank[0:E, :], ACT.Identity).then_inc(s.copied, 1)


def router_exp(act, s, p, r):
    act.wait_ge(s.shifted, p + 1)
    act.activation(r.exp[:, :, :], r.shifted[:, :, :], ACT.Exp).then_inc(s.exp, 1)


def router_copy(act, s, p, r, bank):
    act.wait_ge(s.turned, p + 1)
    act.activation(r.wT[:, :], bank[0:2 * E, :], ACT.Identity).then_inc(s.wT, 1)


def router_shift(dve, s, p, r, bank):
    logits = bank[:, 0:NT * E].rearrange("p (t e) -> p t e", e=E)
    dve.wait_ge(s.lturned, p + 1)
    dve.tensor_reduce(r.nmax[:, :], logits, AX.X, ALU.max, negate=True).then_inc(s.step, 1)
    dve.wait_ge(s.step, p * RouterSems.STEPS + 1)
    dve.tensor_tensor(r.shifted[:, :, :], logits, r.nmax[:, :, None].broadcast_to([P, NT, E]),
                      ALU.add).then_inc(s.shifted, 1)


def router_weights(dve, s, p, r, iota8):
    n = 1

    def link(*instructions):
        nonlocal n
        for ins in instructions:
            ins.then_inc(s.step, 1)
        n += len(instructions)
        hold(dve, s.step, p * RouterSems.STEPS + n, s.passed)

    def rows(v):
        return v.broadcast_to([P, NT, E])

    dve.wait_ge(s.exp, p + 1)
    link(dve.tensor_reduce(r.sum[:, :], r.exp[:, :, :], AX.X, ALU.add))
    link(dve.reciprocal(r.inv[:, :], r.sum[:, :]))
    link(dve.tensor_tensor(r.score[:, :, :], r.exp[:, :, :], rows(r.inv[:, :, None]), ALU.mult))
    link(*[dve.max(r.top[:, t, :], r.score[:, t, :]) for t in range(NT)])
    link(*[dve.max_index(r.at[:, t, :], r.top[:, t, :], r.score[:, t, :]) for t in range(NT)])
    places = iota8[:, None, :].broadcast_to([P, NT, E])
    link(dve.tensor_tensor(r.first[:, :, :], places, rows(r.at[:, :, 0:1]), ALU.is_equal),
         dve.tensor_tensor(r.second[:, :, :], places, rows(r.at[:, :, 1:2]), ALU.is_equal))
    link(dve.tensor_tensor(r.first[:, :, :], r.first[:, :, :], r.second[:, :, :], ALU.add))
    link(dve.tensor_tensor(r.w[:, :, :], r.score[:, :, :], r.first[:, :, :], ALU.mult))
    link(dve.tensor_copy(r.whl[:, :, 0:E], r.w[:, :, :]))
    link(dve.tensor_tensor(r.whl[:, :, E:2 * E], r.w[:, :, :], r.whl[:, :, 0:E].bitcast(F32), ALU.subtract))
    dve.nop().then_inc(s.weights, 1)
    assert n == RouterSems.STEPS


def ge(eng, sem, value):
    if not isinstance(value, int) or value > 0:
        eng.wait_ge(sem, value)


def hold(eng, sem, value, passed):
    eng.wait_ge(sem, value)
    eng.sem_inc(passed)


def turns(pair):
    return (pair + 1) % 2 if isinstance(pair, int) else pair - 1


def other(pair):
    return pair % 2 if isinstance(pair, int) else pair * -1 + 2


def has(pair, by):
    return not isinstance(pair, int) or 0 <= pair + by < NP


def over_pairs(eng, group, body):
    body(group, 0)
    with eng.Fori(1, NP - 1) as p:
        body(group, p)
    body(group, NP - 1)


def step_of(group, pair):
    return pair + group * NP


def split_matmuls(pe, out, pairs):
    total = len(pairs) * len(PASSES)
    for i, (pair, (a, m)) in enumerate((pair, pm) for pair in pairs for pm in PASSES):
        mm = pe.matmul(out, pair[0](a), pair[1](m), start=(i == 0), stop=(i == total - 1))
    return mm


class Attention:

    def __init__(self, nc, ctx, held, layer, nq, nk, vcols, score_cols):
        def sb(n, shape, dt=F32):
            return ctx.enter_context(nc.sbuf_tensor(f"a{layer}_{n}", shape, dt))

        def sem(n):
            held.append(nc.alloc_semaphore(f"a{layer}_{n}"))
            return held[-1]

        self.qT = sb("qT", [P, nq, 2, TOK], F32R)
        self.kT = sb("kT", [P, nk, 2, TOK], F32R)
        self.v = sb("v", [P, 2, NT, vcols], F32R)
        self.prob = sb("prob", [P, 2, 2, score_cols])
        self.probT = sb("probT", [P, 2, 2, score_cols], F32R)
        self.oT = sb("oT", [P, 2, 2, TOK], F32R)
        self.nmax = sb("nmax", [P, 2, 2])
        self.total = sb("total", [P, 2, 2, 2])
        self.inv = sb("inv", [P, 2, 2, 2])
        self.h_loaded = sem("h_loaded")
        self.w_loaded = sem("w_loaded")
        self.q_mm, self.k_mm, self.v_mm = sem("q_mm"), sem("k_mm"), sem("v_mm")
        self.v_hi, self.v_lo = sem("v_hi"), sem("v_lo")
        self.s_mm, self.t_mm, self.pv_mm = sem("s_mm"), sem("t_mm"), sem("pv_mm")
        self.o_mm = sem("o_mm")
        self.max_done, self.exp_done = sem("max"), sem("exp")
        self.inv_done, self.norm_done = sem("inv"), sem("norm")
        self.t_hi, self.t_lo = sem("t_hi"), sem("t_lo")
        self.o_hi, self.o_lo = sem("o_hi"), sem("o_lo")
        self.y_done = sem("y_done")
        self.sb, self.sem = sb, sem

    def scores(self, pe, n, b, k, parts, banks, par, mask=None):
        ge(pe, self.exp_done, n * 2 + (b - 1))
        for qt, (col, keys) in enumerate(parts):
            out = banks[b][:, col:col + keys]
            for i, (a, m) in enumerate(PASSES):
                mm = pe.matmul(out, self.qT[:, par, a, b * S + qt * P:b * S + (qt + 1) * P],
                               k(m)[:, b * S:b * S + keys], start=(i == 0),
                               stop=(mask is None and i == len(PASSES) - 1))
            if mask is not None:
                mm = pe.matmul(banks[b][:, col + keys - P:col + keys], mask[0][:, :],
                               mask[1][:, :], start=False, stop=True)
        mm.then_inc(self.s_mm, 1)

    def turn_probs(self, pe, n, h, b, parts, bank, ident):
        pe.wait_ge(self.norm_done, n * 2 + (b + 1))
        ge(pe, self.t_lo, n * 2 + b)
        for src, dst in parts:
            mm = pe.transpose(bank[:, dst:dst + P], self.prob[:, h % 2, b, src:src + P], ident[:, :])
        mm.then_inc(self.t_mm, 1)

    def times_v(self, pe, n, vcol, parts, bank, score_cols):
        ge(pe, self.o_lo, n)
        for b in range(2):
            pe.wait_ge(self.t_lo, n * 2 + (b + 1))
            total = len(parts) * len(PASSES)
            for i, ((kt, col, w, q0), (a, m)) in enumerate((x, pm) for x in parts for pm in PASSES):
                mm = pe.matmul(bank[:, b * S + q0:b * S + q0 + w],
                               self.v[:, a, 2 * b + kt, vcol:vcol + HD],
                               self.probT[:, b, m, col:col + w], start=(i == 0), stop=(i == total - 1))
            mm.then_inc(self.pv_mm, 1)

    def project_out(self, pe, n, h, step, wts, w, banks):
        pe.wait_ge(self.o_lo, n + 1)
        if h == 0:
            ge(pe, self.y_done, step * 2)
        for c in range(NC):
            for i, (a, m) in enumerate(PASSES):
                mm = pe.matmul(banks[c][:, :], wts.o(w, a, h, c), self.oT[:, h % 2, m, :],
                               start=(h == 0 and i == 0), stop=(h == HG - 1 and i == len(PASSES) - 1))
        mm.then_inc(self.o_mm, 1)

    def exponentials(self, act, n, h, b, parts, banks):
        act.wait_ge(self.max_done, n * 2 + (b + 1))
        ge(act, self.t_mm, n * 2 + (b + 1 - 2 * 2))
        for qt, (col, keys) in enumerate(parts):
            ins = act.activation(self.prob[:, h % 2, b, col:col + keys], banks[b][:, col:col + keys],
                                 ACT.Exp, bias=self.nmax[:, b, qt:qt + 1],
                                 accum_out=self.total[:, h % 2, b, qt:qt + 1])
        ins.then_inc(self.exp_done, 1)

    def probs_hi(self, act, n, b, bank, cols):
        act.wait_ge(self.t_mm, n * 2 + (b + 1))
        ge(act, self.pv_mm, n * 2 + (b - 1))
        act.activation(self.probT[:, b, 0, :], bank[:, 0:cols], ACT.Identity).then_inc(self.t_hi, 1)

    def out_hi(self, act, n, h, bank, bias):
        act.wait_ge(self.pv_mm, n * 2 + 2)
        ge(act, self.o_mm, n - 1)
        kw = {} if bias is None else {"bias": bias}
        act.activation(self.oT[:, h % 2, 0, :], bank[:, :], ACT.Identity, **kw).then_inc(self.o_hi, 1)

    def maxima(self, dve, n, b, parts, banks):
        dve.wait_ge(self.s_mm, n * 2 + (b + 1))
        if len({keys for _, keys in parts}) == 1:
            cols = sum(keys for _, keys in parts)
            ins = dve.tensor_reduce(self.nmax[:, b, :], banks[b][:, 0:cols].rearrange(
                "p (q k) -> p q k", q=len(parts)), AX.X, ALU.max, negate=True)
        else:
            for qt, (col, keys) in enumerate(parts):
                ins = dve.tensor_reduce(self.nmax[:, b, qt:qt + 1], banks[b][:, col:col + keys],
                                        AX.X, ALU.max, negate=True)
        ins.then_inc(self.max_done, 1)

    def inverses(self, dve, n, h, b):
        dve.wait_ge(self.exp_done, n * 2 + (b + 1))
        dve.reciprocal(self.inv[:, h % 2, b, :],
                       self.total[:, h % 2, b, :]).then_inc(self.inv_done, 1)

    def normalize_dve(self, dve, n, h, b, parts):
        dve.wait_ge(self.inv_done, n * 2 + (b + 1))
        for qt, (col, keys) in enumerate(parts):
            pr = self.prob[:, h % 2, b, col:col + keys]
            ins = dve.tensor_scalar(pr, pr, self.inv[:, h % 2, b, qt:qt + 1], None, ALU.mult)
        ins.then_inc(self.norm_done, 1)

    def normalize_act(self, act, n, h, b, parts):
        act.wait_ge(self.inv_done, n * 2 + (b + 1))
        for qt, (col, keys) in enumerate(parts):
            pr = self.prob[:, h % 2, b, col:col + keys]
            ins = act.activation(pr, pr, ACT.Identity, scale=self.inv[:, h % 2, b, qt:qt + 1])
        ins.then_inc(self.norm_done, 1)

    def probs_lo(self, dve, n, b, bank, cols):
        dve.wait_ge(self.t_hi, n * 2 + (b + 1))
        dve.tensor_tensor(self.probT[:, b, 1, :], bank[:, 0:cols],
                          self.probT[:, b, 0, :].bitcast(F32), ALU.subtract).then_inc(self.t_lo, 1)

    def out_lo(self, dve, n, h, bank, bias):
        dve.wait_ge(self.o_hi, n + 1)
        o = self.oT[:, h % 2, :, :]
        if bias is None:
            ins = dve.tensor_tensor(o[:, 1, :], bank[:, :], o[:, 0, :].bitcast(F32), ALU.subtract)
        else:
            ins = dve.scalar_tensor_tensor(out=o[:, 1, :], in0=bank[:, :], scalar=bias,
                                           in1=o[:, 0, :].bitcast(F32), op0=ALU.add, op1=ALU.subtract)
        ins.then_inc(self.o_lo, 1)

    def take_sums(self, dve, step, group, pair, yacc, banks):
        dve.wait_ge(self.o_mm, step * HG + HG)
        for c in range(NC):
            y = yacc[:, c, bass.ds(pair * TOK, TOK)]
            if group == 0:
                ins = dve.tensor_copy(y, banks[c][:, :])
            else:
                ins = dve.tensor_tensor(y, banks[c][:, :], y, ALU.add)
            ins.then_inc(self.y_done, 1)


def before(group, pair):
    if isinstance(pair, int) and pair == 0:
        return (group - 1, NP - 1) if group else None
    return group, pair - 1


def after(group, pair):
    if isinstance(pair, int) and pair == NP - 1:
        return (group + 1, 0) if group < NG - 1 else None
    return group, pair + 1


def back(group, pair, h, by):
    if h >= by:
        return group, pair, h - by
    prev = before(group, pair)
    return None if prev is None else (*prev, h - by + HG)


def ahead(group, pair, h, by):
    if h + by < HG:
        return group, pair, h + by
    nxt = after(group, pair)
    return None if nxt is None else (*nxt, h + by - HG)


def slot_of(where):
    group, pair, h = where
    return pair * HG + (group * NP * HG + h)


def attention0(nc, held, wbuf, h_dram, w_dram, yacc, bank, const):
    wts = Weights(True)
    s_parts = ((0, P), (P, 2 * P))
    t_parts = ((0, 0), (P, P), (2 * P, 2 * P))
    pv_parts = ((0, 0, 2 * P, 0), (1, 2 * P, P, P))
    cols = 3 * P
    b_q, b_k, b_s, b_t, b_o, b_y = bank[0], bank[1], bank[2:4], bank[4], bank[5], bank[6:8]
    ROT = HG + 1

    def q_turn(where):
        group, pair, h = where
        return pair * ROT + (group * NP * ROT + (h + 1))

    def k_turn(step):
        return step * ROT

    with ExitStack() as ctx:
        a = Attention(nc, ctx, held, 0, HG, 2, HD, cols)
        hT = a.sb("hT", [P, 2, NC, TOK], F32R)
        turned, direct, full = a.sb("turned", [P, TOK]), a.sb("direct", [P, TOK]), a.sb("full", [P, TOK])
        wo_loaded = a.sem("wo_loaded")
        rot_half = a.sem("rot_half")
        rot_direct, rot_sin = a.sem("rot_direct"), a.sem("rot_sin")
        rot_hi, rot_full, rot_lo = a.sem("rot_hi"), a.sem("rot_full"), a.sem("rot_lo")
        first, last_slot = (0, 0, 0), (NG - 1, NP - 1, HG - 1)
        block = ctx.enter_context(nc.Block())


        @block.sync
        def _(sp):
            def weights(group):
                sp.dma_start(wbuf[group % 2].bitcast(F32).rearrange("p n a w -> p (n a w)"),
                             w_dram[group]).then_inc(a.w_loaded, 16)

            def first_weights(lo, hi, sem):
                sp.dma_start(wbuf[0][:, lo:hi].bitcast(F32).rearrange("p n a w -> p (n a w)"),
                             w_dram[0][:, lo * 2 * PIECE:hi * 2 * PIECE]).then_inc(sem, 16)

            first_weights(0, 3, a.w_loaded)
            for it in range(NG * NP):
                ge(sp, a.q_mm, it * HG)
                sp.dma_start(hT[:, :, :, :].bitcast(F32).rearrange("p a c t -> p (a c t)"),
                             h_dram[it % NP]).then_inc(a.h_loaded, 16)
                if it == 0:
                    first_weights(3, 5, wo_loaded)
                group = it // NP + 1
                if it % NP == 1 and group < NG:
                    ge(sp, a.o_mm, (group - 1) * NP * HG)
                    weights(group)

        @block.tensor
        def _(pe):
            def project(bank_, w_of, mm_done):
                split_matmuls(pe, bank_[:, :], [(lambda hl, c=c: w_of(hl, c), lambda hl, c=c: hT[:, hl, c, :])
                                                for c in range(NC)]).then_inc(mm_done, 1)

            def q(where):
                group, pair, h = where
                ge(pe, rot_direct, q_turn(where) - (0 if h else 1))
                project(b_q, lambda hl, c: wts.q(wbuf[group % 2], hl, c, h), a.q_mm)

            def k(group, pair):
                step = step_of(group, pair)
                pe.wait_ge(a.h_loaded, step * 16 + 16)
                if isinstance(pair, int) and pair == 0:
                    pe.wait_ge(a.w_loaded, group * 16 + 16)
                ge(pe, a.v_lo, step)
                project(b_k, lambda hl, c: wts.k(wbuf[group % 2], hl, c, 0), a.k_mm)

            def v(group, pair):
                pe.wait_ge(rot_direct, k_turn(step_of(group, pair)) + 1)
                for t in range(NT):
                    mm = split_matmuls(pe, b_k[:, t * HD:(t + 1) * HD],
                                       [(lambda hl, c=c: hT[:, hl, c, t * P:(t + 1) * P],
                                         lambda hl, c=c: wts.v(wbuf[group % 2], hl, c)) for c in range(NC)])
                mm.then_inc(a.v_mm, 1)

            def scores(where, b, kb):
                group, pair, h = where
                pe.wait_ge(rot_lo, q_turn(where) + 1)
                a.scores(pe, slot_of(where), b, lambda hl: a.kT[:, kb, hl, :], s_parts, b_s, h,
                         (const.ident_r, const.mask_r))

            def pv(where):
                group, pair, h = where
                if h == 0:
                    pe.wait_ge(a.v_lo, step_of(group, pair) + 1)
                a.times_v(pe, slot_of(where), 0, pv_parts, b_o, cols)

            def out(where):
                group, pair, h = where
                if isinstance(pair, int) and where == first:
                    pe.wait_ge(wo_loaded, 16)
                a.project_out(pe, slot_of(where), h, step_of(group, pair), wts, wbuf[group % 2], b_y)

            def body(group, pair):
                nxt = after(group, pair)
                for h in range(HG):
                    n = slot_of((group, pair, h))
                    head, last, last2 = (ahead(group, pair, h, 1), back(group, pair, h, 1),
                                         back(group, pair, h, 2))
                    kb = turns(pair) if h < HG - 1 else other(pair)
                    if h == HG - 1:
                        if last2 is not None:
                            out(last2)
                    elif head is not None:
                        scores(head, 0, kb)
                    if last is not None:
                        pv(last)
                    a.turn_probs(pe, n, h, 0, t_parts, b_t, const.ident)
                    if h == HG - 1 and head is not None:
                        scores(head, 0, kb)
                    if head is not None:
                        scores(head, 1, kb)
                    if h == 0:
                        v(group, pair)
                        q((group, pair, 3))
                    if h < HG - 1 and last2 is not None:
                        out(last2)
                    if h == 1 and nxt is not None:
                        k(*nxt)
                        q((*nxt, 0))
                    a.turn_probs(pe, n, h, 1, t_parts, b_t, const.ident)
                    if h >= 2 and nxt is not None:
                        q((*nxt, h - 1))

            k(0, 0)
            for h in range(3):
                q((0, 0, h))
            for b in range(2):
                scores(first, b, turns(0))
            for group in range(NG):
                over_pairs(pe, group, body)
            pv(last_slot)
            out((NG - 1, NP - 1, HG - 2))
            out(last_slot)

        @block.scalar
        def _(act):
            def halves(turn, b, mm_done, count):
                act.wait_ge(mm_done, count)
                ge(act, rot_hi, turn)
                ge(act, rot_full, turn)
                H = HD // 2
                act.activation(turned[0:H, :], b[H:HD, :], ACT.Identity).then_inc(rot_half, 1)
                act.activation(turned[H:HD, :], b[0:H, :], ACT.Identity).then_inc(rot_half, 1)

            def q(where):
                halves(q_turn(where), b_q, a.q_mm, slot_of(where) + 1)

            def k(group, pair):
                step = step_of(group, pair)
                halves(k_turn(step), b_k, a.k_mm, step + 1)

            def normalize(where, b):
                a.normalize_act(act, slot_of(where), where[2], b, s_parts)

            def body(group, pair):
                step = step_of(group, pair)
                nxt = after(group, pair)
                for h in range(HG):
                    n = slot_of((group, pair, h))
                    head, last = ahead(group, pair, h, 1), back(group, pair, h, 1)
                    if last is not None:
                        a.out_hi(act, slot_of(last), last[2], b_o, None)
                    a.probs_hi(act, n, 0, b_t, cols)
                    if h == 2 and nxt is not None:
                        q((*nxt, 0))
                    if head is not None:
                        for b in range(2):
                            a.exponentials(act, slot_of(head), head[2], b, s_parts, b_s)
                    if h == 0:
                        act.wait_ge(a.v_mm, step + 1)
                        ge(act, a.pv_mm, step * HG * 2)
                        act.activation(a.v[:, 0, :, :].rearrange("p t d -> p (t d)"), b_k[:, :],
                                       ACT.Identity).then_inc(a.v_hi, 1)
                    if h == 1 and nxt is not None:
                        k(*nxt)
                    a.probs_hi(act, n, 1, b_t, cols)
                    if head is not None:
                        normalize(head, 0)
                    if h == 2 and nxt is not None:
                        q((*nxt, 1))
                    if head is not None:
                        normalize(head, 1)
                    if h == 0:
                        q((group, pair, 3))
                    if h == 3 and nxt is not None:
                        q((*nxt, 2))

            k(0, 0)
            for h in range(3):
                q((0, 0, h))
            for b in range(2):
                a.exponentials(act, 0, 0, b, s_parts, b_s)
            for b in range(2):
                normalize(first, b)
            for group in range(NG):
                over_pairs(act, group, body)
            a.out_hi(act, slot_of(last_slot), HG - 1, b_o, None)

        @block.vector
        def _(dve):
            def turn_direct(turn, b, cos):
                dve.wait_ge(rot_half, turn * 2 + 2)
                ge(dve, rot_full, turn)
                for i in range(2):
                    ins = dve.tensor_tensor(direct[:, i * S:(i + 1) * S], b[:, i * S:(i + 1) * S],
                                            cos[:, :], ALU.mult)
                ins.then_inc(rot_direct, 1)

            def turn_hi(turn, dst, reader):
                ge(dve, a.s_mm, reader)
                dve.wait_ge(rot_direct, turn + 1)
                dve.wait_ge(rot_sin, turn + 1)
                dve.tensor_tensor(dst, direct[:, :], turned[:, :], ALU.add).then_inc(rot_hi, 1)

            def q_direct(where):
                turn_direct(q_turn(where), b_q, const.cos_q)

            def q_hi(where):
                turn_hi(q_turn(where), a.qT[:, where[2], 0, :], slot_of(where) * 2 - 2 * (HG - 1))

            def k_direct(group, pair):
                turn_direct(k_turn(step_of(group, pair)), b_k, const.cos_k)

            def k_hi(group, pair, buf):
                step = step_of(group, pair)
                turn_hi(k_turn(step), a.kT[:, buf, 0, :], (step - 1) * HG * 2)

            def body(group, pair):
                step = step_of(group, pair)
                nxt, prev = after(group, pair), before(group, pair)
                for h in range(HG):
                    n = slot_of((group, pair, h))
                    head, last = ahead(group, pair, h, 1), back(group, pair, h, 1)
                    late = h == HG - 1
                    turning = (group, pair, h + 2) if h < 2 else (*nxt, 1) if late and nxt is not None else None
                    if h == 2 and nxt is not None:
                        k_direct(*nxt)
                    if head is not None and not late:
                        a.maxima(dve, slot_of(head), 0, s_parts, b_s)
                    if turning is not None:
                        q_direct(turning)
                    if h == 2 and nxt is not None:
                        k_hi(*nxt, other(pair))
                    if last is not None:
                        a.out_lo(dve, slot_of(last), last[2], b_o, None)
                    a.probs_lo(dve, n, 0, b_t, cols)
                    if h == 2 and nxt is not None:
                        q_direct((*nxt, 0))
                    if late and turning is not None:
                        q_hi(turning)
                    if head is not None:
                        if late:
                            a.maxima(dve, slot_of(head), 0, s_parts, b_s)
                        a.maxima(dve, slot_of(head), 1, s_parts, b_s)
                    if not late and turning is not None:
                        q_hi(turning)
                    if h == 2 and nxt is not None:
                        q_hi((*nxt, 0))
                    if h == 0:
                        dve.wait_ge(a.v_hi, step + 1)
                        dve.tensor_tensor(a.v[:, 1, :, :].rearrange("p t d -> p (t d)"), b_k[:, :],
                                          a.v[:, 0, :, :].bitcast(F32).rearrange("p t d -> p (t d)"),
                                          ALU.subtract).then_inc(a.v_lo, 1)
                    if head is not None:
                        for b in range(2):
                            a.inverses(dve, slot_of(head), head[2], b)
                    if h == 1 and prev is not None:
                        a.take_sums(dve, step_of(*prev), *prev, yacc, b_y)
                    a.probs_lo(dve, n, 1, b_t, cols)

            k_direct(0, 0)
            k_hi(0, 0, turns(0))
            for h in range(2):
                q_direct((0, 0, h))
                q_hi((0, 0, h))
            for b in range(2):
                a.maxima(dve, 0, b, s_parts, b_s)
            for b in range(2):
                a.inverses(dve, 0, 0, b)
            for group in range(NG):
                over_pairs(dve, group, body)
            a.out_lo(dve, slot_of(last_slot), HG - 1, b_o, None)
            a.take_sums(dve, NG * NP - 1, NG - 1, NP - 1, yacc, b_y)

        @block.gpsimd
        def _(pool):
            def rotate(turn, sin, dst):
                pool.wait_ge(rot_half, turn * 2 + 2)
                for i in range(2):
                    half = turned[:, i * S:(i + 1) * S]
                    ins = pool.tensor_tensor(half, half, sin[:, :], ALU.mult)
                ins.then_inc(rot_sin, 1)
                pool.wait_ge(rot_direct, turn + 1)
                pool.wait_ge(rot_sin, turn + 1)
                ge(pool, rot_lo, turn)
                pool.tensor_tensor(full[:, :], direct[:, :], turned[:, :], ALU.add).then_inc(rot_full, 1)
                pool.wait_ge(rot_full, turn + 1)
                pool.wait_ge(rot_hi, turn + 1)
                pool.tensor_tensor(dst[:, 1, :], full[:, :], dst[:, 0, :].bitcast(F32),
                                   ALU.subtract).then_inc(rot_lo, 1)

            def q(where):
                rotate(q_turn(where), const.sin_q, a.qT[:, where[2], :, :])

            def k(group, pair, buf):
                rotate(k_turn(step_of(group, pair)), const.sin_k, a.kT[:, buf, :, :])

            def body(group, pair):
                nxt = after(group, pair)
                q((group, pair, 3))
                if nxt is not None:
                    k(*nxt, other(pair))
                    for h in range(3):
                        q((*nxt, h))

            k(0, 0, turns(0))
            for h in range(3):
                q((0, 0, h))
            for group in range(NG):
                over_pairs(pool, group, body)


def attention1(nc, held, wbuf, hT2, hv, h_dram, w_dram, yacc, bank, const):
    wts = Weights(False)
    s_parts = ((0, 2 * P), (2 * P, 2 * P))
    t_parts = tuple((qt * 2 * P + kt * P, kt * 2 * P + qt * P) for kt in range(2) for qt in range(2))
    pv_parts = ((0, 0, 2 * P, 0), (1, 2 * P, 2 * P, 0))
    cols = 4 * P
    b_qk, b_s, b_t, b_o, b_y = bank[0:2], bank[2:4], bank[4], bank[5], bank[6:8]
    first, final = (0, 0, 0), (NG - 1, NP - 1, HG - 1)
    Q, K = 0, 1

    def bias(kind, where):
        col = kind * HEADS + where[0] * HG + where[2]
        return const.biasT[:, col:col + 1]

    with ExitStack() as ctx:
        a = Attention(nc, ctx, held, 1, 2, 2, HG * HD, cols)
        buf = (a.qT, a.kT)
        mm_done = (a.q_mm, a.k_mm)
        hi_done, lo_done = (a.sem("q_hi"), a.sem("k_hi")), (a.sem("q_lo"), a.sem("k_lo"))
        hv_loaded = a.sem("hv_loaded")
        block = ctx.enter_context(nc.Block())


        @block.sync
        def _(sp):
            def weights(group):
                sp.dma_start(wbuf[group % 2].bitcast(F32).rearrange("p n a w -> p (n a w)"),
                             w_dram[group]).then_inc(a.w_loaded, 16)

            for it in range(1, NG * NP):
                ge(sp, a.h_loaded, (it - 1) * 16)
                ge(sp, a.k_mm, (it - 1) * HG)
                sp.dma_start(hT2[:, turns(it % NP), :, :, :].bitcast(F32).rearrange("p a c t -> p (a c t)"),
                             h_dram[it % NP]).then_inc(a.h_loaded, 16)
                ge(sp, a.v_mm, it * NT)
                if it == 1:
                    sp.wait_ge(a.k_mm, HG)
                sp.dma_start(hv[:, :, :, :].bitcast(F32).rearrange("p a c t -> p (a c t)"),
                             h_dram[it % NP]).then_inc(hv_loaded, 16)
                group = it // NP + 1
                if it % NP == 1 and group < NG:
                    ge(sp, a.o_mm, (group - 1) * NP * HG)
                    weights(group)

        @block.tensor
        def _(pe):
            def qk(where, i, turn):
                group, pair, h = where
                start = group == 0 and isinstance(pair, int) and pair == 0
                h_of = (lambda hl, c: hv[:, hl, c, :]) if start else (lambda hl, c: hT2[:, turn, hl, c, :])
                if h == 0 and i == Q and not start:
                    pe.wait_ge(a.h_loaded, step_of(group, pair) * 16)
                    if isinstance(pair, int) and pair == 0 and group:
                        pe.wait_ge(a.w_loaded, group * 16)
                if h == 3:
                    pe.wait_ge(a.v_lo, step_of(group, pair) * NT + (i + 3))
                else:
                    ge(pe, lo_done[i], slot_of(where))
                w_of = (wts.q, wts.k)[i]
                split_matmuls(pe, b_qk[i][:, :],
                              [(lambda hl, c=c: w_of(wbuf[group % 2], hl, c, h),
                                lambda hl, c=c: h_of(hl, c)) for c in range(NC)]
                              ).then_inc(mm_done[i], 1)

            def v(group, pair, t):
                step = step_of(group, pair)
                if t == 0 and (not isinstance(step, int) or step):
                    pe.wait_ge(hv_loaded, step * 16)
                if t < 2:
                    pe.wait_ge(lo_done[t], step * HG + 3)
                else:
                    pe.wait_ge(a.v_lo, step * NT + (t - 1))
                split_matmuls(pe, b_qk[t % 2][:, :],
                              [(lambda hl, c=c: hv[:, hl, c, t * P:(t + 1) * P],
                                lambda hl, c=c: wts.v(wbuf[group % 2], hl, c)) for c in range(NC)]
                              ).then_inc(a.v_mm, 1)

            def scores(where, b):
                n = slot_of(where)
                h = where[2]
                if b == 0:
                    pe.wait_ge(lo_done[Q], n + 1)
                    pe.wait_ge(lo_done[K], n + 1)
                a.scores(pe, n, b, lambda hl: a.kT[:, h % 2, hl, :], s_parts, b_s, h % 2)

            def pv(where):
                group, pair, h = where
                if h == 0:
                    pe.wait_ge(a.v_lo, step_of(group, pair) * NT + NT)
                a.times_v(pe, slot_of(where), h * HD, pv_parts, b_o, cols)

            def out(where):
                group, pair, h = where
                a.project_out(pe, slot_of(where), h, step_of(group, pair), wts, wbuf[group % 2], b_y)

            def body(group, pair):
                for h in range(HG):
                    n = slot_of((group, pair, h))
                    fetch, head = ahead(group, pair, h, 2), ahead(group, pair, h, 1)
                    last, last2 = back(group, pair, h, 1), back(group, pair, h, 2)
                    turn = turns(pair) if h < 2 else other(pair)
                    if head is not None:
                        scores(head, 0)
                    if fetch is not None:
                        qk(fetch, Q, turn)
                    if last is not None:
                        pv(last)
                    a.turn_probs(pe, n, h, 0, t_parts, b_t, const.ident)
                    if fetch is not None:
                        qk(fetch, K, turn)
                    if head is not None:
                        scores(head, 1)
                    if h == 0:
                        v(group, pair, 0)
                        v(group, pair, 1)
                    if last2 is not None:
                        out(last2)
                    if h == 0:
                        v(group, pair, 2)
                        v(group, pair, 3)
                    a.turn_probs(pe, n, h, 1, t_parts, b_t, const.ident)

            for h in range(2):
                qk((0, 0, h), Q, turns(0))
                qk((0, 0, h), K, turns(0))
            for b in range(2):
                scores(first, b)
            for group in range(NG):
                over_pairs(pe, group, body)
            pv(final)
            out((NG - 1, NP - 1, HG - 2))
            out(final)

        @block.scalar
        def _(act):
            def qk(where, i):
                n = slot_of(where)
                act.wait_ge(mm_done[i], n + 1)
                ge(act, a.s_mm, n * 2 - 2)
                act.activation(buf[i][:, where[2] % 2, 0, :], b_qk[i][:, :], ACT.Identity,
                               bias=bias(i, where)).then_inc(hi_done[i], 1)

            def v(step, t):
                act.wait_ge(a.v_mm, step * NT + (t + 1))
                ge(act, a.pv_mm, step * HG * 2)
                act.activation(a.v[:, 0, t, :], b_qk[t % 2][:, :], ACT.Identity).then_inc(a.v_hi, 1)

            def exponentials(where, b):
                a.exponentials(act, slot_of(where), where[2], b, s_parts, b_s)

            def body(group, pair):
                step = step_of(group, pair)
                for h in range(HG):
                    n = slot_of((group, pair, h))
                    fetch, head, last = ahead(group, pair, h, 2), ahead(group, pair, h, 1), back(group, pair, h, 1)
                    if head is not None:
                        exponentials(head, 0)
                    if fetch is not None:
                        qk(fetch, Q)
                    if last is not None:
                        a.out_hi(act, slot_of(last), last[2], b_o, bias(2, last))
                    a.probs_hi(act, n, 0, b_t, cols)
                    if fetch is not None:
                        qk(fetch, K)
                    if head is not None:
                        exponentials(head, 1)
                    if h == 0:
                        for t in range(NT):
                            v(step, t)
                    a.probs_hi(act, n, 1, b_t, cols)

            for h in range(2):
                qk((0, 0, h), Q)
                qk((0, 0, h), K)
            for b in range(2):
                exponentials(first, b)
            for group in range(NG):
                over_pairs(act, group, body)
            a.out_hi(act, slot_of(final), HG - 1, b_o, bias(2, final))

        @block.vector
        def _(dve):
            def qk(where, i):
                dve.wait_ge(hi_done[i], slot_of(where) + 1)
                dst = buf[i][:, where[2] % 2, :, :]
                dve.scalar_tensor_tensor(out=dst[:, 1, :], in0=b_qk[i][:, :], scalar=bias(i, where),
                                         in1=dst[:, 0, :].bitcast(F32), op0=ALU.add,
                                         op1=ALU.subtract).then_inc(lo_done[i], 1)

            def v(step, t):
                dve.wait_ge(a.v_hi, step * NT + (t + 1))
                dve.tensor_tensor(a.v[:, 1, t, :], b_qk[t % 2][:, :], a.v[:, 0, t, :].bitcast(F32),
                                  ALU.subtract).then_inc(a.v_lo, 1)

            def body(group, pair):
                step = step_of(group, pair)
                for h in range(HG):
                    n = slot_of((group, pair, h))
                    fetch, head, last = ahead(group, pair, h, 2), ahead(group, pair, h, 1), back(group, pair, h, 1)
                    if head is not None:
                        a.maxima(dve, slot_of(head), 0, s_parts, b_s)
                    for b in range(2):
                        a.inverses(dve, n, h, b)
                        a.normalize_dve(dve, n, h, b, s_parts)
                    if fetch is not None:
                        qk(fetch, Q)
                    if last is not None:
                        a.out_lo(dve, slot_of(last), last[2], b_o, bias(2, last))
                    a.probs_lo(dve, n, 0, b_t, cols)
                    if head is not None:
                        a.maxima(dve, slot_of(head), 1, s_parts, b_s)
                    if fetch is not None:
                        qk(fetch, K)
                    if h == 0:
                        for t in range(NT):
                            v(step, t)
                    if h == 1 and before(group, pair) is not None:
                        prev = before(group, pair)
                        a.take_sums(dve, step_of(*prev), *prev, yacc, b_y)
                    a.probs_lo(dve, n, 1, b_t, cols)

            for h in range(2):
                qk((0, 0, h), Q)
                qk((0, 0, h), K)
            for b in range(2):
                a.maxima(dve, 0, b, s_parts, b_s)
            for group in range(NG):
                over_pairs(dve, group, body)
            a.out_lo(dve, slot_of(final), HG - 1, b_o, bias(2, final))
            a.take_sums(dve, NG * NP - 1, NG - 1, NP - 1, yacc, b_y)


STAGES = 4


def piece0(ins, group, i):
    wq, wk, wv, wo = (ins[f"L0_attn_W{n}"] for n in "qkvo")
    if i < 2:
        return [(0, PIECE, wq[i * P:(i + 1) * P, group * PIECE:(group + 1) * PIECE])]
    if i == 2:
        return [(at, D, w.rearrange("(c p) n -> p c n", p=P)[:, :, group * HD:(group + 1) * HD])
                for at, w in ((0, wk), (D, wv))]
    h = group * HG + (i - 3) * 2
    return [(0, PIECE, wo[h * HD:(h + 2) * HD, :].rearrange("(h p) n -> p h n", p=P))]


def start(nc, held, ins, persistent, x_all, h_dram, w_dram, bank):
    rb_gu, rb_d, dd, wr, mod, gbo, const = (persistent[k] for k in
                                            ("gu", "down", "small", "routers", "mod", "gbo", "const"))
    with ExitStack() as ctx:
        def sb(n, shape, dt=F32):
            return ctx.enter_context(nc.sbuf_tensor("s_" + n, shape, dt))

        def sem(n):
            held.append(nc.alloc_semaphore("s_" + n))
            return held[-1]

        c_rows = sb("c_rows", [B, 2, D])
        c_silu = sb("c_silu", [B, 2, D])
        c_T = sb("c_T", [P, 2 * NC * B])
        wmod = sb("wmod", [P, NC, 6 * D])
        rows = sb("rows", [3 * HEADS + NC, P])
        r_rows = sb("r_rows", [E, 2, D])
        raw_g = sb("raw_g", [P, NR, D])
        raw_u = sb("raw_u", [P, NR, D])
        raw_d = sb("raw_d", [P, NC, NR * P])
        raw_s = sb("raw_s", [P, 2, NSH, D])
        raw_sd = sb("raw_sd", [P, NC, FS])
        raw_small = sb("raw_small", [P, D])
        raw_up = sb("raw_up", [P, NC, P])
        mask = sb("mask", [P, P])
        sel = sb("sel", [2 * E, NR * P + P])
        mag, sign = sb("mag", [P, 2, NC * B]), sb("sign", [P, 2, NC * B])
        stage = sb("stage", [P, STAGES, PIECE])
        split = sb("split", [P, STAGES, 2, PIECE], F32R)
        hT2 = [persistent["ff"][:, at:at + 2 * NC * TOK].rearrange("p (a c t) -> p a c t", a=2, c=NC)
               for at in (NJ * 8 * P, NJ * 8 * P + 2 * NC * TOK)]
        tmp = NormTiles(lambda n, s: sb(n, s))

        s_ident, s_const, s_c, s_rows = sem("ident_loaded"), sem("const_loaded"), sem("c_loaded"), sem("rows_loaded")
        s_mod = [sem(f"wmod{i}_loaded") for i in range(2)]
        s_x, s_gu, s_dn, s_small = sem("x_loaded"), sem("gu_loaded"), sem("down_loaded"), sem("small_loaded")
        s_silu, s_cT, s_cTs = sem("silu"), sem("c_turned"), sem("c_T")
        s_modmm, s_modraw, s_modstep = sem("mod_mm"), sem("mod_raw"), sem("mod_step")
        s_modready = sem("mod_ready")
        s_rowsT, s_bias, s_rhi, s_rlo = sem("rows_turned"), sem("bias"), sem("router_hi"), sem("router_lo")
        s_wT, s_whi, s_wlo = sem("w_turned"), sem("w_hi"), sem("w_lo")
        s_stage = [sem(f"stage{i}_loaded") for i in range(STAGES)]
        s_pout = [sem(f"piece{i}_stored") for i in range(STAGES)]
        s_phi, s_plo = sem("piece_hi"), sem("piece_lo")
        s_cast = sem("consts_cast")
        n_ = NormSems(sem, "n", residual=False)
        s_hout = [sem(f"h{i}_stored") for i in range(2)]
        PIECES = [(g, i) for g in range(NG) for i in range(5)]
        SOURCES = [2 if i == 2 else 1 for _, i in PIECES]
        b_mod, b_wT = (bank[1], bank[7]), bank[3:7]
        EARLY = 2
        block = ctx.enter_context(nc.Block())

        @block.sync
        def _(sp):
            sp.dma_start(const.ident[:, :], ins["k_ident"]).then_inc(s_ident, 16)
            for l in range(2):
                sp.dma_start(c_rows[:, l, :], ins[f"L{l}_c"]).then_inc(s_c, 16)
            sp.dma_start(wmod[:, :, :], ins["L0_wmod"].rearrange("(c p) n -> p c n", p=P)).then_inc(s_mod[0], 16)
            sp.dma_start(x_all[:, :, :], ins["L0_attn_x"].rearrange("b s d -> (b s) d").rearrange(
                "(t p) d -> p t d", p=P)).then_inc(s_x, 16)
            for i, k in enumerate(("bq", "bk", "bv", "bo")):
                k_rows = ins[f"L1_attn_{k}"].rearrange("(h d) -> h d", d=P)
                sp.dma_start(rows[i * HEADS:i * HEADS + k_rows.shape[0], :], k_rows).then_inc(s_rows, 16)
            sp.dma_start(r_rows[:, 0, :], ins["L0_ffn_Wr"]).then_inc(s_rows, 16)
            sp.dma_start(r_rows[:, 1, :], ins["L1_ffn_router_w"]).then_inc(s_rows, 16)
            for dst, key in ((const.cos_q, "k_cos_q"), (const.sin_q, "k_sin_q"), (const.cos_k, "k_cos_k"),
                             (const.sin_k, "k_sin_k"), (const.iota8, "k_iota"), (mask, "k_mask"), (sel, "k_sel")):
                sp.dma_start(dst[:, :], ins[key]).then_inc(s_const, 16)
            stored = 0

            def load_piece(n):
                if n >= STAGES:
                    sp.wait_ge(s_plo, n - STAGES + 1)
                for at, size, src in piece0(ins, *PIECES[n]):
                    dst = stage[:, n % STAGES, at:at + size]
                    if len(src.shape) == 3:
                        dst = dst.rearrange("p (c w) -> p c w", c=src.shape[1])
                    sp.dma_start(dst, src).then_inc(s_stage[n % STAGES], 16)

            def store_piece(n):
                g, i = PIECES[n]
                sp.wait_ge(s_plo, n + 1)
                sp.dma_start(w_dram[g][:, i * 2 * PIECE:(i + 1) * 2 * PIECE],
                             split[:, n % STAGES, :, :].bitcast(F32).rearrange("p a w -> p (a w)")
                             ).then_inc(s_pout[n % STAGES], 16)

            for n in range(STAGES):
                load_piece(n)
            for dst, key in ((raw_g, "L0_ffn_Wg"), (raw_u, "L0_ffn_Wu")):
                sp.dma_start(dst[:, :, :], ins[key].rearrange("e f d -> (e f) d").rearrange(
                    "(j p) d -> p j d", p=P)).then_inc(s_gu, 16)
            for i, key in enumerate(("L0_ffn_Wsg", "L0_ffn_Wsu")):
                full = (NSH - 1) * P
                sp.dma_start(raw_s[:, i, 0:NSH - 1, :], ins[key][0:full, :].rearrange(
                    "(j p) d -> p j d", p=P)).then_inc(s_gu, 16)
                sp.dma_start(raw_s[0:LASTW, i, NSH - 1, :], ins[key][full:FS, :]).then_inc(s_gu, 16)
            for c in range(NC):
                sp.dma_start(raw_d[:, c, :].rearrange("p (e f) -> p e f", e=E),
                             ins["L0_ffn_Wd"][:, c * P:(c + 1) * P, :].rearrange("e d f -> d e f")).then_inc(s_dn, 16)
            sp.dma_start(raw_sd[:, :, :], ins["L0_ffn_Wsd"].rearrange("(c p) f -> p c f", p=P)).then_inc(s_dn, 16)
            sp.dma_start(raw_small[:, :], ins["L1_ffn_down_w"].rearrange("e i h -> (e i) h")).then_inc(s_small, 16)
            for c in range(NC):
                sp.dma_start(raw_up[:, c, :].rearrange("p (e i) -> p e i", e=E),
                             ins["L1_ffn_up_w"][:, c * P:(c + 1) * P, :].rearrange("e h i -> h e i")
                             ).then_inc(s_small, 16)
            sp.wait_ge(s_modmm, 1)
            sp.dma_start(wmod[:, :, :], ins["L1_wmod"].rearrange("(c p) n -> p c n", p=P)).then_inc(s_mod[1], 16)
            for n in range(len(PIECES)):
                store_piece(n)
                if n + STAGES < len(PIECES):
                    load_piece(n + STAGES)
            for i in range(STAGES):
                sp.wait_ge(s_pout[i], 16 * len(PIECES[i::STAGES]))

        @block.tensor
        def _(pe):
            pe.wait_ge(s_ident, 16)
            pe.wait_ge(s_silu, 1)
            for l in range(2):
                for c in range(NC):
                    at = (l * NC + c) * B
                    mm = pe.transpose(bank[0][:, at:at + B], c_silu[:, l, c * P:(c + 1) * P],
                                      const.ident[0:B, 0:B])
            mm.then_inc(s_cT, 1)
            pe.wait_ge(s_rows, 16 * 6)
            mm = pe.transpose(bank[2][:, 0:3 * HEADS + NC], rows[:, :],
                              const.ident[0:3 * HEADS + NC, 0:3 * HEADS + NC])
            for l in range(2):
                for c in range(NC):
                    at = P + (l * NC + c) * E
                    mm = pe.transpose(bank[2][:, at:at + E], r_rows[:, l, c * P:(c + 1) * P],
                                      const.ident[0:E, 0:E])
            mm.then_inc(s_rowsT, 1)
            pe.wait_ge(s_cTs, 1)
            for l in range(2):
                if l:
                    for p in range(NP):
                        turn_norm(pe, n_, p, tmp, const.ident, bank[5:7])
                pe.wait_ge(s_mod[l], 16)
                for j in range(6 * NC):
                    at = j * B
                    for c in range(NC):
                        mm = pe.matmul(b_mod[l][:, at:at + B], wmod[:, c, j * P:(j + 1) * P],
                                       c_T[:, (l * NC + c) * B:(l * NC + c + 1) * B],
                                       start=(c == 0), stop=(c == NC - 1))
                mm.then_inc(s_modmm, 1)
            for n in range(NJ + NJ + 1):
                out = b_wT[n % 4]
                if n == 2:
                    pe.wait_ge(n_.h, 4 * NP)
                if n >= 4:
                    pe.wait_ge(s_wlo, n - 3)
                if n < NJ:
                    if n == 0:
                        pe.wait_ge(s_gu, 16 * 6)
                    w = width(n)
                    for i, (raw, c) in enumerate((r, c) for r in range(2) for c in range(NC)):
                        if n < NR:
                            src = (raw_g, raw_u)[raw][:, n, c * P:(c + 1) * P]
                        else:
                            src = raw_s[0:w, raw, n - NR, c * P:(c + 1) * P]
                        mm = pe.transpose(out[:, i * P:i * P + w], src, const.ident[0:w, 0:w])
                elif n < 2 * NJ:
                    j = n - NJ
                    if j == 0:
                        pe.wait_ge(s_dn, 16 * 3)
                    w = width(j)
                    for c in range(NC):
                        src = raw_d[:, c, j * P:(j + 1) * P] if j < NR else \
                            raw_sd[:, c, (j - NR) * P:(j - NR) * P + w]
                        mm = pe.transpose(out[0:w, c * P:(c + 1) * P], src, const.ident[:, :])
                else:
                    pe.wait_ge(s_small, 16 * 3)
                    for c in range(NC):
                        pe.transpose(out[:, c * P:(c + 1) * P], raw_small[:, c * P:(c + 1) * P], const.ident[:, :])
                        mm = pe.transpose(out[:, (NC + c) * P:(NC + c + 1) * P], raw_up[:, c, :], const.ident[:, :])
                mm.then_inc(s_wT, 1)

        def weight_parts(n):
            src = b_wT[n % 4]
            if n < NJ:
                w = width(n)
                view = src[:, :].rearrange("p (i w) -> p i w", i=4)[:, :, 0:w]
                return view, [rb_gu[:, n, hl, :, 0:w] for hl in range(2)]
            if n < 2 * NJ:
                j, w = n - NJ, width(n - NJ)
                return src[0:w, 0:D], [rb_d[0:w, hl, j, :] for hl in range(2)]
            return src[:, :], [dd[:, hl, :] for hl in range(2)]

        @block.scalar
        def _(act):
            act.wait_ge(s_c, 32)
            act.activation(c_silu[:, :, :], c_rows[:, :, :], ACT.Silu).then_inc(s_silu, 1)
            act.wait_ge(s_cT, 1)
            act.activation(c_T[:, :], bank[0][:, 0:2 * NC * B], ACT.Identity).then_inc(s_cTs, 1)
            act.wait_ge(s_rowsT, 1)
            act.activation(wr[:, :, 0, :], bank[2][:, P:P + 2 * NC * E].rearrange("p (l w) -> p l w", l=2),
                           ACT.Identity).then_inc(s_rhi, 1)

            def piece(n):
                act.wait_ge(s_stage[n % STAGES], sum(SOURCES[n % STAGES:n + 1:STAGES]) * 16)
                if n >= STAGES:
                    act.wait_ge(s_pout[n % STAGES], 16 * (n // STAGES))
                act.activation(split[:, n % STAGES, 0, :], stage[:, n % STAGES, :], ACT.Identity).then_inc(s_phi, 1)

            def store_h(p):
                act.wait_ge(n_.lo, p * 2 + 2)
                act.dma_start(h_dram[p], hT2[p % 2].bitcast(F32).rearrange("p a c t -> p (a c t)")
                              ).then_inc(s_hout[p % 2], 16)

            for p in range(NP):
                cur = mod[:, 0, :, 2 * p:2 * p + 2]
                ge(act, n_.lo, p * 2)
                modulate(act, n_, p, kinds(cur, SA), kinds(cur, CA), tmp, bank[5:7])
                for n in range(p * EARLY, (p + 1) * EARLY):
                    piece(n)
                if p:
                    store_h(p - 1)
            store_h(NP - 1)
            for n in range(NJ + NJ + 1):
                act.wait_ge(s_wT, n + 1)
                src, (hi, _) = weight_parts(n)
                if n == NJ:
                    for i in range(2):
                        act.wait_ge(s_hout[i], 16 * NP // 2)
                act.activation(hi, src, ACT.Identity).then_inc(s_whi, 1)
                if n % 2 == 0 and NP * EARLY + n // 2 < len(PIECES):
                    piece(NP * EARLY + n // 2)

        @block.vector
        def _(dve):
            step = 0

            def modulation(l):
                nonlocal step
                dve.wait_ge(s_modmm, l + 1)
                dve.tensor_copy(mod[:, l, :, :].rearrange("p k b -> p (k b)"),
                                b_mod[l][:, 0:6 * NC * B]).then_inc(s_modraw, 1)
                dve.wait_ge(s_modraw, l + 1)
                for c_kind, g_kind in ((CA, GA), (CB, GB)):
                    scale = mod[:, l, c_kind * NC:(c_kind + 1) * NC, :]
                    gate = mod[:, l, g_kind * NC:(g_kind + 1) * NC, :]
                    m = mag[:, l, :].rearrange("p (c b) -> p c b", c=NC)
                    sg = sign[:, l, :].rearrange("p (c b) -> p c b", c=NC)
                    for ins_ in (
                            lambda: dve.tensor_scalar(scale, scale, 1.0, None, ALU.add),
                            lambda: dve.scalar_tensor_tensor(out=m, in0=gate, scalar=-1.0, in1=gate,
                                                             op0=ALU.mult, op1=ALU.max),
                            lambda: dve.tensor_scalar(sg, gate, 0.0, 2.0, ALU.is_ge, ALU.mult),
                            lambda: dve.tensor_scalar(sg, sg, -1.0, None, ALU.add),
                            lambda: dve.scalar_tensor_tensor(out=gate, in0=m, scalar=0.25, in1=sg,
                                                             op0=ALU.max, op1=ALU.mult)):
                        step += 1
                        ins_().then_inc(s_modstep, 1)
                        dve.wait_ge(s_modstep, step)

            dve.memset(const.minus_half[:, :], -0.5).then_inc(s_cast, 1)
            modulation(0)
            dve.wait_ge(s_x, 16)
            xs = [x_all[:, p * NT:(p + 1) * NT, :] for p in range(NP)]
            norm_stats(dve, n_, 0, xs[0], tmp)
            for p in range(NP):
                ge(dve, n_.turned, p * 2)
                norm_scale(dve, n_, p, xs[p], tmp)
                if p + 1 < NP:
                    norm_stats(dve, n_, p + 1, xs[p + 1], tmp)
                ge(dve, s_hout[p % 2], p // 2 * 16)
                split_h(dve, n_, p, tmp, hT2[p % 2])
            dve.wait_ge(s_ident, 16)
            dve.wait_ge(s_const, 16 * 7)
            dve.tensor_copy(const.ident_r[:, :], const.ident[:, :]).then_inc(s_cast, 1)
            dve.tensor_copy(const.mask_r[:, :], mask[:, :]).then_inc(s_cast, 1)
            dve.tensor_copy(const.sel_r[:, :], sel[:, :]).then_inc(s_cast, 1)
            dve.wait_ge(s_rhi, 1)
            dve.tensor_copy(const.biasT[:, :], bank[2][:, 0:3 * HEADS + NC]).then_inc(s_bias, 1)
            dve.wait_ge(s_bias, 1)
            dve.tensor_scalar(const.biasT[:, 0:HEADS], const.biasT[:, 0:HEADS], SCALE, None,
                              ALU.mult).then_inc(s_bias, 1)
            dve.tensor_tensor(wr[:, :, 1, :], bank[2][:, P:P + 2 * NC * E].rearrange("p (l w) -> p l w", l=2),
                              wr[:, :, 0, :].bitcast(F32), ALU.subtract).then_inc(s_rlo, 1)
            modulation(1)
            for c in range(NC):
                ga1 = mod[:, 1, GA * NC + c, :]
                ins_ = dve.tensor_scalar(gbo[:, c, :], ga1, const.biasT[:, 3 * HEADS + c:3 * HEADS + c + 1],
                                         None, ALU.mult)
            ins_.then_inc(s_modready, 1)
            for n in range(NJ + NJ + 1):
                dve.wait_ge(s_whi, n + 1)
                src, (hi, lo) = weight_parts(n)
                dve.tensor_tensor(lo, src, hi.bitcast(F32), ALU.subtract).then_inc(s_wlo, 1)

        @block.gpsimd
        def _(pool):
            def piece(n):
                pool.wait_ge(s_phi, n + 1)
                pool.tensor_tensor(split[:, n % STAGES, 1, :], stage[:, n % STAGES, :],
                                   split[:, n % STAGES, 0, :].bitcast(F32), ALU.subtract).then_inc(s_plo, 1)

            pool.wait_ge(s_cast, 1)
            norm_pool(pool, n_, 0, tmp, const.minus_half)
            for p in range(NP):
                if p + 1 < NP:
                    norm_pool(pool, n_, p + 1, tmp, const.minus_half)
                for n in range(p * EARLY, (p + 1) * EARLY):
                    piece(n)
            for n in range(NP * EARLY, len(PIECES)):
                piece(n)


def piece1(ins, group, i):
    if i < 6:
        w, c = "qkv"[i // 2], i % 2
        codes, scales = ins[f"L1_attn_w{w}_codes"], ins[f"L1_attn_w{w}_scales"]
        cols = bass.ds(group * PIECE, PIECE)
        return [(0, PIECE, codes[c * P:(c + 1) * P, cols])], [(0, PIECE, scales[c * 4:(c + 1) * 4, cols])]
    codes, scales = ins["L1_attn_wo_codes"], ins["L1_attn_wo_scales"]
    first = group * HG + (i - 6) * 2
    return ([(k * D, D, codes[bass.ds((first + k) * HD, HD), :]) for k in range(2)],
            [(k * D, D, scales[bass.ds((first + k) * 4, 4), :]) for k in range(2)])


def feed_forward0(nc, held, ins, persistent, spare, first_weights, first_h, yacc, h_dram, w_dram, x_dram, bank):
    gu, down, wr, mod, const = (persistent[k] for k in ("gu", "down", "routers", "mod", "const"))
    PIECES = 8
    with ExitStack() as ctx:
        def sb(n, shape, dt=F32):
            return ctx.enter_context(nc.sbuf_tensor("f0_" + n, shape, dt))

        def sem(n):
            held.append(nc.alloc_semaphore("f0_" + n))
            return held[-1]

        x2 = sb("x", [P, 2, NT, D])
        hT2 = sb("hT", [P, 2, 2, NC, TOK], F32R)
        ys = sb("ys", [P, NC, TOK])
        cur = sb("cur", [P, 6 * NC, 2])
        cur_back = sb("cur_back", [P, 2, 6 * NC, 2])
        tmp = NormTiles(lambda n, s: sb(n, s))
        r = RouterTiles(sb)
        silu = sb("silu", [P, 2, TOK])
        prod = sb("prod", [P, 2, TOK])
        act_hl = sb("act_hl", [P, 2, 2, TOK], F32R)
        codes = sb("codes", [P, 2, PIECE])
        scales = sb("scales", [P, 2, PIECE])
        split = spare.rearrange("p (i a w) -> p i a w", i=2, a=2)
        b_g, b_u, b_w, b_r, b_y = bank[0:2], bank[2:4], bank[4], bank[5], bank[6:8]

        n1, n2 = NormSems(sem, "n1"), NormSems(sem, "n2")
        rs = RouterSems(sem, "r")
        x_in, x_out, h_out = sem("x_loaded"), sem("x_stored"), sem("h_stored")
        gu_mm, w_mm, y_mm = sem("gu_mm"), sem("w_mm"), sem("y_mm")
        silu_done, mul_done, gated = sem("silu"), sem("mul"), sem("gated")
        a_hi, a_lo = sem("a_hi"), sem("a_lo")
        w_in = sem("first_weights_loaded")
        p_w, p_hi, p_lo = (sem("piece_" + k) for k in ("w", "hi", "lo"))
        p_in = [sem(f"piece{i}_loaded") for i in range(2)]
        p_out = [sem(f"piece{i}_stored") for i in range(2)]
        p_passed, sp_passed = sem("piece_passed"), sem("sp_passed")
        LOADS = 3 * 5 + 10
        block = ctx.enter_context(nc.Block())


        @block.sync
        def _(sp):
            def store_piece(p, i):
                sp.wait_ge(p_lo, p * PIECES + i + 1)
                sp.dma_start(w_dram[p][:, i * 2 * PIECE:(i + 1) * 2 * PIECE],
                             split[:, i % 2, :, :].bitcast(F32).rearrange("p a w -> p (a w)")).then_inc(p_out[i % 2], 16)

            def load_x(p, buf):
                sp.dma_start(x2[:, buf, :, :], ins["L0_attn_x"].rearrange("b s d -> (b s) d").rearrange(
                    "(g t p) d -> g p t d", p=P, t=NT)[p]).then_inc(x_in, 16)

            def store_back(p, buf):
                hold(sp, n2.x_new, p * 2 + 2, sp_passed)
                sp.dma_start(x_dram[p], x2[:, buf, :, :].rearrange("p t d -> p (t d)")).then_inc(x_out, 16)

            def store_h(p, buf):
                hold(sp, n2.lo, p * 2 + 2, sp_passed)
                sp.dma_start(h_dram[p], hT2[:, buf, :, :, :].bitcast(F32).rearrange("p a c t -> p (a c t)")
                             ).then_inc(h_out, 16)

            def body(_, p):
                for i in range(PIECES):
                    if i >= 2:
                        sp.wait_ge(p_lo, p * PIECES + i - 1)
                    code_src, scale_src = piece1(ins, p, i)
                    for at, size, src in code_src:
                        sp.dma_start(codes[:, i % 2, at:at + size], src).then_inc(p_in[i % 2], 16)
                    for at, size, src in scale_src:
                        for k in range(4):
                            sp.dma_start(scales[32 * k:32 * k + 32, i % 2, at:at + size],
                                         src[k:k + 1, :].broadcast_to([32, size])).then_inc(p_in[i % 2], 16)
                    if i:
                        store_piece(p, i - 1)
                    if i == 4 and has(p, -1):
                        store_back(p - 1, other(p))
                    if i == 5 and has(p, 1):
                        if has(p, -1):
                            hold(sp, x_out, p * 16, sp_passed)
                            hold(sp, n2.xhat, p * 4, sp_passed)
                        load_x(p + 1, other(p))
                store_piece(p, PIECES - 1)
                if has(p, -1):
                    store_h(p - 1, other(p))

            load_x(0, turns(0))
            over_pairs(sp, 0, body)
            for i in range(2):
                sp.wait_ge(p_out[i], 16 * NP * PIECES // 2)
            sp.dma_start(first_weights, w_dram[0]).then_inc(w_in, 16)
            sp.wait_ge(h_out, 16 * (NP - 1))
            sp.dma_start(first_h, h_dram[0]).then_inc(w_in, 16)
            store_back(NP - 1, turns(NP - 1))
            store_h(NP - 1, turns(NP - 1))
            sp.wait_ge(h_out, 16 * NP)
            sp.wait_ge(x_out, 16 * NP)
            sp.wait_ge(w_in, 32)

        @block.gpsimd
        def _(pool):
            def body(_, p):
                loads = [0, 0]
                for i in range(PIECES):
                    loads[i % 2] += 5 if i < 6 else 10
                    hold(pool, p_in[i % 2], p * (LOADS * 16) + loads[i % 2] * 16, p_passed)
                    w, s_ = codes[:, i % 2, :], scales[:, i % 2, :]
                    if i < 2:
                        pool.tensor_scalar(s_, s_, SCALE, 1.0, ALU.mult, ALU.mult).then_inc(p_hi, 1)
                        pool.wait_ge(p_hi, p * (PIECES + 2) + 2 * i + 1)
                    ge(pool, p_out[i % 2], p * (PIECES // 2 * 16) + i // 2 * 16)
                    pool.tensor_tensor(split[:, i % 2, 0, :], w, s_, ALU.mult).then_inc(p_hi, 1)
                    pool.wait_ge(p_hi, p * (PIECES + 2) + (2 * i + 2 if i < 2 else i + 3))
                    pool.tensor_tensor(w, w, s_, ALU.mult).then_inc(p_w, 1)
                    pool.wait_ge(p_w, p * PIECES + i + 1)
                    pool.tensor_tensor(split[:, i % 2, 1, :], w, split[:, i % 2, 0, :].bitcast(F32),
                                       ALU.subtract).then_inc(p_lo, 1)
                    if i == 3 and has(p, -1):
                        norm_pool(pool, n2, p - 1, tmp, const.minus_half)
                if has(p, 1):
                    norm_pool(pool, n1, p + 1, tmp, const.minus_half)

            norm_pool(pool, n1, 0, tmp, const.minus_half)
            over_pairs(pool, 0, body)
            norm_pool(pool, n2, NP - 1, tmp, const.minus_half)

        @block.tensor
        def _(pe):
            def side(k, p):
                if has(p, -1):
                    q = p - 1
                    if k == 3:
                        pe.wait_ge(n2.scaled, q * 4 + 4)
                        turn_half(pe, n2, 0, ys, const.ident, b_r)
                    if k == 4:
                        pe.wait_ge(n2.x_new, q * 2 + 1)
                        turn_half(pe, n2, 1, ys, const.ident, b_r)
                    if k == 6:
                        pe.wait_ge(n2.xhat, q * 4 + 4)
                        turn_chunk(pe, n2, 0, tmp, const.ident, b_r)
                    if k == 7:
                        pe.wait_ge(n2.h, q * 4 + 2)
                        turn_chunk(pe, n2, 1, tmp, const.ident, b_r)
                if has(p, 1):
                    q = p + 1
                    if k == 8:
                        if has(p, -1):
                            pe.wait_ge(n2.h, p * 4)
                        pe.wait_ge(n1.scaled, q * 4 + 4)
                        turn_half(pe, n1, 0, ys, const.ident, b_r)
                    if k == 10:
                        pe.wait_ge(n1.x_new, q * 2 + 1)
                        turn_half(pe, n1, 1, ys, const.ident, b_r)
                    if k == 12:
                        pe.wait_ge(n1.xhat, q * 4 + 4)
                        turn_chunk(pe, n1, 0, tmp, const.ident, b_r)
                    if k == 13:
                        pe.wait_ge(n1.h, q * 4 + 2)
                        turn_chunk(pe, n1, 1, tmp, const.ident, b_r)

            def body(_, p):
                hT = hT2[:, turns(p), :, :, :]
                pe.wait_ge(n1.lo, p * 2 + 2)
                router_logits(pe, rs, hT, wr[:, 0], b_r)
                for k in range(NJ + 2):
                    if k < NJ:
                        j, w = CHUNKS[k], width(CHUNKS[k])
                        ge(pe, mul_done, p * NJ + (k - 1))
                        for i, bk in ((0, b_g[k % 2]), (2, b_u[k % 2])):
                            mm = split_matmuls(pe, bk[0:w, :], [
                                (lambda hl, c=c, i=i: gu[:, j, hl, i + c, 0:w], lambda hl, c=c: hT[:, hl, c, :])
                                for c in range(NC)])
                        mm.then_inc(gu_mm, 1)
                        if k == 0:
                            router_logits_turn(pe, rs, p, r, const.ident, b_w)
                        if k == NSH:
                            router_turn(pe, rs, p, r, const.ident, b_r)
                        if k > NSH:
                            pe.wait_ge(gated, p * NR + (k - NSH))
                            pe.matmul(b_w[:, :], const.sel_r[:, j * P:(j + 1) * P], r.wT[:, :],
                                      start=True, stop=True).then_inc(w_mm, 1)
                    if k >= 2:
                        j, w = CHUNKS[k - 2], width(CHUNKS[k - 2])
                        pe.wait_ge(a_lo, p * NJ + (k - 1))
                        if k == 2 and has(p, -1):
                            pe.wait_ge(n2.scaled, p * 4)
                        for c in range(NC):
                            for i, (a, m) in enumerate(PASSES):
                                mm = pe.matmul(b_y[c][:, :], down[0:w, a, j, c * P:(c + 1) * P],
                                               act_hl[0:w, k % 2, m, :], start=(k == 2 and i == 0),
                                               stop=(k == NJ + 1 and i == len(PASSES) - 1))
                        mm.then_inc(y_mm, 1)
                    if k == NSH:
                        pe.wait_ge(rs.wT, p + 1)
                        pe.matmul(b_w[:, :], const.sel_r[:, 0:P], r.wT[:, :],
                                  start=True, stop=True).then_inc(w_mm, 1)
                    side(k, p)

            turn_branch(pe, n1, 0, ys, const.ident, b_g)
            turn_norm(pe, n1, 0, tmp, const.ident, b_u)
            over_pairs(pe, 0, body)
            turn_branch(pe, n2, NP - 1, ys, const.ident, b_g)
            turn_norm(pe, n2, NP - 1, tmp, const.ident, b_u)

        @block.scalar
        def _(act):
            def back_scale(q):
                act.wait_ge(n2.mod, q * 2 + 2)
                act.wait_ge(y_mm, q * NJ + NJ)
                scale_branch(act, n2, q, lambda c, b: b_y[c][:, b * S:(b + 1) * S],
                             kinds(cur_back[:, 0], GB), None, ys)

            def front_scale(q):
                act.wait_ge(n1.mod, q + 1)
                scale_branch(act, n1, q, lambda c, b: yacc[:, c, bass.ds(q * TOK + b * S, S)],
                             kinds(cur, GA), None, ys)

            def side(k, p):
                if has(p, -1) and k in (6, 7):
                    modulate_chunk(act, n2, p - 1, k - 6, kinds(cur_back[:, 1], SA), kinds(cur_back[:, 1], CA),
                                   tmp, b_r)
                if has(p, 1):
                    if k == 7:
                        front_scale(p + 1)
                    if k in (12, 14):
                        modulate_chunk(act, n1, p + 1, (k - 12) // 2, kinds(cur, SB), kinds(cur, CB), tmp, b_r)

            def body(_, p):
                if has(p, -1):
                    back_scale(p - 1)
                router_logits_copy(act, rs, p, r, b_r)
                for k in range(NJ + 1):
                    if k < NJ:
                        w = width(CHUNKS[k])
                        act.wait_ge(gu_mm, p * NJ + (k + 1))
                        act.activation(silu[0:w, k % 2, :], b_g[k % 2][0:w, :], ACT.Silu).then_inc(silu_done, 1)
                    if k:
                        w = width(CHUNKS[k - 1])
                        act.wait_ge(mul_done, p * NJ + k)
                        if k - 1 >= NSH:
                            act.wait_ge(gated, p * NR + (k - NSH))
                        ge(act, y_mm, p * NJ + (k - 2))
                        act.activation(act_hl[0:w, (k - 1) % 2, 0, :], prod[0:w, (k - 1) % 2, :],
                                       ACT.Identity).then_inc(a_hi, 1)
                    if k == 0:
                        router_exp(act, rs, p, r)
                    if k == NSH:
                        router_copy(act, rs, p, r, b_r)
                    side(k, p)

            front_scale(0)
            modulate(act, n1, 0, kinds(cur, SB), kinds(cur, CB), tmp, b_u)
            over_pairs(act, 0, body)
            back_scale(NP - 1)
            modulate(act, n2, NP - 1, kinds(cur_back[:, 1], SA), kinds(cur_back[:, 1], CA), tmp, b_u)

        @block.vector
        def _(dve):
            def back_mod(q):
                for l in range(2):
                    copy_mod(dve, n2, q, mod[:, l], cur_back[:, l])

            def side(k, p):
                if has(p, -1):
                    q, x = p - 1, x2[:, other(p), :, :]
                    if k in (3, 4):
                        add_half(dve, n2, q, k - 3, x, b_r)
                        tile_stats(dve, n2, q, k - 3, x, tmp)
                    if k == 4:
                        mean_and_var(dve, n2, q, tmp)
                    if k == 5:
                        norm_scale(dve, n2, q, x, tmp)
                    if k in (7, 8):
                        split_chunk(dve, n2, q, k - 7, tmp, hT2[:, other(p), :, :, :])
                if has(p, 1):
                    q, x = p + 1, x2[:, other(p), :, :]
                    if k == 6:
                        copy_mod(dve, n1, q, mod[:, 0], cur)
                    if k == 9:
                        dve.wait_ge(x_in, q * 16 + 16)
                    if k in (9, 10):
                        add_half(dve, n1, q, k - 9, x, b_r)
                        tile_stats(dve, n1, q, k - 9, x, tmp)
                    if k == 10:
                        mean_and_var(dve, n1, q, tmp)
                    if k == 11:
                        norm_scale(dve, n1, q, x, tmp)
                    if k == 13:
                        ge(dve, h_out, p * 16)
                        for c in range(NC):
                            split_chunk(dve, n1, q, c, tmp, hT2[:, other(p), :, :, :])

            def body(_, p):
                if has(p, -1):
                    back_mod(p - 1)
                router_shift(dve, rs, p, r, b_w)
                for k in range(NJ):
                    w = width(CHUNKS[k])
                    pr = prod[0:w, k % 2, :]
                    dve.wait_ge(silu_done, p * NJ + (k + 1))
                    ge(dve, a_hi, p * NJ + (k - 1))
                    dve.tensor_tensor(pr, b_u[k % 2][0:w, :], silu[0:w, k % 2, :], ALU.mult).then_inc(mul_done, 1)
                    if k == 1:
                        router_weights(dve, rs, p, r, const.iota8)
                    if k >= NSH:
                        dve.wait_ge(mul_done, p * NJ + (k + 1))
                        dve.wait_ge(w_mm, p * NR + (k - NSH + 1))
                        dve.tensor_tensor(pr, b_w[0:w, :], pr, ALU.mult).then_inc(gated, 1)
                    dve.wait_ge(a_hi, p * NJ + (k + 1))
                    dve.tensor_tensor(act_hl[0:w, k % 2, 1, :], pr, act_hl[0:w, k % 2, 0, :].bitcast(F32),
                                      ALU.subtract).then_inc(a_lo, 1)
                    side(k, p)

            copy_mod(dve, n1, 0, mod[:, 0], cur)
            dve.wait_ge(x_in, 16)
            x = x2[:, turns(0), :, :]
            add_branch(dve, n1, 0, x, b_g)
            norm_dve(dve, n1, 0, x, tmp)
            split_h(dve, n1, 0, tmp, hT2[:, turns(0), :, :, :])
            over_pairs(dve, 0, body)
            back_mod(NP - 1)
            x = x2[:, turns(NP - 1), :, :]
            add_branch(dve, n2, NP - 1, x, b_g)
            norm_dve(dve, n2, NP - 1, x, tmp)
            split_h(dve, n2, NP - 1, tmp, hT2[:, turns(NP - 1), :, :, :])


def feed_forward1(nc, held, persistent, yacc, x_dram, out, bank):
    small, wr, mod, gbo, const = (persistent[k] for k in ("small", "routers", "mod", "gbo", "const"))
    with ExitStack() as ctx:
        def sb(n, shape, dt=F32):
            return ctx.enter_context(nc.sbuf_tensor("f1_" + n, shape, dt))

        def sem(n):
            held.append(nc.alloc_semaphore("f1_" + n))
            return held[-1]

        xs = sb("x", [P, NP, NT, D])
        hT2 = sb("hT", [P, 2, 2, NC, TOK], F32R)
        ys, ys_back = sb("ys", [P, NC, TOK]), sb("ys_back", [P, NC, TOK])
        cur, cur_back = sb("cur", [P, 6 * NC, 2]), sb("cur_back", [P, 6 * NC, 2])
        bo = sb("bo", [P, NC, 2])
        tmp = NormTiles(lambda n, s: sb(n, s))
        r = RouterTiles(sb)
        silu = sb("silu", [P, TOK])
        act_hl = sb("act_hl", [P, 2, TOK], F32R)
        b_turn, b_norm, b_w, b_h, b_r, b_y = bank[0:2], bank[2], bank[3], bank[4], bank[5], bank[6:8]
        n1, n2 = NormSems(sem, "n1"), NormSems(sem, "n2", norm=False)
        rs = RouterSems(sem, "r")
        x_in, x_out = sem("x_loaded"), sem("x_stored")
        d_mm, w_mm, y_mm = sem("down_mm"), sem("w_mm"), sem("y_mm")
        silu_done, gated, a_hi, a_lo = sem("silu"), sem("gated"), sem("a_hi"), sem("a_lo")
        bo_done, back_mod, sp_passed = sem("bo"), sem("back_mod"), sem("sp_passed")
        block = ctx.enter_context(nc.Block())


        @block.sync
        def _(sp):
            def load(p):
                sp.dma_start(xs[:, p, :, :].rearrange("p t d -> p (t d)"), x_dram[p]).then_inc(x_in, 16)

            def store(p):
                hold(sp, n2.x_new, p * 2 + 2, sp_passed)
                sp.dma_start(out.rearrange("b s d -> (b s) d").rearrange("(g t p) d -> g p t d", p=P, t=NT)[p],
                             xs[:, p, :, :]).then_inc(x_out, 16)

            def body(_, p):
                if has(p, 1):
                    hold(sp, x_in, p * 16 + 16, sp_passed)
                    load(p + 1)
                if has(p, -1):
                    store(p - 1)

            load(0)
            over_pairs(sp, 0, body)
            store(NP - 1)
            sp.wait_ge(x_out, 16 * NP)

        @block.gpsimd
        def _(pool):
            with pool.Fori(0, NP) as p:
                norm_pool(pool, n1, p, tmp, const.minus_half)

        @block.tensor
        def _(pe):
            def norm_chunk(q, c):
                if c == 0:
                    pe.wait_ge(n1.xhat, q * 4 + 4)
                else:
                    pe.wait_ge(n1.h, q * 4 + 2)
                turn_chunk(pe, n1, c, tmp, const.ident, b_norm)

            def body(_, p):
                hT = hT2[:, turns(p), :, :, :]
                pe.wait_ge(n1.lo, p * 2 + 2)
                router_logits(pe, rs, hT, wr[:, 1], b_r)
                split_matmuls(pe, b_h[:, :], [(lambda hl, c=c: small[:, hl, c * P:(c + 1) * P],
                                               lambda hl, c=c: hT[:, hl, c, :]) for c in range(NC)]
                              ).then_inc(d_mm, 1)
                if has(p, 1):
                    turn_branch(pe, n1, p + 1, ys, const.ident, b_turn)
                if has(p, -1):
                    turn_branch(pe, n2, p - 1, ys_back, const.ident, b_y)
                router_logits_turn(pe, rs, p, r, const.ident, b_w)
                if has(p, 1):
                    norm_chunk(p + 1, 0)
                router_turn(pe, rs, p, r, const.ident, b_r)
                if has(p, 1):
                    norm_chunk(p + 1, 1)
                pe.wait_ge(rs.wT, p + 1)
                pe.matmul(b_w[:, :], const.sel_r[:, NR * P:(NR + 1) * P], r.wT[:, :],
                          start=True, stop=True).then_inc(w_mm, 1)
                pe.wait_ge(a_lo, p + 1)
                if has(p, -1):
                    pe.wait_ge(n2.x_new, p * 2)
                for c in range(NC):
                    mm = split_matmuls(pe, b_y[c][:, :], [(lambda hl: small[:, hl, (NC + c) * P:(NC + c + 1) * P],
                                                           lambda hl: act_hl[:, hl, :])])
                mm.then_inc(y_mm, 1)

            turn_branch(pe, n1, 0, ys, const.ident, b_turn)
            norm_chunk(0, 0)
            norm_chunk(0, 1)
            over_pairs(pe, 0, body)
            turn_branch(pe, n2, NP - 1, ys_back, const.ident, b_turn)

        @block.scalar
        def _(act):
            def front_scale(q):
                act.wait_ge(n1.mod, q + 1)
                act.wait_ge(bo_done, q + 1)
                scale_branch(act, n1, q, lambda c, b: yacc[:, c, bass.ds(q * TOK + b * S, S)],
                             kinds(cur, GA), bo, ys)

            def front_modulate(q):
                for c in range(NC):
                    modulate_chunk(act, n1, q, c, kinds(cur, SB), kinds(cur, CB), tmp, b_norm)

            def body(_, p):
                router_logits_copy(act, rs, p, r, b_r)
                if has(p, 1):
                    front_scale(p + 1)
                router_exp(act, rs, p, r)
                act.wait_ge(d_mm, p + 1)
                act.activation(silu[:, :], b_h[:, :], ACT.Silu).then_inc(silu_done, 1)
                if has(p, 1):
                    front_modulate(p + 1)
                router_copy(act, rs, p, r, b_r)
                act.wait_ge(gated, p + 1)
                act.activation(act_hl[:, 0, :], silu[:, :], ACT.Identity).then_inc(a_hi, 1)
                act.wait_ge(back_mod, p + 1)
                act.wait_ge(y_mm, p + 1)
                scale_branch(act, n2, p, lambda c, b: b_y[c][:, b * S:(b + 1) * S], kinds(cur_back, GB), None,
                             ys_back)

            front_scale(0)
            front_modulate(0)
            over_pairs(act, 0, body)

        @block.vector
        def _(dve):
            def front_mod(q):
                copy_mod(dve, n1, q, mod[:, 1], cur)
                dve.tensor_copy(bo[:, :, :], gbo[:, :, bass.ds(q * 2, 2)]).then_inc(bo_done, 1)

            def front_add(q, x):
                dve.wait_ge(x_in, q * 16 + 16)
                add_branch(dve, n1, q, x, b_turn)
                norm_stats(dve, n1, q, x, tmp)

            def body(_, p):
                if has(p, 1):
                    x_next = xs[:, p + 1, :, :]
                    front_mod(p + 1)
                    front_add(p + 1, x_next)
                router_shift(dve, rs, p, r, b_w)
                if has(p, 1):
                    norm_scale(dve, n1, p + 1, x_next, tmp)
                router_weights(dve, rs, p, r, const.iota8)
                if has(p, -1):
                    add_branch(dve, n2, p - 1, xs[:, p - 1, :, :], b_y)
                dve.tensor_copy(cur_back[:, :, :], mod[:, 1, :, bass.ds(p * 2, 2)]).then_inc(back_mod, 1)
                if has(p, 1):
                    split_h(dve, n1, p + 1, tmp, hT2[:, other(p), :, :, :])
                dve.wait_ge(silu_done, p + 1)
                dve.wait_ge(w_mm, p + 1)
                dve.tensor_tensor(silu[:, :], b_w[:, :], silu[:, :], ALU.mult).then_inc(gated, 1)
                dve.wait_ge(a_hi, p + 1)
                dve.tensor_tensor(act_hl[:, 1, :], silu[:, :], act_hl[:, 0, :].bitcast(F32),
                                  ALU.subtract).then_inc(a_lo, 1)

            x = xs[:, 0, :, :]
            front_mod(0)
            front_add(0, x)
            norm_scale(dve, n1, 0, x, tmp)
            split_h(dve, n1, 0, tmp, hT2[:, turns(0), :, :, :])
            over_pairs(dve, 0, body)
            add_branch(dve, n2, NP - 1, xs[:, NP - 1, :, :], b_turn)


class Constants:
    def __init__(self, sb):
        self.ident = sb("ident", [P, P])
        self.ident_r = sb("ident_r", [P, P], F32R)
        self.mask_r = sb("mask_r", [P, P], F32R)
        self.sel_r = sb("sel_r", [2 * E, (NR + 1) * P], F32R)
        self.cos_q, self.sin_q = sb("cos_q", [P, S]), sb("sin_q", [P, S])
        self.cos_k, self.sin_k = sb("cos_k", [P, S]), sb("sin_k", [P, S])
        self.iota8 = sb("iota8", [P, E])
        self.minus_half = sb("minus_half", [P, NT])
        self.biasT = sb("biasT", [P, 3 * HEADS + NC])


def release(nc, held):
    nc.clear_and_free_semaphores(held)
    nc.all_engine_barrier()


def program(nc, ins, out):
    def dram(name, shape):
        return nc.dram_tensor(name, shape, F32, kind="Internal").ap()

    h0_dram, h1_dram = dram("h0", [NP, P, 2 * NC * TOK]), dram("h1", [NP, P, 2 * NC * TOK])
    w0_dram, w1_dram = dram("w0", [NG, P, 5 * 2 * PIECE]), dram("w1", [NG, P, 8 * 2 * PIECE])
    x_dram = dram("x2", [NP, P, NT * D])
    with ExitStack() as ctx:
        def sb(n, shape, dt=F32):
            return ctx.enter_context(nc.sbuf_tensor(n, shape, dt))

        bank = [ctx.enter_context(nc.psum_tensor(f"bank{i}", [P, 512], F32)) for i in range(8)]
        rb = sb("ff_weights", [P, NJ * 8 * P + 2 * NJ * D], F32R)
        persistent = {
            "ff": rb,
            "gu": rb[:, 0:NJ * 8 * P].rearrange("p (j a i w) -> p j a i w", j=NJ, a=2, i=4),
            "down": rb[:, NJ * 8 * P:NJ * 8 * P + 2 * NJ * D].rearrange("p (a j d) -> p a j d", a=2, j=NJ),
            "small": sb("ff1_weights", [P, 2, 4 * P], F32R),
            "routers": sb("routers", [P, 2, 2, NC * E], F32R),
            "mod": sb("mod", [P, 2, 6 * NC, B]),
            "gbo": sb("gbo", [P, NC, B]),
            "const": Constants(sb),
        }
        yacc = sb("yacc", [P, NC, NP * TOK])
        x_all = yacc[:, :, :].rearrange("p c t -> p (c t)").rearrange("p (t d) -> p t d", d=D)
        routers = persistent["routers"][:, :, :, :].rearrange("p l a (c e) -> p l a c e", c=NC)
        held = []
        start(nc, held, ins, persistent, x_all, h0_dram, w0_dram, bank)
        release(nc, held)
        persistent["routers"] = routers
        ra = sb("attn_weights", [P, 2 * 5 * 2 * PIECE], F32R)

        def pieces(t, at, n):
            return t[:, at:at + n * 2 * PIECE].rearrange("p (n a w) -> p n a w", n=n, a=2)

        const = persistent["const"]
        held = []
        attention0(nc, held, [pieces(ra, 0, 5), pieces(ra, 5 * 2 * PIECE, 5)], h0_dram, w0_dram, yacc, bank, const)
        release(nc, held)
        held = []
        feed_forward0(nc, held, ins, persistent, ra[:, 8 * 2 * PIECE:10 * 2 * PIECE],
                      ra[:, 0:8 * 2 * PIECE].bitcast(F32), ra[:, 8 * 2 * PIECE:10 * 2 * PIECE].bitcast(F32),
                      yacc, h1_dram, w1_dram, x_dram, bank)
        release(nc, held)
        held = []
        hv = ra[:, 8 * 2 * PIECE:10 * 2 * PIECE].rearrange("p (a c t) -> p a c t", a=2, c=NC)
        hT2 = rb[:, 8 * 2 * PIECE:12 * 2 * PIECE].rearrange("p (i a c t) -> p i a c t", i=2, a=2, c=NC)
        attention1(nc, held, [pieces(ra, 0, 8), pieces(rb, 0, 8)], hT2, hv, h1_dram, w1_dram, yacc, bank, const)
        release(nc, held)
        held = []
        feed_forward1(nc, held, persistent, yacc, x_dram, out, bank)
        release(nc, held)


_INS = ["L0_attn_x", "L0_attn_Wq", "L0_attn_Wk", "L0_attn_Wv", "L0_attn_Wo", "L0_ffn_Wr", "L0_ffn_Wg",
        "L0_ffn_Wu", "L0_ffn_Wd", "L0_ffn_Wsg", "L0_ffn_Wsu", "L0_ffn_Wsd", "L0_c", "L0_wmod",
        "L1_attn_wq_codes", "L1_attn_wq_scales", "L1_attn_bq", "L1_attn_wk_codes", "L1_attn_wk_scales",
        "L1_attn_bk", "L1_attn_wv_codes", "L1_attn_wv_scales", "L1_attn_bv", "L1_attn_wo_codes",
        "L1_attn_wo_scales", "L1_attn_bo", "L1_ffn_router_w", "L1_ffn_down_w", "L1_ffn_up_w", "L1_c",
        "L1_wmod"]


def tables():
    import numpy as np
    f = np.float32
    half = HD // 2
    inv_freq = (f(1.0) / f(10000.0) ** (np.arange(0, HD, 2, dtype=f) / f(HD))).astype(f)
    angle = (inv_freq[:, None] * np.arange(S, dtype=f)[None, :]).astype(f)
    cos, sin = np.cos(angle).astype(f), np.sin(angle).astype(f)
    cos, sin = np.concatenate([cos, cos]), np.concatenate([-sin, sin])
    assert cos.shape == (2 * half, S)
    sel = np.zeros((2 * E, (NR + 1) * P), f)
    for j in range(NR * P):
        sel[[j // F0, E + j // F0], j] = 1
    for j in range(P):
        sel[[j // (P // E), E + j // (P // E)], NR * P + j] = 1
    mask = np.where(np.arange(P)[None, :] > np.arange(P)[:, None], f(MASKED), f(0)).astype(f)
    return {"k_ident": np.eye(P, dtype=f), "k_mask": mask, "k_sel": sel,
            "k_cos_q": (cos * f(SCALE)).astype(f), "k_sin_q": (sin * f(SCALE)).astype(f),
            "k_cos_k": cos, "k_sin_k": sin,
            "k_iota": np.tile(np.arange(E, dtype=f), (P, 1))}


def kernel(**inputs):
    import numpy as np
    import concourse.bacc as bacc
    from concourse.bass_utils import run_bass_kernel_spmd as run

    nc = bacc.Bacc("TRN2", target_bir_lowering=False, num_devices=1, dynamic_dma_scratch_size=1024)
    given = {name: np.ascontiguousarray(inputs[name]) for name in _INS}
    given.update(tables())
    arrays, ins = {}, {}
    for name, a in given.items():
        arrays[f"in_{name}"] = a
        ins[name] = nc.dram_tensor(f"in_{name}", a.shape, mybir.dt.from_np(a.dtype), kind="ExternalInput").ap()
    out = nc.dram_tensor("out_0", (B, S, D), F32, kind="ExternalOutput").ap()
    program(nc, ins, out)
    r = run(nc, [arrays], core_ids=[0])
    return r.results[0]["out_0"]
```
